# Optimizing a Trainium2 kernel written in Bass

```python
import numpy as np
import jax
import jax.numpy as jnp

def _softmax(x, axis=-1):
    return jax.nn.softmax(x, axis=axis)

def _gelu(x):
    return jax.nn.gelu(x, approximate=True)

def _silu(x):
    return jax.nn.silu(x)

def _sigmoid(x):
    return jax.nn.sigmoid(x)

def _layernorm(x, axis=-1, eps=1e-05):
    m = jnp.mean(x, axis=axis, keepdims=True)
    v = jnp.var(x, axis=axis, keepdims=True)
    return (x - m) / jnp.sqrt(v + eps)

def _scatter_add(tgt, idx, src, axis=0):
    return tgt.at[idx].add(src)

def _segment_sum(src, seg, n):
    return jax.ops.segment_sum(src, seg, n)
kernel_name = 'mk_seq_postln_d2_jaxref_r8_de514d'

def setup_inputs(seed: int=0):
    np.random.seed(seed)
    _w = jnp.asarray

    def _L0_attn_setup():
        import jax, jax.numpy as jnp
        import numpy as np
        EPS = 1e-12

        def _l2norm(t):
            n = jnp.linalg.norm(t, axis=-1, keepdims=True)
            return t / jnp.maximum(n, EPS)
        key = jax.random.key(seed)
        kx, kq, kk, kv = jax.random.split(key, 4)
        B, N, D = (8, 512, 128)
        s = 1.0 / np.sqrt(D)
        return {'x': jax.random.normal(kx, (B, N, D), dtype=jnp.float32), 'W_q': jax.random.normal(kq, (D, D), dtype=jnp.float32) * s, 'W_k': jax.random.normal(kk, (D, D), dtype=jnp.float32) * s, 'W_v': jax.random.normal(kv, (D, D), dtype=jnp.float32) * s}
    _L0_attn_in = _L0_attn_setup()

    def _L0_ffn_setup():
        import jax, jax.numpy as jnp
        import numpy as np
        SQRT_2_PI = 0.7978845608028654
        GELU_COEF = 0.044715
        LN_EPS = 1e-06
        TOP_K = 2

        def gelu_kernel(x):
            inner = SQRT_2_PI * (x + GELU_COEF * x ** 3)
            return 0.5 * x * (1.0 + jnp.tanh(inner))
        key = jax.random.key(seed)
        ks = jax.random.split(key, 8)
        B, S, D, F, E = (2, 256, 128, 512, 8)
        s = lambda d: 1.0 / np.sqrt(d)
        return {'x': jax.random.normal(ks[0], (B, S, D), jnp.float32), 'Wr1': jax.random.normal(ks[1], (D, D // 2), jnp.float32) * s(D), 'br1': jnp.zeros((D // 2,), jnp.float32), 'ln_scale': jnp.ones((D // 2,), jnp.float32), 'ln_bias': jnp.zeros((D // 2,), jnp.float32), 'Wr2': jax.random.normal(ks[2], (D // 2, E), jnp.float32) * s(D // 2), 'br2': jnp.zeros((E,), jnp.float32), 'W1': jax.random.normal(ks[3], (E, D, 2 * F), jnp.float32) * s(D), 'b1': jnp.zeros((E, 2 * F), jnp.float32), 'W2': jax.random.normal(ks[4], (E, F, D), jnp.float32) * s(F), 'b2': jnp.zeros((E, D), jnp.float32)}
    _L0_ffn_in = _L0_ffn_setup()

    def _L1_attn_setup():
        import jax, jax.numpy as jnp
        import numpy as np
        H = 128
        NH = 16
        L = 4
        B = 4
        N = 256
        EPS_LN = 1e-12

        def gelu(x):
            return jax.nn.gelu(x, approximate=False)

        def layernorm(x, g, b):
            m = jnp.mean(x, axis=-1, keepdims=True)
            v = jnp.mean((x - m) ** 2, axis=-1, keepdims=True)
            return (x - m) / jnp.sqrt(v + EPS_LN) * g + b

        def conv1d_grouped(x, w, b, groups):
            y = jax.lax.conv_general_dilated(x, w, window_strides=(1,), padding=[(2, 2)], dimension_numbers=('NCH', 'OIH', 'NCH'), feature_group_count=groups)
            return y + b[None, :, None]

        def rope(x):
            b, n, c = x.shape
            half = c // 2
            inv = 1.0 / 10000.0 ** (jnp.arange(0, c, 2, dtype=jnp.float32) / c)
            freqs = jnp.arange(n, dtype=jnp.float32)[:, None] * inv[None, :]
            freqs = jnp.repeat(freqs, 2, axis=-1)
            cos, sin = (jnp.cos(freqs), jnp.sin(freqs))
            xp = x.reshape(b, n, half, 2)
            xr = jnp.stack([-xp[..., 1], xp[..., 0]], axis=-1).reshape(b, n, c)
            return x * cos + xr * sin

        def linear_attention(x, Wq, bq, Wk, bk, Wv, bv, g, bb):
            b, n, c = x.shape
            hd = c // NH
            q = gelu(x @ Wq + bq) + 0.21
            k = gelu(x @ Wk + bk) + 0.21
            v = x @ Wv + bv
            q_r = rope(q)
            k_r = rope(k)
            to_h = lambda t: t.reshape(b, n, NH, hd).transpose(0, 2, 1, 3)
            q, k, v, q_r, k_r = map(to_h, (q, k, v, q_r, k_r))
            kmean = jnp.mean(k, axis=2, keepdims=True)
            z = 1.0 / (jnp.einsum('bhnd,bhmd->bhnm', q, kmean) + 1e-06)
            kv = jnp.einsum('bhnd,bhne->bhde', k_r, v) / n
            out = jnp.einsum('bhnd,bhde->bhne', q_r, kv) * z
            out = out.transpose(0, 2, 1, 3).reshape(b, n, c)
            return layernorm(out + x, g, bb)
        key = jax.random.key(seed)
        ks = jax.random.split(key, 10)
        s = 0.02
        r = lambda k, sh: jax.random.normal(k, sh, dtype=jnp.float32) * s
        d = {}
        d['x'] = jax.random.normal(ks[0], (B, N, H), dtype=jnp.float32)
        d['conv1_w'] = r(ks[1], (4 * H, 1, 5))
        d['conv1_b'] = jnp.zeros((4 * H,), jnp.float32)
        d['conv2_w'] = r(ks[2], (H, 4, 5))
        d['conv2_b'] = jnp.zeros((H,), jnp.float32)
        d['ln0_g'] = jnp.ones((H,), jnp.float32)
        d['ln0_b'] = jnp.zeros((H,), jnp.float32)
        d['Wq'] = r(ks[3], (L, H, H))
        d['bq'] = jnp.zeros((L, H), jnp.float32)
        d['Wk'] = r(ks[4], (L, H, H))
        d['bk'] = jnp.zeros((L, H), jnp.float32)
        d['Wv'] = r(ks[5], (L, H, H))
        d['bv'] = jnp.zeros((L, H), jnp.float32)
        d['lnA_g'] = jnp.ones((L, H), jnp.float32)
        d['lnA_b'] = jnp.zeros((L, H), jnp.float32)
        d['W1'] = r(ks[6], (H, 4 * H))
        d['b1'] = jnp.zeros((4 * H,), jnp.float32)
        d['W2'] = r(ks[7], (4 * H, H))
        d['b2'] = jnp.zeros((H,), jnp.float32)
        d['ln2_g'] = jnp.ones((H,), jnp.float32)
        d['ln2_b'] = jnp.zeros((H,), jnp.float32)
        return d
    _L1_attn_in = _L1_attn_setup()

    def _L1_ffn_setup():
        import jax, jax.numpy as jnp
        import numpy as np
        D_IN, D_HID = (128, 512)

        def _ternary(key, shape):
            return jax.random.randint(key, shape, -1, 2).astype(jnp.float32)

        def _tlin(x, w, s):
            return jnp.einsum('bsi,oi->bso', x, w) * s
        key = jax.random.key(seed)
        ks = jax.random.split(key, 12)
        inv = lambda fan: 1.0 / np.sqrt(fan).astype(np.float32)
        return {'x': jax.random.normal(ks[0], (4, 256, D_IN), dtype=jnp.float32), 'w1_w': _ternary(ks[1], (D_HID, D_IN)), 'w1_s': jax.random.uniform(ks[2], (D_HID,), dtype=jnp.float32) * inv(D_IN), 'w2_w': _ternary(ks[3], (D_HID, D_IN)), 'w2_s': jax.random.uniform(ks[4], (D_HID,), dtype=jnp.float32) * inv(D_IN), 'h1_w': _ternary(ks[5], (D_HID, D_HID)), 'h1_s': jax.random.uniform(ks[6], (D_HID,), dtype=jnp.float32) * inv(D_HID), 'h2_w': _ternary(ks[7], (D_HID, D_HID)), 'h2_s': jax.random.uniform(ks[8], (D_HID,), dtype=jnp.float32) * inv(D_HID), 'w3_w': _ternary(ks[9], (D_IN, D_HID)), 'w3_s': jax.random.uniform(ks[10], (D_IN,), dtype=jnp.float32) * inv(D_HID)}
    _L1_ffn_in = _L1_ffn_setup()
    _d = {'L0_attn_x': _L0_attn_in['x'], 'L0_attn_W_q': _L0_attn_in['W_q'], 'L0_attn_W_k': _L0_attn_in['W_k'], 'L0_attn_W_v': _L0_attn_in['W_v'], 'L0_ffn_Wr1': _L0_ffn_in['Wr1'], 'L0_ffn_br1': _L0_ffn_in['br1'], 'L0_ffn_ln_scale': _L0_ffn_in['ln_scale'], 'L0_ffn_ln_bias': _L0_ffn_in['ln_bias'], 'L0_ffn_Wr2': _L0_ffn_in['Wr2'], 'L0_ffn_br2': _L0_ffn_in['br2'], 'L0_ffn_W1': _L0_ffn_in['W1'], 'L0_ffn_b1': _L0_ffn_in['b1'], 'L0_ffn_W2': _L0_ffn_in['W2'], 'L0_ffn_b2': _L0_ffn_in['b2'], 'L1_attn_conv1_w': _L1_attn_in['conv1_w'], 'L1_attn_conv1_b': _L1_attn_in['conv1_b'], 'L1_attn_conv2_w': _L1_attn_in['conv2_w'], 'L1_attn_conv2_b': _L1_attn_in['conv2_b'], 'L1_attn_ln0_g': _L1_attn_in['ln0_g'], 'L1_attn_ln0_b': _L1_attn_in['ln0_b'], 'L1_attn_Wq': _L1_attn_in['Wq'], 'L1_attn_bq': _L1_attn_in['bq'], 'L1_attn_Wk': _L1_attn_in['Wk'], 'L1_attn_bk': _L1_attn_in['bk'], 'L1_attn_Wv': _L1_attn_in['Wv'], 'L1_attn_bv': _L1_attn_in['bv'], 'L1_attn_lnA_g': _L1_attn_in['lnA_g'], 'L1_attn_lnA_b': _L1_attn_in['lnA_b'], 'L1_attn_W1': _L1_attn_in['W1'], 'L1_attn_b1': _L1_attn_in['b1'], 'L1_attn_W2': _L1_attn_in['W2'], 'L1_attn_b2': _L1_attn_in['b2'], 'L1_attn_ln2_g': _L1_attn_in['ln2_g'], 'L1_attn_ln2_b': _L1_attn_in['ln2_b'], 'L1_ffn_w1_w': _L1_ffn_in['w1_w'], 'L1_ffn_w1_s': _L1_ffn_in['w1_s'], 'L1_ffn_w2_w': _L1_ffn_in['w2_w'], 'L1_ffn_w2_s': _L1_ffn_in['w2_s'], 'L1_ffn_h1_w': _L1_ffn_in['h1_w'], 'L1_ffn_h1_s': _L1_ffn_in['h1_s'], 'L1_ffn_h2_w': _L1_ffn_in['h2_w'], 'L1_ffn_h2_s': _L1_ffn_in['h2_s'], 'L1_ffn_w3_w': _L1_ffn_in['w3_w'], 'L1_ffn_w3_s': _L1_ffn_in['w3_s']}
    _x0 = _d['L0_attn_x']
    _d['L0_attn_x'] = jax.random.normal(jax.random.fold_in(jax.random.key(seed), 1), (8, 256, 128), dtype=_x0.dtype)
    del _x0
    return _d

def reference(L0_attn_x, L0_attn_W_q, L0_attn_W_k, L0_attn_W_v, L0_ffn_Wr1, L0_ffn_br1, L0_ffn_ln_scale, L0_ffn_ln_bias, L0_ffn_Wr2, L0_ffn_br2, L0_ffn_W1, L0_ffn_b1, L0_ffn_W2, L0_ffn_b2, L1_attn_conv1_w, L1_attn_conv1_b, L1_attn_conv2_w, L1_attn_conv2_b, L1_attn_ln0_g, L1_attn_ln0_b, L1_attn_Wq, L1_attn_bq, L1_attn_Wk, L1_attn_bk, L1_attn_Wv, L1_attn_bv, L1_attn_lnA_g, L1_attn_lnA_b, L1_attn_W1, L1_attn_b1, L1_attn_W2, L1_attn_b2, L1_attn_ln2_g, L1_attn_ln2_b, L1_ffn_w1_w, L1_ffn_w1_s, L1_ffn_w2_w, L1_ffn_w2_s, L1_ffn_h1_w, L1_ffn_h1_s, L1_ffn_h2_w, L1_ffn_h2_s, L1_ffn_w3_w, L1_ffn_w3_s):

    def _L0_attn_ref(x, W_q, W_k, W_v):
        import jax, jax.numpy as jnp
        import numpy as np
        EPS = 1e-12

        def _l2norm(t):
            n = jnp.linalg.norm(t, axis=-1, keepdims=True)
            return t / jnp.maximum(n, EPS)
        Q = _l2norm(jnp.einsum('bnd,ed->bne', x, W_q))
        K = _l2norm(jnp.einsum('bnd,ed->bne', x, W_k))
        V = jnp.einsum('bnd,ed->bne', x, W_v)
        C = x.shape[1]
        global_feat = jnp.sum(K * V, axis=1, keepdims=True) / C
        return Q * global_feat

    def _L0_ffn_ref(x, Wr1, br1, ln_scale, ln_bias, Wr2, br2, W1, b1, W2, b2):
        import jax, jax.numpy as jnp
        import numpy as np
        SQRT_2_PI = 0.7978845608028654
        GELU_COEF = 0.044715
        LN_EPS = 1e-06
        TOP_K = 2

        def gelu_kernel(x):
            inner = SQRT_2_PI * (x + GELU_COEF * x ** 3)
            return 0.5 * x * (1.0 + jnp.tanh(inner))
        E = W1.shape[0]
        h = jnp.einsum('bsd,dk->bsk', x, Wr1) + br1
        mu = jnp.mean(h, axis=-1, keepdims=True)
        var = jnp.mean((h - mu) ** 2, axis=-1, keepdims=True)
        h = (h - mu) * jax.lax.rsqrt(var + LN_EPS) * ln_scale + ln_bias
        h = gelu_kernel(h)
        router_logits = jnp.einsum('bsk,ke->bse', h, Wr2) + br2
        routing_probs = jax.nn.softmax(router_logits, axis=-1)
        top_k_probs, top_k_indices = jax.lax.top_k(routing_probs, TOP_K)
        top_k_probs = top_k_probs / jnp.sum(top_k_probs, axis=-1, keepdims=True)
        expert_mask = jnp.sum(jax.nn.one_hot(top_k_indices, E, dtype=x.dtype) * top_k_probs[..., None], axis=-2)
        output = jnp.zeros_like(x)
        for e in range(E):
            x12 = jnp.einsum('bsd,df->bsf', x, W1[e]) + b1[e]
            x1, x2 = jnp.split(x12, 2, axis=-1)
            g = x1 * gelu_kernel(x2)
            y = jnp.einsum('bsf,fd->bsd', g, W2[e]) + b2[e]
            output = output + y * expert_mask[:, :, e][:, :, None]
        return output

    def _L1_attn_ref(x, conv1_w, conv1_b, conv2_w, conv2_b, ln0_g, ln0_b, Wq, bq, Wk, bk, Wv, bv, lnA_g, lnA_b, W1, b1, W2, b2, ln2_g, ln2_b):
        import jax, jax.numpy as jnp
        import numpy as np
        H = 128
        NH = 16
        L = 4
        B = 4
        N = 256
        EPS_LN = 1e-12

        def gelu(x):
            return jax.nn.gelu(x, approximate=False)

        def layernorm(x, g, b):
            m = jnp.mean(x, axis=-1, keepdims=True)
            v = jnp.mean((x - m) ** 2, axis=-1, keepdims=True)
            return (x - m) / jnp.sqrt(v + EPS_LN) * g + b

        def conv1d_grouped(x, w, b, groups):
            y = jax.lax.conv_general_dilated(x, w, window_strides=(1,), padding=[(2, 2)], dimension_numbers=('NCH', 'OIH', 'NCH'), feature_group_count=groups)
            return y + b[None, :, None]

        def rope(x):
            b, n, c = x.shape
            half = c // 2
            inv = 1.0 / 10000.0 ** (jnp.arange(0, c, 2, dtype=jnp.float32) / c)
            freqs = jnp.arange(n, dtype=jnp.float32)[:, None] * inv[None, :]
            freqs = jnp.repeat(freqs, 2, axis=-1)
            cos, sin = (jnp.cos(freqs), jnp.sin(freqs))
            xp = x.reshape(b, n, half, 2)
            xr = jnp.stack([-xp[..., 1], xp[..., 0]], axis=-1).reshape(b, n, c)
            return x * cos + xr * sin

        def linear_attention(x, Wq, bq, Wk, bk, Wv, bv, g, bb):
            b, n, c = x.shape
            hd = c // NH
            q = gelu(x @ Wq + bq) + 0.21
            k = gelu(x @ Wk + bk) + 0.21
            v = x @ Wv + bv
            q_r = rope(q)
            k_r = rope(k)
            to_h = lambda t: t.reshape(b, n, NH, hd).transpose(0, 2, 1, 3)
            q, k, v, q_r, k_r = map(to_h, (q, k, v, q_r, k_r))
            kmean = jnp.mean(k, axis=2, keepdims=True)
            z = 1.0 / (jnp.einsum('bhnd,bhmd->bhnm', q, kmean) + 1e-06)
            kv = jnp.einsum('bhnd,bhne->bhde', k_r, v) / n
            out = jnp.einsum('bhnd,bhde->bhne', q_r, kv) * z
            out = out.transpose(0, 2, 1, 3).reshape(b, n, c)
            return layernorm(out + x, g, bb)
        b, n, c = x.shape
        h = x.transpose(0, 2, 1)
        h = conv1d_grouped(h, conv1_w, conv1_b, c)
        h = gelu(h)
        h = conv1d_grouped(h, conv2_w, conv2_b, c)
        h = h.transpose(0, 2, 1)
        h = layernorm(h + x, ln0_g, ln0_b)
        for i in range(Wq.shape[0]):
            h = linear_attention(h, Wq[i], bq[i], Wk[i], bk[i], Wv[i], bv[i], lnA_g[i], lnA_b[i])
        f = gelu(h @ W1 + b1) @ W2 + b2
        return layernorm(f + h, ln2_g, ln2_b)

    def _L1_ffn_ref(x, w1_w, w1_s, w2_w, w2_s, h1_w, h1_s, h2_w, h2_s, w3_w, w3_s):
        import jax, jax.numpy as jnp
        import numpy as np
        D_IN, D_HID = (128, 512)

        def _ternary(key, shape):
            return jax.random.randint(key, shape, -1, 2).astype(jnp.float32)

        def _tlin(x, w, s):
            return jnp.einsum('bsi,oi->bso', x, w) * s
        h = jax.nn.silu(_tlin(x, w1_w, w1_s)) * _tlin(x, w2_w, w2_s)
        h = jax.nn.gelu(_tlin(h, h1_w, h1_s), approximate=False)
        h = jax.nn.gelu(_tlin(h, h2_w, h2_s), approximate=False)
        return _tlin(h, w3_w, w3_s)
    x = L0_attn_x
    x = _layernorm(x + _L0_attn_ref(x, L0_attn_W_q, L0_attn_W_k, L0_attn_W_v), axis=-1)
    x = _layernorm(x + _L0_ffn_ref(x, L0_ffn_Wr1, L0_ffn_br1, L0_ffn_ln_scale, L0_ffn_ln_bias, L0_ffn_Wr2, L0_ffn_br2, L0_ffn_W1, L0_ffn_b1, L0_ffn_W2, L0_ffn_b2), axis=-1)
    x = _layernorm(x + _L1_attn_ref(x, L1_attn_conv1_w, L1_attn_conv1_b, L1_attn_conv2_w, L1_attn_conv2_b, L1_attn_ln0_g, L1_attn_ln0_b, L1_attn_Wq, L1_attn_bq, L1_attn_Wk, L1_attn_bk, L1_attn_Wv, L1_attn_bv, L1_attn_lnA_g, L1_attn_lnA_b, L1_attn_W1, L1_attn_b1, L1_attn_W2, L1_attn_b2, L1_attn_ln2_g, L1_attn_ln2_b), axis=-1)
    x = _layernorm(x + _L1_ffn_ref(x, L1_ffn_w1_w, L1_ffn_w1_s, L1_ffn_w2_w, L1_ffn_w2_s, L1_ffn_h1_w, L1_ffn_h1_s, L1_ffn_h2_w, L1_ffn_h2_s, L1_ffn_w3_w, L1_ffn_w3_s), axis=-1)
    return x

_drawn_inputs = setup_inputs


def setup_inputs(seed=0):
    import zlib

    import numpy as np

    out = dict(_drawn_inputs(seed))
    spreads = {'L0_ffn_br1': (0.0, 0.1),
     'L0_ffn_ln_scale': (1.0, 0.2),
     'L0_ffn_ln_bias': (0.0, 0.1),
     'L0_ffn_br2': (0.0, 0.1),
     'L0_ffn_b1': (0.0, 0.1),
     'L0_ffn_b2': (0.0, 0.1),
     'L1_attn_conv1_b': (0.0, 0.8),
     'L1_attn_conv2_b': (0.0, 0.1),
     'L1_attn_ln0_g': (1.0, 0.2),
     'L1_attn_ln0_b': (0.0, 0.1),
     'L1_attn_bq': (0.0, 2.0),
     'L1_attn_bk': (0.0, 2.0),
     'L1_attn_bv': (0.0, 0.1),
     'L1_attn_lnA_g': (1.0, 0.2),
     'L1_attn_lnA_b': (0.0, 0.1),
     'L1_attn_b1': (0.0, 0.565),
     'L1_attn_b2': (0.0, 0.1),
     'L1_attn_ln2_g': (1.0, 0.2),
     'L1_attn_ln2_b': (0.0, 0.1)}
    factors = {'L0_attn_W_q': 8.0,
     'L0_attn_W_k': 7.193,
     'L0_attn_W_v': 7.286,
     'L1_attn_conv1_w': 8.0,
     'L1_attn_conv2_w': 8.0,
     'L1_attn_Wq': 8.0,
     'L1_attn_Wk': 8.0,
     'L1_ffn_w1_w': 8.0,
     'L1_ffn_w1_s': 8.0,
     'L1_ffn_w2_w': 8.0,
     'L1_ffn_w2_s': 8.0,
     'L1_ffn_h1_w': 8.0,
     'L1_ffn_h1_s': 8.0,
     'L1_ffn_h2_w': 8.0,
     'L1_ffn_h2_s': 8.0,
     'L1_ffn_w3_w': 8.0,
     'L1_ffn_w3_s': 8.0}
    for name, (base, spread) in spreads.items():
        noise = np.random.default_rng([zlib.crc32(name.encode()), seed]).standard_normal(out[name].shape)
        drawn = base * np.exp(spread * noise) if base else spread * noise
        out[name] = jnp.asarray(drawn.astype(out[name].dtype))
    for name, factor in factors.items():
        out[name] = (out[name] * factor).astype(out[name].dtype)
    return out
```

```python
from contextlib import ExitStack

import numpy as np

import concourse.bass as bass
from concourse import mybir

F32 = mybir.dt.float32
F32R = mybir.dt.float32r
ALU = mybir.AluOpType
ACT = mybir.ActivationFunctionType
AX = mybir.AxisListType

P = 128
B, N, D = 8, 256, 128
SEQS = 2
T = SEQS * N // P
W = T * P
BLOCKS = B // SEQS
E, F = 8, 512
FC = F // P
R = D // 2
L = 4
HEADS = 16
HD = D // HEADS
TAPS, PAD = 5, 2
STEPS = E * FC

ROWS = {}
_at = 0
for _name, _n in (("e_b1", 2 * FC * E), ("f_b1", FC), ("f_b2", 1), ("c2_b", 1), ("w1_s", FC), ("w2_s", FC),
                  ("h1_s", FC), ("h2_s", FC), ("w3_s", 1)):
    ROWS[_name] = (_at, _n)
    _at += _n
NROWS = _at


class Steps:

    def __init__(self, sem, *steps, unit=1):
        self.sem, self.unit, self.first, self.n = sem, unit, {}, 0
        for name, count in steps:
            self.first[name] = self.n
            self.n += count

    def after(self, blk, name, k=0):
        return self.before(blk) + (self.first[name] + k + 1) * self.unit

    def before(self, blk):
        return blk * (self.n * self.unit) + 1


def norm_steps(name, affine):
    s = [(name + "stats", T), (name + "aggr", T), (name + "eps", 1), (name + "apply", T)]
    return s + ([(name + "gain", 1), (name + "shift", 1)] if affine else [])


def build(nc, x_in, out, a):
    ctx = ExitStack()
    with ctx:
        def sb(name, shape, dt=F32):
            return ctx.enter_context(nc.sbuf_tensor(name, shape, dt))

        def sem(name):
            return ctx.enter_context(nc.semaphore(name))

        def bank(name):
            return ctx.enter_context(nc.psum_tensor(name, [P, 512], F32))

        gate = [bank(f"gate{i}") for i in range(2)]
        up = [bank(f"up{i}") for i in range(2)]
        ybank = bank("ybank")
        tr = bank("tr")
        mb = [bank(f"mb{i}") for i in range(2)]

        ident = sb("ident", [P, P])
        mean_of = sb("mean_of", [P, P])
        headmask = sb("headmask", [P, P])
        cos = sb("cos", [P, N // P, D])
        sin = sb("sin", [P, N // P, D])
        earlier = sb("earlier", [P, E, E])
        pick = sb("pick", [E, E, P])
        minus_half = sb("minus_half", [P, 2 * T])
        rows = sb("rows", [P, P])
        cols = sb("cols", [P, NROWS])
        wqkv0_raw = sb("wqkv0_raw", [P, 3, D])
        wqkv0 = sb("wqkv0", [P, 3 * D])
        wr1 = sb("wr1", [P, R])
        wr2 = sb("wr2", [R, E])
        e_w1 = sb("e_w1", [P, E, 2 * F])
        e_w2 = sb("e_w2", [P, E, FC, D])
        e_b2 = sb("e_b2", [E, D])
        br1 = sb("br1", [P, R])
        r_g = sb("r_g", [P, R])
        r_b = sb("r_b", [P, R])
        br2 = sb("br2", [P, E])
        c1_w = sb("c1_w", [P, 4, TAPS])
        c1_b = sb("c1_b", [P, 4])
        c2_w = sb("c2_w", [P, 4, TAPS])
        gains = sb("gains", [P, L + 2, D])
        shifts = sb("shifts", [P, L + 2, D])
        a_w = sb("a_w", [P, L, 3 * D])
        a_bs = sb("a_bs", [33, L, 3 * D], F32R)
        one_rows = sb("one_rows", [33, P], F32R)
        f_w1 = sb("f_w1", [P, F])
        f_w2 = sb("f_w2", [P, FC, D])
        t_w12 = sb("t_w12", [P, 2, F])
        t_h = sb("t_h", [P, 2, FC, F])
        t_w3 = sb("t_w3", [P, FC, D])

        x_t = sb("x_t", [P, T, D])
        room = sb("room", [P, 3, 2 * T * D])
        qk, rot, big = (room[:, i].rearrange("p (t c d) -> p t c d", t=T, c=2) for i in range(3))
        qkv = room[:].rearrange("p a b -> p (a b)")[:, 0:T * 3 * D].rearrange("p (t c d) -> p t c d", t=T, c=3)
        c1 = room[:, 0:2].rearrange("p a b -> p (a b)").rearrange("p (j s n) -> p j s n", j=4, s=SEQS)
        ffh = room[:, 0:2].rearrange("p a b -> p (a b)").rearrange("p (c w) -> p c w", c=FC)
        ssq = sb("ssq", [P, T, 2])
        rn = sb("rn", [P, T, 2])
        sum_t = sb("sum_t", [P, T, D])
        x1_t = sb("x1_t", [P, T, D])
        x1F = sb("x1F", [P, W])
        hr = sb("hr", [P, T, R])
        hg = sb("hg", [P, T, R])
        hT = sb("hT", [R, W])
        lg = sb("lg", [P, T, E])
        cmp1 = sb("cmp1", [P, T, E, E])
        cmp2 = sb("cmp2", [P, T, E, E])
        rank = sb("rank", [P, T, E])
        lmax = sb("lmax", [P, T])
        lex = sb("lex", [P, T, E])
        wts = sb("wts", [P, T, E])
        wT = sb("wT", [E, W])
        wB = sb("wB", [P, E, W])
        stage = wB[:].rearrange("p (a c) w -> p a c w", a=2)
        tA, tB = stage[:, 0], stage[:, 1]
        g = sb("g", [P, 3, W])
        a_b = g[0:1].rearrange("p a w -> p (a w)").rearrange("p (l n) -> p l n", l=L)
        gw = sb("gw", [P, 2, W])
        p = sb("p", [P, 2, W])
        yF = sb("yF", [P, W])
        x2_t = sb("x2_t", [P, T, D])
        x2F = sb("x2F", [P, SEQS, N + 2 * PAD])
        c1F = sb("c1F", [P, 4, SEQS, N + 2 * PAD])
        c2 = sb("c2", [P, 2, SEQS, N])
        h_t = sb("h_t", [P, T, D])
        hF = sb("hF", [P, W])
        vt = sb("vt", [P, T, D])
        den = sb("den", [P, T, D])
        z = sb("z", [P, T * HEADS])
        kvm = sb("kvm", [P, SEQS, D])
        qF = sb("qF", [P, W])
        x3_t = sb("x3_t", [P, T, D])
        x3F = sb("x3F", [P, W])
        u = sb("u", [P, 2, W])
        o_t = sb("o_t", [P, T, D])
        st = sb("st", [P, T, 6])
        mv = sb("mv", [P, T, 2])
        ve = sb("ve", [P, T])
        rs = sb("rs", [P, T])

        def col(name, k=0):
            return cols[:, ROWS[name][0] + k:ROWS[name][0] + k + 1]

        x_got = Steps(sem("x_got"), ("x", 1), unit=16)
        out_put = Steps(sem("out_put"), ("out", 1), unit=16)
        mix_pe = Steps(sem("mix_pe"), ("xT", 1), ("qkv", T), ("mean", 1))
        mix_act = Steps(sem("mix_act"), ("xF", 1), ("qkv", T))
        mix_vec = Steps(sem("mix_vec"), ("square", 1), ("ssq", 1), ("clip", 1), ("kv", T), ("q", T), ("sum", 1),
                        *norm_steps("", False))
        mix_pool = Steps(sem("mix_pool"), ("len", 1), ("rstd", 1))
        route_pe = Steps(sem("route_pe"), ("x1T", 1), ("h", 1), ("hT", 1), ("logit", 1), ("wT", 1))
        route_act = Steps(sem("route_act"), ("x1F", 1), ("gelu", 1), ("hT", 1), ("exp", 1), ("wT", 1))
        route_vec = Steps(sem("route_vec"), ("h", 1), *norm_steps("", True), ("logit", 1), ("above", 1), ("tie", 1),
                          ("tie_earlier", 1), ("beats", 1), ("rank", 1), ("chosen", 1), ("max", 1), ("less_max", 1),
                          ("keep", 1), ("total", 1), ("recip", 1), ("weight", 1))
        route_pool = Steps(sem("route_pool"), ("rstd", 1))
        moe_pe = Steps(sem("moe_pe"), ("wB", E))
        moe_y = Steps(sem("moe_y"), ("y", STEPS), ("yT", 1))
        moe_gate = Steps(sem("moe_gate"), ("gate", STEPS))
        moe_up = Steps(sem("moe_up"), ("up", STEPS))
        moe_act = Steps(sem("moe_act"), ("wB", E // 2), ("gelu", STEPS), ("yF", 1))
        moe_pool = Steps(sem("moe_pool"), ("gw", STEPS), ("rstd", 1))
        moe_vec = Steps(sem("moe_vec"), ("wB", E // 2), ("p", STEPS), ("sum", 1), *norm_steps("", False))
        conv_pe = Steps(sem("conv_pe"), ("x2T", 1), ("c2T", 1))
        conv_act = Steps(sem("conv_act"), ("x2F", 1), ("gelu", 4))
        conv_vec = Steps(sem("conv_vec"), ("tap1", 4 * TAPS), ("tap2", 4 * TAPS), ("c2", 1), ("sum", 1),
                         *norm_steps("", True))
        conv_pool = Steps(sem("conv_pool"), ("rstd", 1))
        att_pe, att_act, att_vec, att_pool = [], [], [], []
        att_pe = Steps(sem("att_pe"), *[(f"{i}{s}", n) for i in range(L) for s, n in (
            ("hT", 1), ("qkv", T), ("kmean", 1), ("kv", 1), ("qT", 1), ("o", 1))])
        att_act = Steps(sem("att_act"), *[(f"{i}{s}", n) for i in range(L) for s, n in (
            ("hF", 1), ("v", T), ("qF", 1))])
        att_vec = Steps(sem("att_vec"), *[s for i in range(L) for s in (
            (f"{i}swap", 2 * SEQS), (f"{i}rot", SEQS), (f"{i}den", SEQS), (f"{i}head", 1), (f"{i}eps6", 1),
            (f"{i}z", 1), (f"{i}kvm", 1), (f"{i}oz", 1), (f"{i}sum", 1), *norm_steps(str(i), True))])
        att_pool = Steps(sem("att_pool"), *[(f"{i}{s}", n) for i in range(L) for s, n in (
            ("plus", SEQS), ("cos", SEQS), ("rstd", 1))])
        ffn_pe = Steps(sem("ffn_pe"), ("hT", 1), ("up", FC), ("down", 1), ("fT", 1))
        ffn_act = Steps(sem("ffn_act"), ("hF", 1), ("gelu", FC), ("fF", 1))
        ffn_vec = Steps(sem("ffn_vec"), ("sum", 1), *norm_steps("i", True), ("sum2", 1), *norm_steps("o", False))
        ffn_pool = Steps(sem("ffn_pool"), ("irstd", 1), ("orstd", 1))
        ter_pe = Steps(sem("ter_pe"), ("x3T", 1), ("gu", FC), ("h1", FC), ("h2", FC), ("w3", 1), ("yT", 1))
        ter_act = Steps(sem("ter_act"), ("x3F", 1), ("silu", FC), ("g1", FC), ("g2", FC), ("yF", 1))
        ter_vec = Steps(sem("ter_vec"), ("h", FC), ("sum", 1), *norm_steps("", False))
        ter_pool = Steps(sem("ter_pool"), ("rstd", 1))

        def begin(eng, *counts):
            for c in counts:
                eng.sem_inc(c.sem, 1)

        begun = sem("begun")
        passed = sem("passed")
        early = sem("early")
        e_got, later = sem("e_got"), sem("later")
        staged = [sem(f"staged{i}") for i in range(3)]
        set_pe, set_act = sem("set_pe"), sem("set_act")

        block = ctx.enter_context(nc.Block())

        def load_early(sp):
            n = 0
            for dst, src in (
                (ident[:], a["c_ident"]), (wqkv0_raw[:, 0, :], a["L0_attn_W_q"]), (wqkv0_raw[:, 1, :], a["L0_attn_W_k"]),
                (wqkv0_raw[:, 2, :], a["L0_attn_W_v"]), (mean_of[:], a["c_mean_of"]), (wr1[:], a["L0_ffn_Wr1"]),
                (wr2[:], a["L0_ffn_Wr2"]), (br1[:], row(a["L0_ffn_br1"])), (r_g[:], row(a["L0_ffn_ln_scale"])),
                (r_b[:], row(a["L0_ffn_ln_bias"])), (br2[:], row(a["L0_ffn_br2"])), (earlier[:], a["c_earlier"]),
                (pick[:], a["c_pick"]), (e_b2[:], a["L0_ffn_b2"]),
                (rows_of("e_b1"), a["L0_ffn_b1"].rearrange("e (c p) -> (e c) p", p=P)),
                (rows_of("f_b1"), a["L1_attn_b1"].rearrange("(c p) -> c p", p=P)),
                (rows_of("f_b2"), a["L1_attn_b2"].rearrange("(c p) -> c p", p=P)),
                (rows_of("c2_b"), a["L1_attn_conv2_b"].rearrange("(c p) -> c p", p=P)),
                (rows_of("w1_s"), a["L1_ffn_w1_s"].rearrange("(c p) -> c p", p=P)),
                (rows_of("w2_s"), a["L1_ffn_w2_s"].rearrange("(c p) -> c p", p=P)),
                (rows_of("h1_s"), a["L1_ffn_h1_s"].rearrange("(c p) -> c p", p=P)),
                (rows_of("h2_s"), a["L1_ffn_h2_s"].rearrange("(c p) -> c p", p=P)),
                (rows_of("w3_s"), a["L1_ffn_w3_s"].rearrange("(c p) -> c p", p=P)),
                (a_b[:, :, 0:D], a["L1_attn_bq"].rearrange("(a l) d -> a l d", a=1)),
                (a_b[:, :, D:2 * D], a["L1_attn_bk"].rearrange("(a l) d -> a l d", a=1)),
                (a_b[:, :, 2 * D:3 * D], a["L1_attn_bv"].rearrange("(a l) d -> a l d", a=1)),
            ):
                sp.dma_start(dst, src).then_inc(early, 16)
                n += 1
            return n

        EARLY = 26

        def load_experts(sp):
            for e in range(E):
                sp.dma_start(e_w1[:, e, :], a["L0_ffn_W1"][e]).then_inc(e_got, 16)
                sp.dma_start(e_w2[:, e, :, :], a["L0_ffn_W2"][e].rearrange("(c p) d -> p c d", p=P)).then_inc(e_got, 16)

        def load_later(sp):
            n = 0
            for dst, src in (
                (c1_w[:], a["L1_attn_conv1_w"].rearrange("(c j) o k -> c j (o k)", j=4)),
                (c1_b[:], a["L1_attn_conv1_b"].rearrange("(c j) -> c j", j=4)), (c2_w[:], a["L1_attn_conv2_w"]),
                (cos[:], a["c_cos"]), (sin[:], a["c_sin"]), (headmask[:], a["c_headmask"]),
                (gains[:, 0, :], row(a["L1_attn_ln0_g"])), (shifts[:, 0, :], row(a["L1_attn_ln0_b"])),
                (gains[:, L + 1, :], row(a["L1_attn_ln2_g"])), (shifts[:, L + 1, :], row(a["L1_attn_ln2_b"])),
                (gains[:, 1:L + 1, :], a["L1_attn_lnA_g"].rearrange("(a l) d -> a l d", a=1).partition_broadcast(P)),
                (shifts[:, 1:L + 1, :], a["L1_attn_lnA_b"].rearrange("(a l) d -> a l d", a=1).partition_broadcast(P)),
                (a_w[:, :, 0:D], a["L1_attn_Wq"].rearrange("l i o -> i l o")),
                (a_w[:, :, D:2 * D], a["L1_attn_Wk"].rearrange("l i o -> i l o")),
                (a_w[:, :, 2 * D:3 * D], a["L1_attn_Wv"].rearrange("l i o -> i l o")),
                (f_w1[:], a["L1_attn_W1"]), (f_w2[:], a["L1_attn_W2"].rearrange("(c p) d -> p c d", p=P)),
            ):
                sp.dma_start(dst, src).then_inc(later, 16)
                n += 1
            return n

        LATER = 17

        def row(v):
            return v.rearrange("(a n) -> a n", a=1).partition_broadcast(P)

        def rows_of(name):
            at, n = ROWS[name]
            return rows[at:at + n, :]

        stage_src = [
            [(stage[:, 0, 0, :].rearrange("p (c i) -> p c i", c=FC), "L1_ffn_w1_w"),
             (stage[:, 0, 1, :].rearrange("p (c i) -> p c i", c=FC), "L1_ffn_w2_w"),
             (stage[:, 0, 2, :].rearrange("p (c i) -> p c i", c=1), "L1_ffn_w3_w")],
            [(stage[:, 1, :, :], "L1_ffn_h1_w")],
            [(stage[:, 0, :, :], "L1_ffn_h2_w")],
        ]
        groups = []
        for w in range(2):
            groups.append((0, [stage[:, 0, w, c * P:(c + 1) * P] for c in range(FC)], t_w12[:, w, :]))
        groups.append((0, [stage[:, 0, 2, k * P:(k + 1) * P] for k in range(FC)], t_w3[:].rearrange("p k d -> p (k d)")))
        for w in range(2):
            for k in range(FC):
                groups.append((w + 1, [stage[:, 1 - w, c, k * P:(k + 1) * P] for c in range(FC)], t_h[:, w, k, :]))
        first = [wqkv0_raw[:, i, :] for i in range(3)]

        def load_ternary(sp):
            for r, loads in enumerate(stage_src):
                if r == 2:
                    sp.wait_ge(set_pe, 2 + 3)
                for dst, name in loads:
                    sp.dma_start(dst, a[name].rearrange("(c p) i -> p c i", p=P)).then_inc(staged[r], 16)

        def wait_apart(eng, s, value):
            eng.wait_ge(s, value)
            eng.sem_inc(passed, 1)

        def norm_vec(dve, steps, blk, name, src, dst, eps, rstd, affine=None):
            s = steps.sem
            for t in range(T):
                nc.vector.bn_stats(st[:, t, :], src[:, t, :]).then_inc(s, 1)
            wait_apart(dve, s, steps.after(blk, name + "stats", T - 1))
            for t in range(T):
                nc.vector.bn_aggr(mv[:, t, :], st[:, t, :]).then_inc(s, 1)
            dve.wait_ge(s, steps.after(blk, name + "aggr", T - 1))
            nc.vector.tensor_scalar(ve[:], mv[:, :, 1], eps, None, ALU.add).then_inc(s, 1)
            dve.wait_ge(rstd[0].sem, rstd[0].after(blk, rstd[1]))
            for t in range(T):
                nc.vector.tensor_scalar(dst[:, t, :], src[:, t, :], mv[:, t, 0:1], rs[:, t:t + 1],
                                        ALU.subtract, ALU.mult).then_inc(s, 1)
            if affine is not None:
                gain, shift = affine
                shape = list(dst.shape)
                dve.wait_ge(s, steps.after(blk, name + "apply", T - 1))
                nc.vector.tensor_tensor(dst, dst, gain.unsqueeze(1).to_broadcast(shape), ALU.mult).then_inc(s, 1)
                dve.wait_ge(s, steps.after(blk, name + "gain"))
                nc.vector.tensor_tensor(dst, dst, shift.unsqueeze(1).to_broadcast(shape), ALU.add).then_inc(s, 1)

        def norm_pool(pool, steps, blk, name, vec, vec_name):
            pool.wait_ge(vec.sem, vec.after(blk, vec_name))
            nc.gpsimd.tensor_tensor(rs[:], ve[:], minus_half[:, 0:T], ALU.pow).then_inc(steps.sem, 1)

        def turn(pe, src, bank):
            for t in range(T):
                mm = nc.tensor.transpose(bank[0:src.shape[2], t * P:(t + 1) * P], src[:, t, :], ident[:])
            return mm

        def turn_back(pe, srcF, bank):
            for t in range(T):
                mm = nc.tensor.transpose(bank[:, t * P:(t + 1) * P], srcF[:, t * P:(t + 1) * P], ident[:])
            return mm

        def tok(bank):
            return bank[:].rearrange("p (t d) -> p t d", t=T)

        class Sync:
            @staticmethod
            def block(sp, blk):
                sp.wait_ge(mix_vec.sem, mix_vec.before(blk))
                sp.dma_start(x_t[:], x_in[bass.ds(blk * W, W), :].rearrange("(t p) d -> p t d", p=P)).then_inc(x_got.sem, 16)

            @staticmethod
            def put(sp, blk):
                sp.wait_ge(ter_vec.sem, ter_vec.before(blk + 1))
                sp.dma_start(out[bass.ds(blk * W, W), :].rearrange("(t p) d -> p t d", p=P), o_t[:]).then_inc(out_put.sem, 16)

        class Pe:
            @staticmethod
            def setup(pe):
                pe.wait_ge(early, 16 * EARLY)
                for i, src in enumerate(first):
                    mm = nc.tensor.transpose(tr[:, i * P:(i + 1) * P], src, ident[:])
                mm.then_inc(set_pe, 1)
                nc.tensor.transpose(mb[0][:, 0:NROWS], rows[0:NROWS, :], ident[0:NROWS, 0:NROWS]).then_inc(set_pe, 1)

            @staticmethod
            def ternary(pe):
                for n, (r, srcs, _) in enumerate(groups):
                    pe.wait_ge(staged[r], 16 * len(stage_src[r]))
                    if n >= 2:
                        pe.wait_ge(set_act, 2 + n - 1)
                    for c, src in enumerate(srcs):
                        mm = nc.tensor.transpose(gate[n % 2][:, c * P:(c + 1) * P], src, ident[:])
                    mm.then_inc(set_pe, 1)

            @staticmethod
            def mix(pe, blk):
                pe.wait_ge(x_got.sem, x_got.after(blk, "x"))
                pe.wait_ge(set_act, 2)
                pe.wait_ge(ter_vec.sem, ter_vec.before(blk))
                turn(pe, x_t, tr).then_inc(mix_pe.sem, 1)
                pe.wait_ge(mix_act.sem, mix_act.after(blk, "xF"))
                for t in range(T):
                    if t >= 2:
                        pe.wait_ge(mix_act.sem, mix_act.after(blk, "qkv", t - 2))
                    nc.tensor.matmul(mb[t % 2][:, 0:3 * D], hF[:, t * P:(t + 1) * P], wqkv0[:],
                                     start=True, stop=True).then_inc(mix_pe.sem, 1)
                pe.wait_ge(mix_vec.sem, mix_vec.after(blk, "kv", T - 1))
                for s in range(SEQS):
                    for i in range(N // P):
                        mm = nc.tensor.matmul(mb[0][:, s * D:(s + 1) * D], mean_of[:], vt[:, s * (N // P) + i, :],
                                              start=(i == 0), stop=(i == N // P - 1))
                mm.then_inc(mix_pe.sem, 1)

            @staticmethod
            def route(pe, blk):
                pe.wait_ge(mix_vec.sem, mix_vec.after(blk, "apply", T - 1))
                turn(pe, x1_t, tr).then_inc(route_pe.sem, 1)
                pe.wait_ge(route_act.sem, route_act.after(blk, "x1F"))
                for t in range(T):
                    mm = nc.tensor.matmul(mb[0][:, t * R:(t + 1) * R], x1F[:, t * P:(t + 1) * P], wr1[:], start=True, stop=True)
                mm.then_inc(route_pe.sem, 1)
                wait_apart(pe, route_act.sem, route_act.after(blk, "gelu"))
                turn(pe, hg, tr).then_inc(route_pe.sem, 1)
                pe.wait_ge(route_act.sem, route_act.after(blk, "hT"))
                for t in range(T):
                    mm = nc.tensor.matmul(mb[1][:, t * E:(t + 1) * E], hT[:, t * P:(t + 1) * P], wr2[:], start=True, stop=True)
                mm.then_inc(route_pe.sem, 1)
                pe.wait_ge(route_vec.sem, route_vec.after(blk, "weight"))
                turn(pe, wts, tr).then_inc(route_pe.sem, 1)

            @staticmethod
            def moe_spread(pe, blk):
                pe.wait_ge(route_act.sem, route_act.after(blk, "wT"))
                banks = [gate[0], up[0], gate[1], up[1]]
                for e in range(E):
                    if e >= 4:
                        emptied = moe_act if e % 2 == 0 else moe_vec
                        pe.wait_ge(emptied.sem, emptied.after(blk, "wB", (e - 4) // 2))
                    nc.tensor.matmul(banks[e % 4][:], pick[:, e, :], wT[:], start=True, stop=True).then_inc(moe_pe.sem, 1)

            @staticmethod
            def moe_step(pe, blk, s):
                e, j = divmod(s, FC)
                if s < STEPS:
                    if s == 0:
                        pe.wait_ge(e_got, 32 * E)
                    name, k = ("gelu", s - 2) if s >= 2 else ("wB", E // 2 - 2 + s)
                    pe.wait_ge(moe_act.sem, moe_act.after(blk, name, k))
                    nc.tensor.matmul(gate[s % 2][:], e_w1[:, e, F + j * P:F + (j + 1) * P], x1F[:],
                                     start=True, stop=True).then_inc(moe_gate.sem, 1)
                    name, k = ("p", s - 2) if s >= 2 else ("wB", E // 2 - 2 + s)
                    pe.wait_ge(moe_vec.sem, moe_vec.after(blk, name, k))
                    nc.tensor.matmul(up[s % 2][:], e_w1[:, e, j * P:(j + 1) * P], x1F[:],
                                     start=True, stop=True).then_inc(moe_up.sem, 1)
                if s == 0:
                    nc.tensor.matmul(ybank[:], e_b2[:], wT[:], start=True, stop=False)
                if s >= 1:
                    r = s - 1
                    pe.wait_ge(moe_vec.sem, moe_vec.after(blk, "p", r))
                    nc.tensor.matmul(ybank[:], e_w2[:, r // FC, r % FC, :], p[:, r % 2, :],
                                     start=False, stop=(r == STEPS - 1)).then_inc(moe_y.sem, 1)

            @staticmethod
            def moe_out(pe, blk):
                pe.wait_ge(moe_act.sem, moe_act.after(blk, "yF"))
                turn_back(pe, yF, gate[0]).then_inc(moe_y.sem, 1)

            @staticmethod
            def conv(pe, blk):
                pe.wait_ge(moe_vec.sem, moe_vec.after(blk, "apply", T - 1))
                turn(pe, x2_t, tr).then_inc(conv_pe.sem, 1)
                pe.wait_ge(conv_vec.sem, conv_vec.after(blk, "c2"))
                turn_back(pe, c2[:, 0].rearrange("p s n -> p (s n)"), tr).then_inc(conv_pe.sem, 1)

            @staticmethod
            def att(pe, blk, i):
                if i == 0:
                    pe.wait_ge(conv_vec.sem, conv_vec.after(blk, "shift"))
                    pe.wait_ge(later, 16 * LATER)
                else:
                    pe.wait_ge(att_vec.sem, att_vec.after(blk, f"{i - 1}shift"))
                turn(pe, h_t, tr).then_inc(att_pe.sem, 1)
                pe.wait_ge(att_act.sem, att_act.after(blk, f"{i}hF"))
                for t in range(T):
                    if t >= 2:
                        pe.wait_ge(att_act.sem, att_act.after(blk, f"{i}v", t - 2))
                    nc.tensor.matmul(mb[t % 2][:, 0:3 * D], hF[:, t * P:(t + 1) * P], a_w[:, i, :], start=True, stop=False)
                    nc.tensor.matmul(mb[t % 2][:, 0:3 * D], one_rows[:], a_bs[:, i, :],
                                     start=False, stop=True).then_inc(att_pe.sem, 1)
                pe.wait_ge(att_pool.sem, att_pool.after(blk, f"{i}plus", SEQS - 1))
                pe.wait_ge(att_act.sem, att_act.after(blk, f"{i}v", T - 1))
                for s in range(SEQS):
                    for n in range(N // P):
                        mm = nc.tensor.matmul(mb[1][:, s * D:(s + 1) * D], mean_of[:], qk[:, s * (N // P) + n, 1, :],
                                              start=(n == 0), stop=(n == N // P - 1))
                mm.then_inc(att_pe.sem, 1)
                pe.wait_ge(att_vec.sem, att_vec.after(blk, f"{i}rot", SEQS - 1))
                for s in range(SEQS):
                    for n in range(N // P):
                        t = s * (N // P) + n
                        mm = nc.tensor.matmul(mb[0][:, s * D:(s + 1) * D], rot[:, t, 1, :], vt[:, t, :],
                                              start=(n == 0), stop=(n == N // P - 1))
                mm.then_inc(att_pe.sem, 1)
                turn(pe, rot[:, :, 0, :], tr).then_inc(att_pe.sem, 1)
                pe.wait_ge(att_act.sem, att_act.after(blk, f"{i}qF"))
                pe.wait_ge(att_vec.sem, att_vec.after(blk, f"{i}kvm"))
                for t in range(T):
                    mm = nc.tensor.matmul(mb[0][:, t * P:(t + 1) * P], qF[:, t * P:(t + 1) * P], kvm[:, t // (N // P), :],
                                          start=True, stop=True)
                mm.then_inc(att_pe.sem, 1)

            @staticmethod
            def ffn(pe, blk):
                pe.wait_ge(att_vec.sem, att_vec.before(blk + 1))
                turn(pe, h_t, tr).then_inc(ffn_pe.sem, 1)
                pe.wait_ge(ffn_act.sem, ffn_act.after(blk, "hF"))
                for j in range(FC):
                    if j >= 2:
                        pe.wait_ge(ffn_act.sem, ffn_act.after(blk, "gelu", j - 2))
                    nc.tensor.matmul(mb[j % 2][:], f_w1[:, j * P:(j + 1) * P], hF[:], start=True, stop=True).then_inc(ffn_pe.sem, 1)
                for j in range(FC):
                    pe.wait_ge(ffn_act.sem, ffn_act.after(blk, "gelu", j))
                    mm = nc.tensor.matmul(tr[:], f_w2[:, j, :], ffh[:, j, :], start=(j == 0), stop=(j == FC - 1))
                mm.then_inc(ffn_pe.sem, 1)
                pe.wait_ge(ffn_act.sem, ffn_act.after(blk, "fF"))
                turn_back(pe, hF, mb[0]).then_inc(ffn_pe.sem, 1)

            @staticmethod
            def ter(pe, blk):
                pe.wait_ge(ffn_vec.sem, ffn_vec.before(blk + 1))
                turn(pe, x3_t, gate[0]).then_inc(ter_pe.sem, 1)
                pe.wait_ge(ter_act.sem, ter_act.after(blk, "x3F"))
                for c in range(FC):
                    if c >= 2:
                        pe.wait_ge(ter_act.sem, ter_act.after(blk, "silu", c - 2))
                        pe.wait_ge(ter_vec.sem, ter_vec.after(blk, "h", c - 2))
                    nc.tensor.matmul(gate[c % 2][:], t_w12[:, 0, c * P:(c + 1) * P], x3F[:], start=True, stop=True)
                    nc.tensor.matmul(up[c % 2][:], t_w12[:, 1, c * P:(c + 1) * P], x3F[:],
                                     start=True, stop=True).then_inc(ter_pe.sem, 1)
                for w, (src, name) in enumerate(((tA, "g1"), (tB, "g2"))):
                    for c in range(FC):
                        if w == 0:
                            pe.wait_ge(ter_act.sem, ter_act.after(blk, "silu", FC - 1) if c < 2 else ter_act.after(blk, name, c - 2))
                            pe.wait_ge(ter_vec.sem, ter_vec.after(blk, "h", FC - 1))
                        else:
                            pe.wait_ge(ter_act.sem, ter_act.after(blk, "g1", FC - 1) if c < 2 else ter_act.after(blk, name, c - 2))
                        for k in range(FC):
                            mm = nc.tensor.matmul(gate[c % 2][:], t_h[:, w, k, c * P:(c + 1) * P], src[:, k, :],
                                                  start=(k == 0), stop=(k == FC - 1))
                        mm.then_inc(ter_pe.sem, 1)
                for k in range(FC):
                    pe.wait_ge(ter_act.sem, ter_act.after(blk, "g2", k))
                    mm = nc.tensor.matmul(ybank[:], t_w3[:, k, :], tA[:, k, :], start=(k == 0), stop=(k == FC - 1))
                mm.then_inc(ter_pe.sem, 1)
                pe.wait_ge(ter_act.sem, ter_act.after(blk, "yF"))
                turn_back(pe, x3F, up[0]).then_inc(ter_pe.sem, 1)

        class Act:
            @staticmethod
            def setup(act):
                act.wait_ge(set_pe, 1)
                nc.scalar.copy(wqkv0[:], tr[:, 0:3 * D]).then_inc(set_act, 1)
                act.wait_ge(set_pe, 2)
                nc.scalar.copy(cols[:], mb[0][:, 0:NROWS]).then_inc(set_act, 1)

            @staticmethod
            def ternary(act):
                for n, (_, _, dst) in enumerate(groups):
                    act.wait_ge(set_pe, 2 + n + 1)
                    nc.scalar.copy(dst, gate[n % 2][:]).then_inc(set_act, 1)

            @staticmethod
            def mix(act, blk):
                act.wait_ge(mix_pe.sem, mix_pe.after(blk, "xT"))
                nc.scalar.copy(hF[:], tr[:]).then_inc(mix_act.sem, 1)
                for t in range(T):
                    act.wait_ge(mix_pe.sem, mix_pe.after(blk, "qkv", t))
                    nc.scalar.copy(qkv[:, t].rearrange("p c d -> p (c d)"), mb[t % 2][:, 0:3 * D]).then_inc(mix_act.sem, 1)

            @staticmethod
            def route(act, blk):
                act.wait_ge(route_pe.sem, route_pe.after(blk, "x1T"))
                nc.scalar.copy(x1F[:], tr[:]).then_inc(route_act.sem, 1)
                act.wait_ge(route_vec.sem, route_vec.after(blk, "shift"))
                nc.scalar.activation(hg[:], hr[:], ACT.Gelu_apprx_tanh).then_inc(route_act.sem, 1)
                act.wait_ge(route_pe.sem, route_pe.after(blk, "hT"))
                nc.scalar.copy(hT[:], tr[0:R, :]).then_inc(route_act.sem, 1)
                act.wait_ge(route_vec.sem, route_vec.after(blk, "less_max"))
                nc.scalar.activation(lex[:], lex[:], ACT.Exp).then_inc(route_act.sem, 1)
                act.wait_ge(route_pe.sem, route_pe.after(blk, "wT"))
                nc.scalar.copy(wT[:], tr[0:E, :]).then_inc(route_act.sem, 1)

            @staticmethod
            def moe_spread(act, blk):
                for k in range(E // 2):
                    act.wait_ge(moe_pe.sem, moe_pe.after(blk, "wB", 2 * k))
                    nc.scalar.copy(wB[:, 2 * k, :], gate[k % 2][:]).then_inc(moe_act.sem, 1)

            @staticmethod
            def moe_step(act, blk, s):
                e, j = divmod(s, FC)
                act.wait_ge(moe_gate.sem, moe_gate.after(blk, "gate", s))
                if s >= 3:
                    act.wait_ge(moe_pool.sem, moe_pool.after(blk, "gw", s - 3))
                nc.scalar.activation(g[:, s % 3, :], gate[s % 2][:], ACT.Gelu_apprx_tanh,
                                     bias=col("e_b1", e * 2 * FC + FC + j)).then_inc(moe_act.sem, 1)

            @staticmethod
            def moe_out(act, blk):
                act.wait_ge(moe_y.sem, moe_y.after(blk, "y", STEPS - 1))
                nc.scalar.copy(yF[:], ybank[:]).then_inc(moe_act.sem, 1)

            @staticmethod
            def conv(act, blk):
                act.wait_ge(conv_pe.sem, conv_pe.after(blk, "x2T"))
                nc.scalar.copy(x2F[:, :, PAD:PAD + N], tr[:].rearrange("p (s n) -> p s n", s=SEQS)).then_inc(conv_act.sem, 1)
                for j in range(4):
                    act.wait_ge(conv_vec.sem, conv_vec.after(blk, "tap1", 4 * (TAPS - 1) + j))
                    nc.scalar.activation(c1F[:, j, :, PAD:PAD + N], c1[:, j], ACT.Gelu, bias=c1_b[:, j:j + 1]).then_inc(conv_act.sem, 1)

            @staticmethod
            def att(act, blk, i):
                act.wait_ge(att_pe.sem, att_pe.after(blk, f"{i}hT"))
                nc.scalar.copy(hF[:], tr[:]).then_inc(att_act.sem, 1)
                for t in range(T):
                    act.wait_ge(att_pe.sem, att_pe.after(blk, f"{i}qkv", t))
                    nc.scalar.activation(qk[:, t].rearrange("p c d -> p (c d)"), mb[t % 2][:, 0:2 * D], ACT.Gelu)
                    nc.scalar.copy(vt[:, t, :], mb[t % 2][:, 2 * D:3 * D]).then_inc(att_act.sem, 1)
                act.wait_ge(att_pe.sem, att_pe.after(blk, f"{i}qT"))
                nc.scalar.copy(qF[:], tr[:]).then_inc(att_act.sem, 1)

            @staticmethod
            def ffn(act, blk):
                act.wait_ge(ffn_pe.sem, ffn_pe.after(blk, "hT"))
                nc.scalar.copy(hF[:], tr[:]).then_inc(ffn_act.sem, 1)
                for j in range(FC):
                    act.wait_ge(ffn_pe.sem, ffn_pe.after(blk, "up", j))
                    nc.scalar.activation(ffh[:, j, :], mb[j % 2][:], ACT.Gelu, bias=col("f_b1", j)).then_inc(ffn_act.sem, 1)
                act.wait_ge(ffn_pe.sem, ffn_pe.after(blk, "down"))
                nc.scalar.activation(hF[:], tr[:], ACT.Identity, bias=col("f_b2")).then_inc(ffn_act.sem, 1)

            @staticmethod
            def ter(act, blk):
                act.wait_ge(ter_pe.sem, ter_pe.after(blk, "x3T"))
                nc.scalar.copy(x3F[:], gate[0][:]).then_inc(ter_act.sem, 1)
                for c in range(FC):
                    act.wait_ge(ter_pe.sem, ter_pe.after(blk, "gu", c))
                    if c >= 2:
                        act.wait_ge(ter_vec.sem, ter_vec.after(blk, "h", c - 2))
                    nc.scalar.activation(u[:, c % 2, :], gate[c % 2][:], ACT.Silu, scale=col("w1_s", c)).then_inc(ter_act.sem, 1)
                for name, rows_, dst in (("h1", "h1_s", tB), ("h2", "h2_s", tA)):
                    for c in range(FC):
                        act.wait_ge(ter_pe.sem, ter_pe.after(blk, name, c))
                        if name == "h2" and c == 0:
                            act.wait_ge(ter_pe.sem, ter_pe.after(blk, "h1", FC - 1))
                        nc.scalar.activation(dst[:, c, :], gate[c % 2][:], ACT.Gelu, scale=col(rows_, c)).then_inc(ter_act.sem, 1)
                act.wait_ge(ter_pe.sem, ter_pe.after(blk, "w3"))
                nc.scalar.activation(x3F[:], ybank[:], ACT.Identity, scale=col("w3_s")).then_inc(ter_act.sem, 1)

        class Vec:
            @staticmethod
            def setup(dve):
                nc.vector.memset(minus_half[:], -0.5).then_inc(begun, 1)
                nc.vector.memset(x2F[:], 0.0).then_inc(begun, 1)
                nc.vector.memset(c1F[:].rearrange("p j s n -> p (j s n)"), 0.0).then_inc(begun, 1)
                nc.vector.memset(a_bs[:].rearrange("p l n -> p (l n)").bitcast(F32), 0.0).then_inc(begun, 1)
                nc.vector.memset(one_rows[:].bitcast(F32), 0.0).then_inc(begun, 1)
                dve.wait_ge(begun, 5)
                nc.vector.memset(one_rows[0:1, :].bitcast(F32), 1.0).then_inc(begun, 1)
                nc.vector.memset(one_rows[32:33, :].bitcast(F32), 1.0).then_inc(begun, 1)
                dve.wait_ge(early, 16 * EARLY)
                nc.vector.tensor_copy(a_bs[0:1], a_b).then_inc(begun, 1)
                dve.wait_ge(begun, 8)
                nc.vector.tensor_tensor(a_bs[32:33], a_b, a_bs[0:1].bitcast(F32), ALU.subtract).then_inc(begun, 1)

            @staticmethod
            def mix(dve, blk):
                s = mix_vec.sem
                qk0 = qkv[:, :, 0:2, :]
                dve.wait_ge(mix_act.sem, mix_act.after(blk, "qkv", T - 1))
                nc.vector.tensor_tensor(big[:], qk0, qk0, ALU.mult).then_inc(s, 1)
                dve.wait_ge(s, mix_vec.after(blk, "square"))
                nc.vector.tensor_reduce(ssq[:], big[:], AX.X, ALU.add).then_inc(s, 1)
                dve.wait_ge(s, mix_vec.after(blk, "ssq"))
                nc.vector.tensor_scalar(ssq[:], ssq[:], 1e-24, None, ALU.max).then_inc(s, 1)
                dve.wait_ge(mix_pool.sem, mix_pool.after(blk, "len"))
                for t in range(T):
                    nc.vector.scalar_tensor_tensor(out=vt[:, t, :], in0=qkv[:, t, 1, :], scalar=rn[:, t, 1:2],
                                                   in1=qkv[:, t, 2, :], op0=ALU.mult, op1=ALU.mult).then_inc(s, 1)
                dve.wait_ge(mix_pe.sem, mix_pe.after(blk, "mean"))
                for t in range(T):
                    q = t // (N // P)
                    nc.vector.scalar_tensor_tensor(out=sum_t[:, t, :], in0=qkv[:, t, 0, :], scalar=rn[:, t, 0:1],
                                                   in1=mb[0][:, q * D:(q + 1) * D], op0=ALU.mult, op1=ALU.mult).then_inc(s, 1)
                dve.wait_ge(s, mix_vec.after(blk, "q", T - 1))
                nc.vector.tensor_tensor(sum_t[:], sum_t[:], x_t[:], ALU.add).then_inc(s, 1)
                dve.wait_ge(s, mix_vec.after(blk, "sum"))
                norm_vec(dve, mix_vec, blk, "", sum_t, x1_t, 1e-5, (mix_pool, "rstd"))

            @staticmethod
            def route(dve, blk):
                s = route_vec.sem

                def after(name):
                    dve.wait_ge(s, route_vec.after(blk, name))

                dve.wait_ge(route_pe.sem, route_pe.after(blk, "h"))
                nc.vector.tensor_tensor(hr[:], mb[0][:, 0:T * R].rearrange("p (t d) -> p t d", t=T),
                                        br1[:].unsqueeze(1).to_broadcast([P, T, R]), ALU.add).then_inc(s, 1)
                after("h")
                norm_vec(dve, route_vec, blk, "", hr, hr[:], 1e-6, (route_pool, "rstd"), (r_g[:], r_b[:]))
                dve.wait_ge(route_pe.sem, route_pe.after(blk, "logit"))
                nc.vector.tensor_tensor(lg[:], mb[1][:, 0:T * E].rearrange("p (t e) -> p t e", t=T),
                                        br2[:].unsqueeze(1).to_broadcast([P, T, E]), ALU.add).then_inc(s, 1)
                full = [P, T, E, E]
                other, own = lg[:].unsqueeze(2).to_broadcast(full), lg[:].unsqueeze(3).to_broadcast(full)
                after("logit")
                nc.vector.tensor_tensor(cmp1[:], other, own, ALU.is_gt).then_inc(s, 1)
                nc.vector.tensor_tensor(cmp2[:], other, own, ALU.is_equal).then_inc(s, 1)
                after("tie")
                nc.vector.tensor_tensor(cmp2[:], cmp2[:], earlier[:].unsqueeze(1).to_broadcast(full), ALU.mult).then_inc(s, 1)
                after("tie_earlier")
                nc.vector.tensor_tensor(cmp1[:], cmp1[:], cmp2[:], ALU.add).then_inc(s, 1)
                after("beats")
                nc.vector.tensor_reduce(rank[:], cmp1[:], AX.X, ALU.add).then_inc(s, 1)
                after("rank")
                nc.vector.tensor_scalar(rank[:], rank[:], 1.5, None, ALU.is_lt).then_inc(s, 1)
                nc.vector.tensor_reduce(lmax[:], lg[:], AX.X, ALU.max).then_inc(s, 1)
                after("max")
                nc.vector.tensor_tensor(lex[:], lg[:], lmax[:].unsqueeze(2).to_broadcast([P, T, E]), ALU.subtract).then_inc(s, 1)
                dve.wait_ge(route_act.sem, route_act.after(blk, "exp"))
                nc.vector.tensor_tensor(lex[:], lex[:], rank[:], ALU.mult).then_inc(s, 1)
                after("keep")
                nc.vector.tensor_reduce(lmax[:], lex[:], AX.X, ALU.add).then_inc(s, 1)
                after("total")
                nc.vector.reciprocal(lmax[:], lmax[:]).then_inc(s, 1)
                after("recip")
                nc.vector.tensor_tensor(wts[:], lex[:], lmax[:].unsqueeze(2).to_broadcast([P, T, E]), ALU.mult).then_inc(s, 1)

            @staticmethod
            def moe_spread(dve, blk):
                for k in range(E // 2):
                    dve.wait_ge(moe_pe.sem, moe_pe.after(blk, "wB", 2 * k + 1))
                    nc.vector.tensor_copy(wB[:, 2 * k + 1, :], up[k % 2][:]).then_inc(moe_vec.sem, 1)

            @staticmethod
            def moe_step(dve, blk, s):
                e, j = divmod(s, FC)
                dve.wait_ge(moe_up.sem, moe_up.after(blk, "up", s))
                dve.wait_ge(moe_pool.sem, moe_pool.after(blk, "gw", s))
                if s >= 2:
                    dve.wait_ge(moe_y.sem, moe_y.after(blk, "y", s - 2))
                nc.vector.scalar_tensor_tensor(out=p[:, s % 2, :], in0=up[s % 2][:], scalar=col("e_b1", e * 2 * FC + j),
                                               in1=gw[:, s % 2, :], op0=ALU.add, op1=ALU.mult).then_inc(moe_vec.sem, 1)

            @staticmethod
            def moe_out(dve, blk):
                s = moe_vec.sem
                dve.wait_ge(moe_y.sem, moe_y.after(blk, "yT"))
                nc.vector.tensor_tensor(sum_t[:], tok(gate[0]), x1_t[:], ALU.add).then_inc(s, 1)
                dve.wait_ge(s, moe_vec.after(blk, "sum"))
                norm_vec(dve, moe_vec, blk, "", sum_t, x2_t, 1e-5, (moe_pool, "rstd"))

            @staticmethod
            def conv(dve, blk):
                s = conv_vec.sem
                dve.wait_ge(conv_act.sem, conv_act.after(blk, "x2F"))
                dve.wait_ge(later, 16 * LATER)
                for k in range(TAPS):
                    for j in range(4):
                        src = x2F[:, :, k:k + N]
                        if k == 0:
                            nc.vector.tensor_scalar(c1[:, j], src, c1_w[:, j, k:k + 1], None, ALU.mult).then_inc(s, 1)
                        else:
                            dve.wait_ge(s, conv_vec.after(blk, "tap1", 4 * (k - 1) + j))
                            nc.vector.scalar_tensor_tensor(out=c1[:, j], in0=src, scalar=c1_w[:, j, k:k + 1], in1=c1[:, j],
                                                           op0=ALU.mult, op1=ALU.add).then_inc(s, 1)
                for j in range(4):
                    dve.wait_ge(conv_act.sem, conv_act.after(blk, "gelu", j))
                    for k in range(TAPS):
                        n = j * TAPS + k
                        src, w = c1F[:, j, :, k:k + N], c2_w[:, j, k:k + 1]
                        if n == 0:
                            nc.vector.tensor_scalar(c2[:, 0], src, w, col("c2_b"), ALU.mult, ALU.add).then_inc(s, 1)
                        elif n == 1:
                            nc.vector.tensor_scalar(c2[:, 1], src, w, None, ALU.mult).then_inc(s, 1)
                        else:
                            dve.wait_ge(s, conv_vec.after(blk, "tap2", n - 2))
                            nc.vector.scalar_tensor_tensor(out=c2[:, n % 2], in0=src, scalar=w, in1=c2[:, n % 2],
                                                           op0=ALU.mult, op1=ALU.add).then_inc(s, 1)
                dve.wait_ge(s, conv_vec.after(blk, "tap2", 4 * TAPS - 1))
                nc.vector.tensor_tensor(c2[:, 0], c2[:, 0], c2[:, 1], ALU.add).then_inc(s, 1)
                dve.wait_ge(conv_pe.sem, conv_pe.after(blk, "c2T"))
                nc.vector.tensor_tensor(sum_t[:], tok(tr), x2_t[:], ALU.add).then_inc(s, 1)
                dve.wait_ge(s, conv_vec.after(blk, "sum"))
                norm_vec(dve, conv_vec, blk, "", sum_t, h_t[:], 1e-12, (conv_pool, "rstd"), (gains[:, 0], shifts[:, 0]))

            @staticmethod
            def att(dve, blk, i):
                s = att_vec.sem

                def after(name, k=0):
                    dve.wait_ge(s, att_vec.after(blk, f"{i}{name}", k))

                half = N // P
                for q in range(SEQS):
                    dve.wait_ge(att_pool.sem, att_pool.after(blk, f"{i}plus", q))
                    for odd in range(2):
                        nc.vector.tensor_tensor(
                            rot[:, q * half:(q + 1) * half, :, odd::2], qk[:, q * half:(q + 1) * half, :, 1 - odd::2],
                            sin[:, :, odd::2].unsqueeze(2).to_broadcast([P, half, 2, D // 2]), ALU.mult).then_inc(s, 1)
                for q in range(SEQS):
                    dve.wait_ge(att_pool.sem, att_pool.after(blk, f"{i}cos", q))
                    after("swap", 2 * q + 1)
                    r = rot[:, q * half:(q + 1) * half]
                    nc.vector.tensor_tensor(r, r, big[:, q * half:(q + 1) * half], ALU.add).then_inc(s, 1)
                dve.wait_ge(att_pe.sem, att_pe.after(blk, f"{i}kmean"))
                for q in range(SEQS):
                    nc.vector.tensor_tensor(den[:, q * half:(q + 1) * half, :], qk[:, q * half:(q + 1) * half, 0, :],
                                            mb[1][:, q * D:(q + 1) * D].unsqueeze(1).to_broadcast([P, half, D]),
                                            ALU.mult).then_inc(s, 1)
                after("den", SEQS - 1)
                nc.vector.tensor_reduce(z[:], den[:].rearrange("p t (h e) -> p (t h) e", e=HD), AX.X, ALU.add).then_inc(s, 1)
                after("head")
                nc.vector.tensor_scalar(z[:], z[:], 1e-6, None, ALU.add).then_inc(s, 1)
                after("eps6")
                nc.vector.reciprocal(z[:], z[:]).then_inc(s, 1)
                dve.wait_ge(att_pe.sem, att_pe.after(blk, f"{i}kv"))
                nc.vector.tensor_tensor(kvm[:], mb[0][:, 0:SEQS * D].rearrange("p (s d) -> p s d", s=SEQS),
                                        headmask[:].unsqueeze(1).to_broadcast([P, SEQS, D]), ALU.mult).then_inc(s, 1)
                dve.wait_ge(att_pe.sem, att_pe.after(blk, f"{i}o"))
                after("z")
                heads = [P, T * HEADS, HD]
                nc.vector.tensor_tensor(sum_t[:].rearrange("p t (h e) -> p (t h) e", e=HD),
                                        mb[0][:].rearrange("p (h e) -> p h e", e=HD),
                                        z[:].unsqueeze(2).to_broadcast(heads), ALU.mult).then_inc(s, 1)
                after("oz")
                nc.vector.tensor_tensor(sum_t[:], sum_t[:], h_t[:], ALU.add).then_inc(s, 1)
                after("sum")
                norm_vec(dve, att_vec, blk, str(i), sum_t, h_t[:], 1e-12, (att_pool, f"{i}rstd"),
                         (gains[:, 1 + i], shifts[:, 1 + i]))

            @staticmethod
            def ffn(dve, blk):
                s = ffn_vec.sem
                dve.wait_ge(ffn_pe.sem, ffn_pe.after(blk, "fT"))
                nc.vector.tensor_tensor(sum_t[:], tok(mb[0]), h_t[:], ALU.add).then_inc(s, 1)
                dve.wait_ge(s, ffn_vec.after(blk, "sum"))
                norm_vec(dve, ffn_vec, blk, "i", sum_t, h_t[:], 1e-12, (ffn_pool, "irstd"), (gains[:, L + 1], shifts[:, L + 1]))
                dve.wait_ge(s, ffn_vec.after(blk, "ishift"))
                nc.vector.tensor_tensor(sum_t[:], h_t[:], x2_t[:], ALU.add).then_inc(s, 1)
                dve.wait_ge(s, ffn_vec.after(blk, "sum2"))
                norm_vec(dve, ffn_vec, blk, "o", sum_t, x3_t, 1e-5, (ffn_pool, "orstd"))

            @staticmethod
            def ter(dve, blk):
                s = ter_vec.sem
                for c in range(FC):
                    dve.wait_ge(ter_pe.sem, ter_pe.after(blk, "gu", c))
                    dve.wait_ge(ter_act.sem, ter_act.after(blk, "silu", c))
                    nc.vector.scalar_tensor_tensor(out=tA[:, c, :], in0=up[c % 2][:], scalar=col("w2_s", c), in1=u[:, c % 2, :],
                                                   op0=ALU.mult, op1=ALU.mult).then_inc(s, 1)
                dve.wait_ge(ter_pe.sem, ter_pe.after(blk, "yT"))
                nc.vector.tensor_tensor(sum_t[:], tok(up[0]), x3_t[:], ALU.add).then_inc(s, 1)
                dve.wait_ge(s, ter_vec.after(blk, "sum"))
                dve.wait_ge(out_put.sem, out_put.before(blk))
                norm_vec(dve, ter_vec, blk, "", sum_t, o_t, 1e-5, (ter_pool, "rstd"))

        class Pool:
            @staticmethod
            def mix(pool, blk):
                pool.wait_ge(begun, 1)
                pool.wait_ge(mix_vec.sem, mix_vec.after(blk, "clip"))
                nc.gpsimd.tensor_tensor(rn[:].rearrange("p t c -> p (t c)"), ssq[:].rearrange("p t c -> p (t c)"),
                                        minus_half[:], ALU.pow).then_inc(mix_pool.sem, 1)
                norm_pool(pool, mix_pool, blk, "rstd", mix_vec, "eps")

            @staticmethod
            def route(pool, blk):
                norm_pool(pool, route_pool, blk, "rstd", route_vec, "eps")

            @staticmethod
            def moe_step(pool, blk, s):
                e = s // FC
                if s == 0:
                    pool.wait_ge(moe_vec.sem, moe_vec.after(blk, "wB", E // 2 - 1))
                pool.wait_ge(moe_act.sem, moe_act.after(blk, "gelu", s))
                if s >= 2:
                    pool.wait_ge(moe_vec.sem, moe_vec.after(blk, "p", s - 2))
                nc.gpsimd.tensor_tensor(gw[:, s % 2, :], g[:, s % 3, :], wB[:, e, :], ALU.mult).then_inc(moe_pool.sem, 1)

            @staticmethod
            def moe_out(pool, blk):
                norm_pool(pool, moe_pool, blk, "rstd", moe_vec, "eps")

            @staticmethod
            def conv(pool, blk):
                norm_pool(pool, conv_pool, blk, "rstd", conv_vec, "eps")

            @staticmethod
            def att(pool, blk, i):
                half = N // P
                for q in range(SEQS):
                    wait_apart(pool, att_act.sem, att_act.after(blk, f"{i}v", half * (q + 1) - 1))
                    v = qk[:, q * half:(q + 1) * half]
                    nc.gpsimd.tensor_scalar(v, v, 0.21, None, ALU.add).then_inc(att_pool.sem, 1)
                for q in range(SEQS):
                    pool.wait_ge(att_pool.sem, att_pool.after(blk, f"{i}plus", q))
                    nc.gpsimd.tensor_tensor(big[:, q * half:(q + 1) * half], qk[:, q * half:(q + 1) * half],
                                            cos[:].unsqueeze(2).to_broadcast([P, half, 2, D]), ALU.mult).then_inc(att_pool.sem, 1)
                norm_pool(pool, att_pool, blk, f"{i}rstd", att_vec, f"{i}eps")

            @staticmethod
            def ffn(pool, blk):
                norm_pool(pool, ffn_pool, blk, "irstd", ffn_vec, "ieps")
                norm_pool(pool, ffn_pool, blk, "orstd", ffn_vec, "oeps")

            @staticmethod
            def ter(pool, blk):
                norm_pool(pool, ter_pool, blk, "rstd", ter_vec, "eps")

        @block.sync
        def _(sp):
            begin(sp, x_got, out_put)
            assert load_early(sp) == EARLY
            load_experts(sp)
            assert load_later(sp) == LATER
            load_ternary(sp)
            with sp.Fori(0, BLOCKS) as blk:
                Sync.block(sp, blk)
                Sync.put(sp, blk)
            sp.wait_ge(out_put.sem, out_put.before(BLOCKS))

        @block.tensor
        def _(pe):
            begin(pe, mix_pe, route_pe, moe_pe, moe_gate, moe_up, moe_y, conv_pe, att_pe, ffn_pe, ter_pe)
            Pe.setup(pe)
            Pe.ternary(pe)
            with pe.Fori(0, BLOCKS) as blk:
                Pe.mix(pe, blk)
                Pe.route(pe, blk)
                Pe.moe_spread(pe, blk)
                for s in range(STEPS + 1):
                    Pe.moe_step(pe, blk, s)
                Pe.moe_out(pe, blk)
                Pe.conv(pe, blk)
                for i in range(L):
                    Pe.att(pe, blk, i)
                Pe.ffn(pe, blk)
                Pe.ter(pe, blk)

        @block.scalar
        def _(act):
            begin(act, mix_act, route_act, moe_act, conv_act, att_act, ffn_act, ter_act)
            Act.setup(act)
            Act.ternary(act)
            with act.Fori(0, BLOCKS) as blk:
                Act.mix(act, blk)
                Act.route(act, blk)
                Act.moe_spread(act, blk)
                for s in range(STEPS):
                    Act.moe_step(act, blk, s)
                Act.moe_out(act, blk)
                Act.conv(act, blk)
                for i in range(L):
                    Act.att(act, blk, i)
                Act.ffn(act, blk)
                Act.ter(act, blk)

        @block.vector
        def _(dve):
            begin(dve, mix_vec, route_vec, moe_vec, conv_vec, att_vec, ffn_vec, ter_vec)
            Vec.setup(dve)
            with dve.Fori(0, BLOCKS) as blk:
                Vec.mix(dve, blk)
                Vec.route(dve, blk)
                Vec.moe_spread(dve, blk)
                for s in range(STEPS):
                    Vec.moe_step(dve, blk, s)
                Vec.moe_out(dve, blk)
                Vec.conv(dve, blk)
                for i in range(L):
                    Vec.att(dve, blk, i)
                Vec.ffn(dve, blk)
                Vec.ter(dve, blk)

        @block.gpsimd
        def _(pool):
            begin(pool, mix_pool, route_pool, moe_pool, conv_pool, att_pool, ffn_pool, ter_pool)
            with pool.Fori(0, BLOCKS) as blk:
                Pool.mix(pool, blk)
                Pool.route(pool, blk)
                for s in range(STEPS):
                    Pool.moe_step(pool, blk, s)
                Pool.moe_out(pool, blk)
                Pool.conv(pool, blk)
                for i in range(L):
                    Pool.att(pool, blk, i)
                Pool.ffn(pool, blk)
                Pool.ter(pool, blk)


_INS = ["L0_attn_x", "L0_attn_W_q", "L0_attn_W_k", "L0_attn_W_v", "L0_ffn_Wr1", "L0_ffn_br1", "L0_ffn_ln_scale",
        "L0_ffn_ln_bias", "L0_ffn_Wr2", "L0_ffn_br2", "L0_ffn_W1", "L0_ffn_b1", "L0_ffn_W2", "L0_ffn_b2",
        "L1_attn_conv1_w", "L1_attn_conv1_b", "L1_attn_conv2_w", "L1_attn_conv2_b", "L1_attn_ln0_g", "L1_attn_ln0_b",
        "L1_attn_Wq", "L1_attn_bq", "L1_attn_Wk", "L1_attn_bk", "L1_attn_Wv", "L1_attn_bv", "L1_attn_lnA_g",
        "L1_attn_lnA_b", "L1_attn_W1", "L1_attn_b1", "L1_attn_W2", "L1_attn_b2", "L1_attn_ln2_g", "L1_attn_ln2_b",
        "L1_ffn_w1_w", "L1_ffn_w1_s", "L1_ffn_w2_w", "L1_ffn_w2_s", "L1_ffn_h1_w", "L1_ffn_h1_s", "L1_ffn_h2_w",
        "L1_ffn_h2_s", "L1_ffn_w3_w", "L1_ffn_w3_s"]


def constants():
    f = np.float32
    inv = f(1.0) / f(10000.0) ** (np.arange(0, D, 2, dtype=f) / f(D))
    freqs = np.repeat(np.arange(N, dtype=f)[:, None] * inv[None, :], 2, axis=-1)
    sign = np.where(np.arange(D) % 2 == 0, f(-1), f(1))
    tiles = lambda m: np.ascontiguousarray(m.reshape(N // P, P, D).transpose(1, 0, 2)).astype(f)
    head = np.arange(D) // HD
    e = np.arange(E)
    pick = np.zeros((E, E, P), f)
    pick[e, e, :] = 1
    return {
        "c_ident": np.eye(P, dtype=f),
        "c_mean_of": np.full((P, P), 1.0 / N, f),
        "c_headmask": np.where(head[:, None] == head[None, :], f(1.0 / N), f(0)).astype(f),
        "c_cos": tiles(np.cos(freqs)),
        "c_sin": tiles(np.sin(freqs) * sign),
        "c_earlier": np.broadcast_to((e[None, :] < e[:, None]).astype(f), (P, E, E)).copy(),
        "c_pick": pick,
    }


def kernel(**inputs):
    import concourse.bacc as _bacc
    from concourse.bass_utils import run_bass_kernel_spmd as _run

    nc = _bacc.Bacc("TRN2", target_bir_lowering=False, num_devices=1)
    arrays, aps = {}, {}
    for name, value in {**{n: inputs[n] for n in _INS}, **constants()}.items():
        v = np.ascontiguousarray(value)
        arrays[f"in_{name}_dram"] = v
        aps[name] = nc.dram_tensor(f"in_{name}_dram", v.shape, mybir.dt.from_np(v.dtype), kind="ExternalInput").ap()
    out = nc.dram_tensor("out_0_dram", (B, N, D), F32, kind="ExternalOutput").ap()
    build(nc, aps["L0_attn_x"].rearrange("b n d -> (b n) d"), out.rearrange("b n d -> (b n) d"), aps)
    r = _run(nc, [arrays], core_ids=[0])
    return r.results[0]["out_0_dram"]
```

```python
from contextlib import ExitStack

import numpy as np

import concourse.bass as bass
from concourse import mybir

F32 = mybir.dt.float32
F32R = mybir.dt.float32r
ALU = mybir.AluOpType
ACT = mybir.ActivationFunctionType
AX = mybir.AxisListType

P = 128
B, N, D = 8, 256, 128
SEQS = 2
H = N // P
T = SEQS * H
W = T * P
BLOCKS = B // SEQS
E, F = 8, 512
FC = F // P
R = D // 2
L = 4
HEADS = 16
HD = D // HEADS
TAPS, PAD = 5, 2
STEPS = E * FC

ROWS = {}
_at = 0
for _name, _n in (("e_b1", 2 * FC * E), ("f_b1", FC), ("f_b2", 1), ("c2_b", 1), ("w1_s", FC), ("w2_s", FC),
                  ("h1_s", FC), ("h2_s", FC), ("w3_s", 1)):
    ROWS[_name] = (_at, _n)
    _at += _n
NROWS = _at


class Steps:

    def __init__(self, sem, *steps, unit=1):
        self.sem, self.unit, self.first, self.n = sem, unit, {}, 0
        for name, count in steps:
            self.first[name] = self.n
            self.n += count

    def after(self, blk, name, k=0):
        return self.before(blk) + (self.first[name] + k + 1) * self.unit

    def before(self, blk):
        return blk * (self.n * self.unit) + 1


def norm_steps(name, tiles, affine=False):
    s = [(name + "stats", tiles), (name + "aggr", tiles), (name + "eps", 1), (name + "apply", tiles)]
    return s + ([(name + "gain", 1), (name + "shift", 1)] if affine else [])


MIX_SLOTS, ROUTE_SLOTS, CONV_SLOTS, ATT_SLOTS, FFN_SLOTS = 11, 15, 17, 13, 14
MOE_SLOTS, MOE_OUT_SLOTS, TER_SLOTS = 5 + 2 * (STEPS + 2), 5, 25
BODY_SLOTS = CONV_SLOTS + L * ATT_SLOTS + FFN_SLOTS
HEAD_SLOTS = MIX_SLOTS + ROUTE_SLOTS


def weave(*threads):
    done = [0] * len(threads)
    for r in range(max(end for _, _, _, end in threads)):
        for i, (gen, slots, first, end) in enumerate(threads):
            due = slots if r >= end - 1 else max(0, slots * (r + 1 - first) // (end - first))
            while done[i] < due:
                next(gen, None)
                done[i] += 1
    for gen, _, _, _ in threads:
        assert next(gen, "end") == "end", "a stage has more slots than it says"


def chain(*gens):
    for gen in gens:
        yield from gen


def build(nc, x_in, out, a):
    ctx = ExitStack()
    with ctx:
        def sb(name, shape, dt=F32):
            return ctx.enter_context(nc.sbuf_tensor(name, shape, dt))

        def sem(name):
            return ctx.enter_context(nc.semaphore(name))

        def bank(name):
            return ctx.enter_context(nc.psum_tensor(name, [P, 512], F32))

        gate = [bank(f"gate{i}") for i in range(2)]
        up = bank("up")
        ybank = bank("ybank")
        ab = [[bank(f"seq{q}_{i}") for i in range(2)] for q in range(SEQS)]

        ident = sb("ident", [P, P])
        mean_of = sb("mean_of", [P, P])
        headmask = sb("headmask", [P, P])
        cos = sb("cos", [P, H, D])
        sin = sb("sin", [P, H, D])
        earlier = sb("earlier", [P, E, E])
        minus_half = sb("minus_half", [P, 2 * T])
        cols = sb("cols", [P, NROWS])
        wqkv0 = sb("wqkv0", [P, 3 * D])
        wr1 = sb("wr1", [P, R])
        wr2 = sb("wr2", [R, E])
        e_w1 = sb("e_w1", [P, E, 2 * F])
        e_w2 = sb("e_w2", [P, E, FC, D])
        e_b2 = sb("e_b2", [E, D])
        br1 = sb("br1", [P, R])
        r_g = sb("r_g", [P, R])
        r_b = sb("r_b", [P, R])
        br2 = sb("br2", [P, E])
        c1_w = sb("c1_w", [P, 4, TAPS])
        c1_b = sb("c1_b", [P, 4])
        c2_w = sb("c2_w", [P, 4, TAPS])
        gains = sb("gains", [P, L + 2, D])
        shifts = sb("shifts", [P, L + 2, D])
        a_w = sb("a_w", [P, L, 3 * D])
        a_bs = sb("a_bs", [32 + L, 3 * D], F32R)
        a_sel = sb("a_sel", [32 + L, L], F32R)
        f_w1 = sb("f_w1", [P, F])
        f_w2 = sb("f_w2", [P, FC, D])
        t_w12 = sb("t_w12", [P, 2, F])
        t_h = sb("t_h", [P, 2, FC, F])
        t_w3 = sb("t_w3", [P, FC, D])

        x_t = sb("x_t", [P, T, D])
        x1_t = sb("x1_t", [P, T, D])
        x1F = sb("x1F", [P, W])
        x2_t = sb("x2_t", [P, T, D])
        x3_t = sb("x3_t", [P, T, D])
        wT = sb("wT", [E, W])
        wB = sb("wB", [P, E, W])
        tA, tB = (wB[:].rearrange("p (a c) w -> p a c w", a=2)[:, i] for i in range(2))
        g = sb("g", [P, 2, W])
        gw = sb("gw", [P, 2, W])
        p = sb("p", [P, 2, W])
        u, x3F, yF, tyF = g, gw[:, 0], p[:, 0], p[:, 1]
        o_t = sb("o_t", [P, T, D])
        sumx = sb("sumx", [P, T, D])

        ROOM = 9 * 2 * P
        room = sb("room", [P, SEQS, ROOM])
        hh = sb("hh", [P, SEQS, 2, H * D])
        x2F = sb("x2F", [P, SEQS, N + 2 * PAD])
        sum_t = sb("sum_t", [P, SEQS, H, D])

        class Seq:

            def __init__(self, q):
                self.q, self.ts = q, slice(q * H, (q + 1) * H)
                self.a, self.b = ab[q]
                self.h_t = hh[:, q, 0].rearrange("p (t d) -> p t d", t=H)
                self.hF = hh[:, q, 1]
                self.c2 = hh[:, q]
                self.at = 0

                def part(n):
                    self.at += n
                    assert self.at <= ROOM
                    return room[:, q, self.at - n:self.at]

                self.qk, self.rot, self.big = (part(2 * N).rearrange("p (t c d) -> p t c d", t=H, c=2) for _ in range(3))
                self.vt, self.den = (part(N).rearrange("p (t d) -> p t d", t=H) for _ in range(2))
                self.qF = part(N)
                self.at = 0
                self.qkv = part(3 * N).rearrange("p (t c d) -> p t c d", t=H, c=3)
                self.sq = part(2 * N).rearrange("p (t c d) -> p t c d", t=H, c=2)
                self.kvt = part(N).rearrange("p (t d) -> p t d", t=H)
                self.at = 0
                self.hr, self.hg = (part(H * R).rearrange("p (t d) -> p t d", t=H) for _ in range(2))
                self.hT = part(N)
                self.cmp1, self.cmp2 = (part(H * E * E).rearrange("p (t e f) -> p t e f", t=H, e=E) for _ in range(2))
                self.at = 0
                self.c1 = part(4 * N).rearrange("p (j n) -> p j n", j=4)
                self.c1F = part(4 * (N + 2 * PAD)).rearrange("p (j n) -> p j n", j=4)
                self.at = 0
                self.ffh = part(FC * N).rearrange("p (c n) -> p c n", c=FC)
                self.ssq, self.rn = (sb(f"{n}{q}", [P, H, 2]) for n in ("ssq", "rn"))
                self.lg, self.rank, self.lex, self.wts = (sb(f"{n}{q}", [P, H, E]) for n in ("lg", "rank", "lex", "wts"))
                self.lmax = sb(f"lmax{q}", [P, H])
                self.z = sb(f"z{q}", [P, H * HEADS])
                self.kvm = sb(f"kvm{q}", [P, D])

        seqs = [Seq(q) for q in range(SEQS)]
        stat = [(sb(f"st{i}", [P, T, 6]), sb(f"mv{i}", [P, T, 2]), sb(f"ve{i}", [P, T]), sb(f"rs{i}", [P, T])) for i in range(3)]
        X = 2

        raw = room[:].rearrange("p q n -> p (q n)")
        wqkv0_raw = x3_t[:, 0:3, :]
        rows = x3_t[:, 3, :]
        a_b = sumx[:].rearrange("p t d -> p (t d)")[:, 0:3 * D]

        def col(name, k=0):
            return cols[:, ROWS[name][0] + k:ROWS[name][0] + k + 1]

        x_got = Steps(sem("x_got"), ("x", 1), unit=16)
        out_put = Steps(sem("out_put"), ("out", 1), unit=16)

        def pair(name, *steps):
            return [Steps(sem(f"{name}{q}"), *steps) for q in range(SEQS)]

        mix_pe = pair("mix_pe", ("xT", 1), ("qkv", H), ("mean", 1))
        mix_act = pair("mix_act", ("xF", 1), ("qkv", H))
        mix_vec = pair("mix_vec", ("square", 1), ("ssq", 1), ("clip", 1), ("kv", H), ("q", H), ("sum", 1), *norm_steps("", H))
        mix_pool = pair("mix_pool", ("len", 1), ("rstd", 1))
        route_pe = pair("route_pe", ("x1T", 1), ("h", 1), ("hT", 1), ("logit", 1), ("wT", 1))
        route_act = pair("route_act", ("x1F", 1), ("gelu", 1), ("hT", 1), ("exp", 1), ("wT", 1))
        route_vec = pair("route_vec", ("h", 1), *norm_steps("", H, True), ("logit", 1), ("above", 1), ("tie", 1),
                         ("tie_earlier", 1), ("beats", 1), ("rank", 1), ("chosen", 1), ("max", 1), ("less_max", 1),
                         ("keep", 1), ("total", 1), ("recip", 1), ("weight", 1))
        route_pool = pair("route_pool", ("rstd", 1))
        conv_pe = pair("conv_pe", ("x2T", 1), ("c2T", 1))
        conv_act = pair("conv_act", ("x2F", 1), ("gelu", 4))
        conv_vec = pair("conv_vec", ("tap1", 4 * TAPS), ("tap2", 4 * TAPS), ("c2", 1), ("sum", 1), *norm_steps("", H, True))
        conv_pool = pair("conv_pool", ("pad", 2), ("rstd", 1))
        att_pe = pair("att_pe", *[(f"{i}{s}", n) for i in range(L) for s, n in (
            ("hT", 1), ("qkv", H), ("kmean", 1), ("kv", 1), ("qT", 1), ("o", 1))])
        att_act = pair("att_act", *[(f"{i}{s}", n) for i in range(L) for s, n in (("hF", 1), ("v", H), ("qF", 1))])
        att_vec = pair("att_vec", *[s for i in range(L) for s in (
            (f"{i}swap", 2), (f"{i}den", 1), (f"{i}rot", 1), (f"{i}head", 1), (f"{i}eps6", 1),
            (f"{i}z", 1), (f"{i}kvm", 1), (f"{i}oz", 1), (f"{i}sum", 1), *norm_steps(str(i), H, True))])
        att_pool = pair("att_pool", *[(f"{i}{s}", n) for i in range(L) for s, n in (("plus", 1), ("cos", 1), ("rstd", 1))])
        ffn_pe = pair("ffn_pe", ("hT", 1), ("up", FC), ("down", 1), ("fT", 1))
        ffn_act = pair("ffn_act", ("hF", 1), ("gelu", FC), ("fF", 1))
        ffn_vec = pair("ffn_vec", ("sum", 1), *norm_steps("i", H, True), ("sum2", 1), *norm_steps("o", H))
        ffn_pool = pair("ffn_pool", ("irstd", 1), ("orstd", 1))

        moe_wB = Steps(sem("moe_wB"), ("wB", E))
        moe_gate = Steps(sem("moe_gate"), ("gate", STEPS))
        moe_up = Steps(sem("moe_up"), ("up", STEPS))
        moe_y = Steps(sem("moe_y"), ("y", STEPS), ("yT", 1))
        moe_act = Steps(sem("moe_act"), ("wB", E // 2), ("gelu", STEPS), ("yF", 1))
        moe_pool = Steps(sem("moe_pool"), ("gw", STEPS), ("rstd", 1))
        moe_vec = Steps(sem("moe_vec"), ("wB", E // 2), ("p", STEPS), ("sum", 1), *norm_steps("", T))
        ter_pe = Steps(sem("ter_pe"), ("x3T", 1), ("gu", FC), ("h1", FC), ("h2", FC), ("w3", 1), ("yT", 1))
        ter_act = Steps(sem("ter_act"), ("x3F", 1), ("silu", FC), ("h1", FC), ("h2", FC), ("yF", 1))
        ter_vec = Steps(sem("ter_vec"), ("h", FC), ("sum", 1), *norm_steps("", T))
        ter_pool = Steps(sem("ter_pool"), ("rstd", 1))

        def begin(eng, *counts):
            for c in counts:
                eng.sem_inc(c.sem, 1)

        begun = sem("begun")
        passed = sem("passed")
        early = sem("early")
        later = sem("later")
        e_got = [sem(f"e_got{e}") for e in range(E)]
        staged = [sem(f"staged{i}") for i in range(3)]
        set_pe, set_act = sem("set_pe"), sem("set_act")

        block = ctx.enter_context(nc.Block())

        def row(v):
            return v.rearrange("(a n) -> a n", a=1).partition_broadcast(P)

        def rows_of(name):
            at, n = ROWS[name]
            return rows[at:at + n, :]

        early_loads = [
            (ident[:], a["c_ident"]), (wqkv0_raw[:, 0, :], a["L0_attn_W_q"]), (wqkv0_raw[:, 1, :], a["L0_attn_W_k"]),
            (wqkv0_raw[:, 2, :], a["L0_attn_W_v"]), (mean_of[:], a["c_mean_of"]), (wr1[:], a["L0_ffn_Wr1"]),
            (wr2[:], a["L0_ffn_Wr2"]), (br1[:], row(a["L0_ffn_br1"])), (r_g[:], row(a["L0_ffn_ln_scale"])),
            (r_b[:], row(a["L0_ffn_ln_bias"])), (br2[:], row(a["L0_ffn_br2"])), (earlier[:], a["c_earlier"]),
            (e_b2[:], a["L0_ffn_b2"]),
            (rows_of("e_b1"), a["L0_ffn_b1"].rearrange("e (c p) -> (e c) p", p=P)),
        ] + [(rows_of(n), a[v].rearrange("(c p) -> c p", p=P)) for n, v in (
            ("f_b1", "L1_attn_b1"), ("f_b2", "L1_attn_b2"), ("c2_b", "L1_attn_conv2_b"), ("w1_s", "L1_ffn_w1_s"),
            ("w2_s", "L1_ffn_w2_s"), ("h1_s", "L1_ffn_h1_s"), ("h2_s", "L1_ffn_h2_s"), ("w3_s", "L1_ffn_w3_s"))
        ] + [(a_b[at:at + L, i * D:(i + 1) * D], a[v]) for at in (0, 32) for i, v in enumerate(
            ("L1_attn_bq", "L1_attn_bk", "L1_attn_bv"))]
        later_loads = [
            (c1_w[:], a["L1_attn_conv1_w"].rearrange("(c j) o k -> c j (o k)", j=4)),
            (c1_b[:], a["L1_attn_conv1_b"].rearrange("(c j) -> c j", j=4)), (c2_w[:], a["L1_attn_conv2_w"]),
            (cos[:], a["c_cos"]), (sin[:], a["c_sin"]), (headmask[:], a["c_headmask"]),
            (gains[:, 0, :], row(a["L1_attn_ln0_g"])), (shifts[:, 0, :], row(a["L1_attn_ln0_b"])),
            (gains[:, L + 1, :], row(a["L1_attn_ln2_g"])), (shifts[:, L + 1, :], row(a["L1_attn_ln2_b"])),
            (gains[:, 1:L + 1, :], a["L1_attn_lnA_g"].rearrange("(a l) d -> a l d", a=1).partition_broadcast(P)),
            (shifts[:, 1:L + 1, :], a["L1_attn_lnA_b"].rearrange("(a l) d -> a l d", a=1).partition_broadcast(P)),
            (a_w[:, :, 0:D], a["L1_attn_Wq"].rearrange("l i o -> i l o")),
            (a_w[:, :, D:2 * D], a["L1_attn_Wk"].rearrange("l i o -> i l o")),
            (a_w[:, :, 2 * D:3 * D], a["L1_attn_Wv"].rearrange("l i o -> i l o")),
            (f_w1[:], a["L1_attn_W1"]), (f_w2[:], a["L1_attn_W2"].rearrange("(c p) d -> p c d", p=P)),
        ]

        def chunked(at, c):
            return raw[:, at:at + F * (c if c == FC else 1)].rearrange("p (c i) -> p c i", c=c)

        loads = [[(raw[:, w * F:(w + 1) * F].rearrange("p (c i) -> p c i", c=FC if w < 2 else 1), f"L1_ffn_w{w + 1}_w")
                  for w in range(3)],
                 [(raw[:, 3 * F:3 * F + FC * F].rearrange("p (c i) -> p c i", c=FC), "L1_ffn_h1_w")],
                 [(raw[:, 0:FC * F].rearrange("p (c i) -> p c i", c=FC), "L1_ffn_h2_w")]]
        groups = []
        for w in range(2):
            groups.append((0, [w * F + c * P for c in range(FC)], t_w12[:, w, :]))
        groups.append((0, [2 * F + k * P for k in range(FC)], t_w3[:].rearrange("p k d -> p (k d)")))
        for w, at in ((0, 3 * F), (1, 0)):
            for k in range(FC):
                groups.append((w + 1, [at + c * F + k * P for c in range(FC)], t_h[:, w, k, :]))
        ROUND0, ROUND1 = 3, 3 + FC
        TERNARY_SLOTS = len(groups) + 1

        def wait_apart(eng, s, value):
            eng.wait_ge(s, value)
            eng.sem_inc(passed, 1)

        def norm_stats(dve, steps, blk, name, src, thread, eps):
            st, mv, ve, _ = stat[thread]
            s, n = steps.sem, src.shape[1]
            for t in range(n):
                nc.vector.bn_stats(st[:, t, :], src[:, t, :]).then_inc(s, 1)
            wait_apart(dve, s, steps.after(blk, name + "stats", n - 1))
            for t in range(n):
                nc.vector.bn_aggr(mv[:, t, :], st[:, t, :]).then_inc(s, 1)
            dve.wait_ge(s, steps.after(blk, name + "aggr", n - 1))
            nc.vector.tensor_scalar(ve[:, 0:n], mv[:, 0:n, 1], eps, None, ALU.add).then_inc(s, 1)

        def norm_power(pool, steps, blk, name, vec, thread, n):
            _, _, ve, rs = stat[thread]
            pool.wait_ge(vec.sem, vec.after(blk, name + "eps"))
            nc.gpsimd.tensor_tensor(rs[:, 0:n], ve[:, 0:n], minus_half[:, 0:n], ALU.pow).then_inc(steps.sem, 1)

        def norm_apply(dve, steps, blk, name, src, dst, thread, power, affine=None):
            _, mv, _, rs = stat[thread]
            s, n = steps.sem, src.shape[1]
            dve.wait_ge(power.sem, power.after(blk, name + "rstd"))
            for t in range(n):
                nc.vector.tensor_scalar(dst[:, t, :], src[:, t, :], mv[:, t, 0:1], rs[:, t:t + 1],
                                        ALU.subtract, ALU.mult).then_inc(s, 1)
            if affine is not None:
                gain, shift = (v.unsqueeze(1).to_broadcast(list(dst.shape)) for v in affine)
                dve.wait_ge(s, steps.after(blk, name + "apply", n - 1))
                nc.vector.tensor_tensor(dst, dst, gain, ALU.mult).then_inc(s, 1)
                dve.wait_ge(s, steps.after(blk, name + "gain"))
                nc.vector.tensor_tensor(dst, dst, shift, ALU.add).then_inc(s, 1)

        def turn(src, bank):
            for t in range(src.shape[1]):
                mm = nc.tensor.transpose(bank[0:src.shape[2], t * P:(t + 1) * P], src[:, t, :], ident[:])
            return mm

        def turn_back(srcF, bank):
            for t in range(srcF.shape[1] // P):
                mm = nc.tensor.transpose(bank[:, t * P:(t + 1) * P], srcF[:, t * P:(t + 1) * P], ident[:])
            return mm

        def tok(bank, tiles):
            return bank[:, 0:tiles * D].rearrange("p (t d) -> p t d", t=tiles)

        class Pe:
            @staticmethod
            def setup(pe):
                pe.wait_ge(early, 16 * len(early_loads))
                for i in range(3):
                    mm = nc.tensor.transpose(gate[0][:, i * P:(i + 1) * P], wqkv0_raw[:, i, :], ident[:])
                mm.then_inc(set_pe, 1)
                nc.tensor.transpose(gate[1][:, 0:NROWS], rows[0:NROWS, :], ident[0:NROWS, 0:NROWS]).then_inc(set_pe, 1)

            @staticmethod
            def ternary(pe):
                banks = [up, ab[0][0]]
                for n, (r, starts, _) in enumerate(groups):
                    pe.wait_ge(staged[r], 16 * len(loads[r]))
                    if n >= 2:
                        pe.wait_ge(set_act, 2 + n - 1)
                    for c, at in enumerate(starts):
                        mm = nc.tensor.transpose(ab[n % 2][1][:, c * P:(c + 1) * P], raw[:, at:at + P], ident[:])
                    mm.then_inc(set_pe, 1)
                    yield
                yield

            @staticmethod
            def mix(pe, blk, y):
                m, act, vec = mix_pe[y.q], mix_act[y.q], mix_vec[y.q]
                pe.wait_ge(x_got.sem, x_got.after(blk, "x"))
                pe.wait_ge(ffn_vec[y.q].sem, ffn_vec[y.q].before(blk - 1 if not isinstance(blk, int) else max(blk - 1, 0)))
                turn(x_t[:, y.ts, :], y.a).then_inc(m.sem, 1)
                yield
                yield
                pe.wait_ge(set_act, 1)
                pe.wait_ge(act.sem, act.after(blk, "xF"))
                for t in range(H):
                    nc.tensor.matmul((y.b, y.a)[t][:, 0:3 * D], y.hF[:, t * P:(t + 1) * P], wqkv0[:],
                                     start=True, stop=True).then_inc(m.sem, 1)
                yield
                for _ in range(4):
                    yield
                pe.wait_ge(vec.sem, vec.after(blk, "kv", H - 1))
                for t in range(H):
                    mm = nc.tensor.matmul(y.b[:, 0:D], mean_of[:], y.kvt[:, t, :], start=(t == 0), stop=(t == H - 1))
                mm.then_inc(m.sem, 1)
                yield
                for _ in range(3):
                    yield

            @staticmethod
            def route(pe, blk, y):
                m, act, vec = route_pe[y.q], route_act[y.q], route_vec[y.q]
                pe.wait_ge(mix_vec[y.q].sem, mix_vec[y.q].after(blk, "apply", H - 1))
                turn(x1_t[:, y.ts, :], y.a).then_inc(m.sem, 1)
                yield
                yield
                pe.wait_ge(act.sem, act.after(blk, "x1F"))
                for t in range(H):
                    mm = nc.tensor.matmul(y.b[:, t * R:(t + 1) * R], x1F[:, (y.ts.start + t) * P:(y.ts.start + t + 1) * P],
                                          wr1[:], start=True, stop=True)
                mm.then_inc(m.sem, 1)
                yield
                for _ in range(4):
                    yield
                wait_apart(pe, act.sem, act.after(blk, "gelu"))
                turn(y.hg, y.a).then_inc(m.sem, 1)
                yield
                yield
                pe.wait_ge(act.sem, act.after(blk, "hT"))
                for t in range(H):
                    mm = nc.tensor.matmul(y.b[:, t * E:(t + 1) * E], y.hT[0:R, t * P:(t + 1) * P], wr2[:], start=True, stop=True)
                mm.then_inc(m.sem, 1)
                yield
                for _ in range(3):
                    yield
                pe.wait_ge(vec.sem, vec.after(blk, "weight"))
                turn(y.wts[:], y.a).then_inc(m.sem, 1)
                yield
                yield

            @staticmethod
            def conv(pe, blk, y):
                m, vec = conv_pe[y.q], conv_vec[y.q]
                pe.wait_ge(moe_vec.sem, moe_vec.after(blk, "apply", T - 1))
                turn(x2_t[:, y.ts, :], y.a).then_inc(m.sem, 1)
                yield
                for _ in range(12):
                    yield
                pe.wait_ge(vec.sem, vec.after(blk, "c2"))
                turn_back(y.c2[:, 0], y.a).then_inc(m.sem, 1)
                yield
                for _ in range(3):
                    yield

            @staticmethod
            def att(pe, blk, y, i):
                m, act, vec, pool = att_pe[y.q], att_act[y.q], att_vec[y.q], att_pool[y.q]
                if i == 0:
                    pe.wait_ge(conv_vec[y.q].sem, conv_vec[y.q].after(blk, "shift"))
                else:
                    pe.wait_ge(vec.sem, vec.after(blk, f"{i - 1}shift"))
                turn(y.h_t, y.a).then_inc(m.sem, 1)
                yield
                yield
                pe.wait_ge(later, 16 * len(later_loads))
                pe.wait_ge(begun, SETUP_STEPS)
                pe.wait_ge(act.sem, act.after(blk, f"{i}hF"))
                for t in range(H):
                    bank = (y.b, y.a)[t]
                    nc.tensor.matmul(bank[:, 0:3 * D], y.hF[:, t * P:(t + 1) * P], a_w[:, i, :], start=True, stop=False)
                    nc.tensor.matmul(bank[:, 0:3 * D], a_sel[:, i:i + 1].to_broadcast([32 + L, P]), a_bs[:],
                                     start=False, stop=True).then_inc(m.sem, 1)
                yield
                yield
                yield
                pe.wait_ge(pool.sem, pool.after(blk, f"{i}plus"))
                for t in range(H):
                    mm = nc.tensor.matmul(y.b[:, 0:D], mean_of[:], y.qk[:, t, 1, :], start=(t == 0), stop=(t == H - 1))
                mm.then_inc(m.sem, 1)
                yield
                yield
                pe.wait_ge(vec.sem, vec.after(blk, f"{i}rot"))
                for t in range(H):
                    mm = nc.tensor.matmul(y.a[:, 0:D], y.rot[:, t, 1, :], y.vt[:, t, :], start=(t == 0), stop=(t == H - 1))
                mm.then_inc(m.sem, 1)
                turn(y.rot[:, :, 0, :], y.b).then_inc(m.sem, 1)
                yield
                yield
                pe.wait_ge(act.sem, act.after(blk, f"{i}qF"))
                pe.wait_ge(vec.sem, vec.after(blk, f"{i}kvm"))
                for t in range(H):
                    mm = nc.tensor.matmul(y.a[:, t * P:(t + 1) * P], y.qF[:, t * P:(t + 1) * P], y.kvm[:], start=True, stop=True)
                mm.then_inc(m.sem, 1)
                yield
                for _ in range(3):
                    yield

            @staticmethod
            def ffn(pe, blk, y):
                m, act = ffn_pe[y.q], ffn_act[y.q]
                pe.wait_ge(att_vec[y.q].sem, att_vec[y.q].before(blk + 1))
                turn(y.h_t, y.a).then_inc(m.sem, 1)
                yield
                yield
                for j in range(FC):
                    pe.wait_ge(act.sem, act.after(blk, "hF") if j < 2 else act.after(blk, "gelu", j - 2))
                    nc.tensor.matmul((y.b, y.a)[j % 2][:, 0:N], f_w1[:, j * P:(j + 1) * P], y.hF, start=True, stop=True).then_inc(m.sem, 1)
                    if j % 2:
                        yield
                        yield
                for j in range(FC):
                    pe.wait_ge(act.sem, act.after(blk, "gelu", FC - 1))
                    mm = nc.tensor.matmul(y.b[:, 0:N], f_w2[:, j, :], y.ffh[:, j, :], start=(j == 0), stop=(j == FC - 1))
                mm.then_inc(m.sem, 1)
                yield
                yield
                pe.wait_ge(act.sem, act.after(blk, "fF"))
                turn_back(y.hF, y.a).then_inc(m.sem, 1)
                yield
                for _ in range(5):
                    yield

            @staticmethod
            def moe(pe, blk):
                for q in range(SEQS):
                    pe.wait_ge(route_act[q].sem, route_act[q].after(blk, "wT"))
                pe.wait_ge(set_act, 2)
                for e in range(E):
                    if e >= 2:
                        emptied = moe_act if e % 2 == 0 else moe_vec
                        pe.wait_ge(emptied.sem, emptied.after(blk, "wB", e // 2 - 1))
                    else:
                        pe.wait_ge(ter_act.sem, ter_act.before(blk - 1 if not isinstance(blk, int) else max(blk - 1, 0)))
                    nc.tensor.matmul(gate[e % 2][:], ident[0:E, e:e + 1].to_broadcast([E, P]), wT[:],
                                     start=True, stop=True).then_inc(moe_wB.sem, 1)
                    if e % 2:
                        yield
                yield
                for s in range(STEPS + 2):
                    if s < STEPS:
                        e, j = divmod(s, FC)
                        if j == 0:
                            if isinstance(blk, int) and blk == 0:
                                pe.wait_ge(e_got[e], 32)
                        if s >= 2:
                            pe.wait_ge(moe_act.sem, moe_act.after(blk, "gelu", s - 2))
                        else:
                            last = (moe_act, moe_vec)[s]
                            pe.wait_ge(last.sem, last.after(blk, "wB", E // 2 - 1))
                        nc.tensor.matmul(gate[s % 2][:], e_w1[:, e, F + j * P:F + (j + 1) * P], x1F[:],
                                         start=True, stop=True).then_inc(moe_gate.sem, 1)
                    if s == 0:
                        nc.tensor.matmul(ybank[:], e_b2[:], wT[:], start=True, stop=False)
                    if s >= 2:
                        r = s - 2
                        pe.wait_ge(moe_vec.sem, moe_vec.after(blk, "p", r))
                        nc.tensor.matmul(ybank[:], e_w2[:, r // FC, r % FC, :], p[:, r % 2, :],
                                         start=False, stop=(r == STEPS - 1)).then_inc(moe_y.sem, 1)
                    if 1 <= s <= STEPS:
                        e, j = divmod(s - 1, FC)
                        if s >= 2:
                            pe.wait_ge(moe_vec.sem, moe_vec.after(blk, "p", s - 2))
                        nc.tensor.matmul(up[:], e_w1[:, e, j * P:(j + 1) * P], x1F[:],
                                         start=True, stop=True).then_inc(moe_up.sem, 1)
                    yield
                    yield

            @staticmethod
            def moe_out(pe, blk):
                yield
                pe.wait_ge(moe_act.sem, moe_act.after(blk, "yF"))
                turn_back(yF, gate[0]).then_inc(moe_y.sem, 1)
                yield
                for _ in range(3):
                    yield

            @staticmethod
            def ter(pe, blk, done):
                m, act, vec = ter_pe, ter_act, ter_vec
                for q in range(SEQS):
                    pe.wait_ge(ffn_vec[q].sem, ffn_vec[q].before(blk + 1))
                turn(x3_t, gate[1]).then_inc(m.sem, 1)
                yield
                yield
                pe.wait_ge(moe_vec.sem, moe_vec.after(done, "sum"))
                pe.wait_ge(act.sem, act.after(blk, "x3F"))
                for c in range(FC):
                    if c >= 2:
                        pe.wait_ge(act.sem, act.after(blk, "silu", c - 2))
                        pe.wait_ge(vec.sem, vec.after(blk, "h", c - 2))
                    nc.tensor.matmul(gate[c % 2][:], t_w12[:, 0, c * P:(c + 1) * P], x3F, start=True, stop=True)
                    nc.tensor.matmul((up, ybank)[c % 2][:], t_w12[:, 1, c * P:(c + 1) * P], x3F,
                                     start=True, stop=True).then_inc(m.sem, 1)
                    yield
                yield
                for w, (src, name) in enumerate(((tA, "h1"), (tB, "h2"))):
                    for c in range(FC):
                        before = act.after(blk, ("silu", "h1")[w], FC - 2 + c) if c < 2 else act.after(blk, name, c - 2)
                        pe.wait_ge(act.sem, before)
                        for k in range(FC):
                            if c == 0 and w == 0:
                                pe.wait_ge(vec.sem, vec.after(blk, "h", k))
                            elif c == 0:
                                pe.wait_ge(act.sem, act.after(blk, "h1", k))
                            mm = nc.tensor.matmul(gate[c % 2][:], t_h[:, w, k, c * P:(c + 1) * P], src[:, k, :],
                                                  start=(k == 0), stop=(k == FC - 1))
                        mm.then_inc(m.sem, 1)
                        yield
                for k in range(FC):
                    pe.wait_ge(act.sem, act.after(blk, "h2", k))
                    mm = nc.tensor.matmul(ybank[:], t_w3[:, k, :], tA[:, k, :], start=(k == 0), stop=(k == FC - 1))
                mm.then_inc(m.sem, 1)
                yield
                yield
                pe.wait_ge(act.sem, act.after(blk, "yF"))
                turn_back(tyF, up).then_inc(m.sem, 1)
                yield
                for _ in range(6):
                    yield

        class Act:
            @staticmethod
            def setup(act):
                act.wait_ge(set_pe, 1)
                nc.scalar.copy(wqkv0[:], gate[0][:, 0:3 * D]).then_inc(set_act, 1)
                act.wait_ge(set_pe, 2)
                nc.scalar.copy(cols[:], gate[1][:, 0:NROWS]).then_inc(set_act, 1)

            @staticmethod
            def ternary(act):
                yield
                for n, (_, _, dst) in enumerate(groups):
                    act.wait_ge(set_pe, 2 + n + 1)
                    nc.scalar.copy(dst, ab[n % 2][1][:]).then_inc(set_act, 1)
                    yield

            @staticmethod
            def mix(act, blk, y):
                m, pe = mix_act[y.q], mix_pe[y.q]
                yield
                act.wait_ge(pe.sem, pe.after(blk, "xT"))
                nc.scalar.copy(y.hF, y.a[:, 0:N]).then_inc(m.sem, 1)
                yield
                yield
                for t in range(H):
                    act.wait_ge(pe.sem, pe.after(blk, "qkv", t))
                    nc.scalar.copy(y.qkv[:, t].rearrange("p c d -> p (c d)"), (y.b, y.a)[t][:, 0:3 * D]).then_inc(m.sem, 1)
                yield
                for _ in range(7):
                    yield

            @staticmethod
            def route(act, blk, y):
                m, pe, vec = route_act[y.q], route_pe[y.q], route_vec[y.q]
                yield
                act.wait_ge(pe.sem, pe.after(blk, "x1T"))
                nc.scalar.copy(x1F[:, y.q * N:(y.q + 1) * N], y.a[:, 0:N]).then_inc(m.sem, 1)
                yield
                for _ in range(4):
                    yield
                act.wait_ge(vec.sem, vec.after(blk, "shift"))
                nc.scalar.activation(y.hg, y.hr, ACT.Gelu_apprx_tanh).then_inc(m.sem, 1)
                yield
                yield
                act.wait_ge(pe.sem, pe.after(blk, "hT"))
                nc.scalar.copy(y.hT[0:R, :], y.a[0:R, 0:N]).then_inc(m.sem, 1)
                yield
                yield
                yield
                act.wait_ge(vec.sem, vec.after(blk, "less_max"))
                nc.scalar.activation(y.lex[:], y.lex[:], ACT.Exp).then_inc(m.sem, 1)
                yield
                yield
                yield
                act.wait_ge(pe.sem, pe.after(blk, "wT"))
                nc.scalar.copy(wT[:, y.q * N:(y.q + 1) * N], y.a[0:E, 0:N]).then_inc(m.sem, 1)
                yield

            @staticmethod
            def conv(act, blk, y):
                m, pe, vec = conv_act[y.q], conv_pe[y.q], conv_vec[y.q]
                yield
                act.wait_ge(pe.sem, pe.after(blk, "x2T"))
                nc.scalar.copy(x2F[:, y.q, PAD:PAD + N], y.a[:, 0:N]).then_inc(m.sem, 1)
                yield
                for _ in range(5):
                    yield
                act.wait_ge(conv_pool[y.q].sem, conv_pool[y.q].after(blk, "pad", 1))
                for j in range(4):
                    act.wait_ge(vec.sem, vec.after(blk, "tap1", 4 * (TAPS - 1) + j))
                    nc.scalar.activation(y.c1F[:, j, PAD:PAD + N], y.c1[:, j], ACT.Gelu, bias=c1_b[:, j:j + 1]).then_inc(m.sem, 1)
                yield
                for _ in range(9):
                    yield

            @staticmethod
            def att(act, blk, y, i):
                m, pe = att_act[y.q], att_pe[y.q]
                yield
                act.wait_ge(pe.sem, pe.after(blk, f"{i}hT"))
                nc.scalar.copy(y.hF, y.a[:, 0:N]).then_inc(m.sem, 1)
                yield
                yield
                for t in range(H):
                    bank = (y.b, y.a)[t]
                    act.wait_ge(pe.sem, pe.after(blk, f"{i}qkv", t))
                    nc.scalar.activation(y.qk[:, t].rearrange("p c d -> p (c d)"), bank[:, 0:2 * D], ACT.Gelu)
                    nc.scalar.copy(y.vt[:, t, :], bank[:, 2 * D:3 * D]).then_inc(m.sem, 1)
                yield
                for _ in range(4):
                    yield
                act.wait_ge(pe.sem, pe.after(blk, f"{i}qT"))
                nc.scalar.copy(y.qF, y.b[:, 0:N]).then_inc(m.sem, 1)
                yield
                for _ in range(4):
                    yield

            @staticmethod
            def ffn(act, blk, y):
                m, pe = ffn_act[y.q], ffn_pe[y.q]
                yield
                act.wait_ge(pe.sem, pe.after(blk, "hT"))
                nc.scalar.copy(y.hF, y.a[:, 0:N]).then_inc(m.sem, 1)
                yield
                for j in range(FC):
                    if j % 2 == 0:
                        yield
                    act.wait_ge(pe.sem, pe.after(blk, "up", j))
                    nc.scalar.activation(y.ffh[:, j, :], (y.b, y.a)[j % 2][:, 0:N], ACT.Gelu, bias=col("f_b1", j)).then_inc(m.sem, 1)
                    if j % 2:
                        yield
                yield
                act.wait_ge(pe.sem, pe.after(blk, "down"))
                nc.scalar.activation(y.hF, y.b[:, 0:N], ACT.Identity, bias=col("f_b2")).then_inc(m.sem, 1)
                yield
                for _ in range(6):
                    yield

            @staticmethod
            def moe(act, blk):
                yield
                for k in range(E // 2):
                    act.wait_ge(moe_wB.sem, moe_wB.after(blk, "wB", 2 * k))
                    nc.scalar.copy(wB[:, 2 * k, :], gate[0][:]).then_inc(moe_act.sem, 1)
                    yield
                for s in range(STEPS + 2):
                    yield
                    if s < STEPS:
                        e, j = divmod(s, FC)
                        act.wait_ge(moe_gate.sem, moe_gate.after(blk, "gate", s))
                        if s >= 2:
                            act.wait_ge(moe_pool.sem, moe_pool.after(blk, "gw", s - 2))
                        nc.scalar.activation(g[:, s % 2, :], gate[s % 2][:], ACT.Gelu_apprx_tanh,
                                             bias=col("e_b1", e * 2 * FC + FC + j)).then_inc(moe_act.sem, 1)
                    yield

            @staticmethod
            def moe_out(act, blk):
                act.wait_ge(moe_y.sem, moe_y.after(blk, "y", STEPS - 1))
                nc.scalar.copy(yF, ybank[:]).then_inc(moe_act.sem, 1)
                yield
                for _ in range(4):
                    yield

            @staticmethod
            def ter(act, blk, done):
                m, pe, vec = ter_act, ter_pe, ter_vec
                yield
                act.wait_ge(pe.sem, pe.after(blk, "x3T"))
                nc.scalar.copy(x3F, gate[1][:]).then_inc(m.sem, 1)
                yield
                yield
                for c in range(FC):
                    act.wait_ge(pe.sem, pe.after(blk, "gu", c))
                    if c >= 2:
                        act.wait_ge(vec.sem, vec.after(blk, "h", c - 2))
                    nc.scalar.activation(u[:, c % 2, :], gate[c % 2][:], ACT.Silu, scale=col("w1_s", c)).then_inc(m.sem, 1)
                    yield
                yield
                for name, scale, dst in (("h1", "h1_s", tB), ("h2", "h2_s", tA)):
                    for c in range(FC):
                        act.wait_ge(pe.sem, pe.after(blk, name, c))
                        nc.scalar.activation(dst[:, c, :], gate[c % 2][:], ACT.Gelu, scale=col(scale, c)).then_inc(m.sem, 1)
                        yield
                act.wait_ge(pe.sem, pe.after(blk, "w3"))
                nc.scalar.activation(tyF, ybank[:], ACT.Identity, scale=col("w3_s")).then_inc(m.sem, 1)
                yield
                for _ in range(7):
                    yield

        SETUP_STEPS = 9

        class Vec:
            @staticmethod
            def setup(dve):
                nc.vector.memset(minus_half[:], -0.5).then_inc(begun, 1)
                nc.vector.memset(x2F[:], 0.0).then_inc(begun, 1)
                nc.vector.memset(a_bs[:].bitcast(F32), 0.0).then_inc(begun, 1)
                nc.vector.memset(a_sel[:].bitcast(F32), 0.0).then_inc(begun, 1)
                dve.wait_ge(early, 16 * len(early_loads))
                dve.wait_ge(begun, 4)
                for at in (0, 32):
                    nc.vector.tensor_copy(a_bs[at:at + L, :], a_b[at:at + L, :]).then_inc(begun, 1)
                    nc.vector.tensor_copy(a_sel[at:at + L, :], ident[at:at + L, at:at + L]).then_inc(begun, 1)
                dve.wait_ge(begun, 8)
                nc.vector.tensor_tensor(a_bs[32:32 + L, :], a_b[32:32 + L, :], a_bs[32:32 + L, :].bitcast(F32),
                                        ALU.subtract).then_inc(begun, 1)

            @staticmethod
            def mix(dve, blk, y):
                m = mix_vec[y.q]
                s = m.sem
                for _ in range(4):
                    yield
                qk0 = y.qkv[:, :, 0:2, :]
                dve.wait_ge(mix_act[y.q].sem, mix_act[y.q].after(blk, "qkv", H - 1))
                nc.vector.tensor_tensor(y.sq, qk0, qk0, ALU.mult).then_inc(s, 1)
                dve.wait_ge(s, m.after(blk, "square"))
                nc.vector.tensor_reduce(y.ssq[:], y.sq, AX.X, ALU.add).then_inc(s, 1)
                dve.wait_ge(s, m.after(blk, "ssq"))
                nc.vector.tensor_scalar(y.ssq[:], y.ssq[:], 1e-24, None, ALU.max).then_inc(s, 1)
                yield
                yield
                dve.wait_ge(mix_pool[y.q].sem, mix_pool[y.q].after(blk, "len"))
                for t in range(H):
                    nc.vector.scalar_tensor_tensor(out=y.kvt[:, t, :], in0=y.qkv[:, t, 1, :], scalar=y.rn[:, t, 1:2],
                                                   in1=y.qkv[:, t, 2, :], op0=ALU.mult, op1=ALU.mult).then_inc(s, 1)
                yield
                yield
                dve.wait_ge(mix_pe[y.q].sem, mix_pe[y.q].after(blk, "mean"))
                for t in range(H):
                    nc.vector.scalar_tensor_tensor(out=sum_t[:, y.q, t, :], in0=y.qkv[:, t, 0, :], scalar=y.rn[:, t, 0:1],
                                                   in1=y.b[:, 0:D], op0=ALU.mult, op1=ALU.mult).then_inc(s, 1)
                dve.wait_ge(s, m.after(blk, "q", H - 1))
                nc.vector.tensor_tensor(sum_t[:, y.q], sum_t[:, y.q], x_t[:, y.ts, :], ALU.add).then_inc(s, 1)
                dve.wait_ge(s, m.after(blk, "sum"))
                norm_stats(dve, m, blk, "", sum_t[:, y.q], y.q, 1e-5)
                yield
                yield
                if not (isinstance(blk, int) and blk == 0):
                    dve.wait_ge(moe_vec.sem, moe_vec.after(blk - 1, "sum"))
                norm_apply(dve, m, blk, "", sum_t[:, y.q], x1_t[:, y.ts, :], y.q, mix_pool[y.q])
                yield

            @staticmethod
            def route(dve, blk, y):
                m, pe = route_vec[y.q], route_pe[y.q]
                s = m.sem

                def after(name):
                    dve.wait_ge(s, m.after(blk, name))

                for _ in range(3):
                    yield
                dve.wait_ge(pe.sem, pe.after(blk, "h"))
                nc.vector.tensor_tensor(y.hr, y.b[:, 0:H * R].rearrange("p (t d) -> p t d", t=H),
                                        br1[:].unsqueeze(1).to_broadcast([P, H, R]), ALU.add).then_inc(s, 1)
                after("h")
                norm_stats(dve, m, blk, "", y.hr, y.q, 1e-6)
                yield
                yield
                norm_apply(dve, m, blk, "", y.hr, y.hr, y.q, route_pool[y.q], (r_g[:], r_b[:]))
                yield
                for _ in range(4):
                    yield
                dve.wait_ge(pe.sem, pe.after(blk, "logit"))
                nc.vector.tensor_tensor(y.lg[:], y.b[:, 0:H * E].rearrange("p (t e) -> p t e", t=H),
                                        br2[:].unsqueeze(1).to_broadcast([P, H, E]), ALU.add).then_inc(s, 1)
                full, small = [P, H, E, E], [P, H, E]
                other, own = y.lg[:].unsqueeze(2).to_broadcast(full), y.lg[:].unsqueeze(3).to_broadcast(full)
                after("logit")
                nc.vector.tensor_tensor(y.cmp1, other, own, ALU.is_gt).then_inc(s, 1)
                nc.vector.tensor_tensor(y.cmp2, other, own, ALU.is_equal).then_inc(s, 1)
                after("tie")
                nc.vector.tensor_tensor(y.cmp2, y.cmp2, earlier[:].unsqueeze(1).to_broadcast(full), ALU.mult).then_inc(s, 1)
                after("tie_earlier")
                nc.vector.tensor_tensor(y.cmp1, y.cmp1, y.cmp2, ALU.add).then_inc(s, 1)
                after("beats")
                nc.vector.tensor_reduce(y.rank[:], y.cmp1, AX.X, ALU.add).then_inc(s, 1)
                after("rank")
                nc.vector.tensor_scalar(y.rank[:], y.rank[:], 1.5, None, ALU.is_lt).then_inc(s, 1)
                nc.vector.tensor_reduce(y.lmax[:], y.lg[:], AX.X, ALU.max).then_inc(s, 1)
                after("max")
                nc.vector.tensor_tensor(y.lex[:], y.lg[:], y.lmax[:].unsqueeze(2).to_broadcast(small), ALU.subtract).then_inc(s, 1)
                yield
                yield
                dve.wait_ge(route_act[y.q].sem, route_act[y.q].after(blk, "exp"))
                nc.vector.tensor_tensor(y.lex[:], y.lex[:], y.rank[:], ALU.mult).then_inc(s, 1)
                after("keep")
                nc.vector.tensor_reduce(y.lmax[:], y.lex[:], AX.X, ALU.add).then_inc(s, 1)
                after("total")
                nc.vector.reciprocal(y.lmax[:], y.lmax[:]).then_inc(s, 1)
                after("recip")
                nc.vector.tensor_tensor(y.wts[:], y.lex[:], y.lmax[:].unsqueeze(2).to_broadcast(small), ALU.mult).then_inc(s, 1)
                yield
                yield

            @staticmethod
            def conv(dve, blk, y):
                m = conv_vec[y.q]
                s = m.sem
                yield
                yield
                dve.wait_ge(conv_act[y.q].sem, conv_act[y.q].after(blk, "x2F"))
                dve.wait_ge(later, 16 * len(later_loads))
                for k in range(TAPS):
                    for j in range(4):
                        src, w = x2F[:, y.q, k:k + N], c1_w[:, j, k:k + 1]
                        if k == 0:
                            nc.vector.tensor_scalar(y.c1[:, j], src, w, None, ALU.mult).then_inc(s, 1)
                        else:
                            dve.wait_ge(s, m.after(blk, "tap1", 4 * (k - 1) + j))
                            nc.vector.scalar_tensor_tensor(out=y.c1[:, j], in0=src, scalar=w, in1=y.c1[:, j],
                                                           op0=ALU.mult, op1=ALU.add).then_inc(s, 1)
                    yield
                yield
                for j in range(4):
                    dve.wait_ge(conv_act[y.q].sem, conv_act[y.q].after(blk, "gelu", j))
                    for k in range(TAPS):
                        n = j * TAPS + k
                        src, w = y.c1F[:, j, k:k + N], c2_w[:, j, k:k + 1]
                        if n == 0:
                            nc.vector.tensor_scalar(y.c2[:, 0], src, w, col("c2_b"), ALU.mult, ALU.add).then_inc(s, 1)
                        elif n == 1:
                            nc.vector.tensor_scalar(y.c2[:, 1], src, w, None, ALU.mult).then_inc(s, 1)
                        else:
                            dve.wait_ge(s, m.after(blk, "tap2", n - 2))
                            nc.vector.scalar_tensor_tensor(out=y.c2[:, n % 2], in0=src, scalar=w, in1=y.c2[:, n % 2],
                                                           op0=ALU.mult, op1=ALU.add).then_inc(s, 1)
                    yield
                dve.wait_ge(s, m.after(blk, "tap2", 4 * TAPS - 1))
                nc.vector.tensor_tensor(y.c2[:, 0], y.c2[:, 0], y.c2[:, 1], ALU.add).then_inc(s, 1)
                yield
                yield
                dve.wait_ge(conv_pe[y.q].sem, conv_pe[y.q].after(blk, "c2T"))
                nc.vector.tensor_tensor(sum_t[:, y.q], tok(y.a, H), x2_t[:, y.ts, :], ALU.add).then_inc(s, 1)
                dve.wait_ge(s, m.after(blk, "sum"))
                norm_stats(dve, m, blk, "", sum_t[:, y.q], y.q, 1e-12)
                yield
                yield
                norm_apply(dve, m, blk, "", sum_t[:, y.q], y.h_t, y.q, conv_pool[y.q], (gains[:, 0], shifts[:, 0]))
                yield

            @staticmethod
            def att(dve, blk, y, i):
                m, pe, pool = att_vec[y.q], att_pe[y.q], att_pool[y.q]
                s = m.sem

                def after(name, k=0):
                    dve.wait_ge(s, m.after(blk, f"{i}{name}", k))

                for _ in range(5):
                    yield
                dve.wait_ge(pool.sem, pool.after(blk, f"{i}plus"))
                for odd in range(2):
                    nc.vector.tensor_tensor(y.rot[:, :, :, odd::2], y.qk[:, :, :, 1 - odd::2],
                                            sin[:, :, odd::2].unsqueeze(2).to_broadcast([P, H, 2, D // 2]),
                                            ALU.mult).then_inc(s, 1)
                yield
                dve.wait_ge(pe.sem, pe.after(blk, f"{i}kmean"))
                nc.vector.tensor_tensor(y.den, y.qk[:, :, 0, :], y.b[:, 0:D].unsqueeze(1).to_broadcast([P, H, D]),
                                        ALU.mult).then_inc(s, 1)
                dve.wait_ge(pool.sem, pool.after(blk, f"{i}cos"))
                after("swap", 1)
                nc.vector.tensor_tensor(y.rot, y.rot, y.big, ALU.add).then_inc(s, 1)
                yield
                after("den")
                nc.vector.tensor_reduce(y.z[:], y.den.rearrange("p t (h e) -> p (t h) e", e=HD), AX.X, ALU.add).then_inc(s, 1)
                yield
                after("head")
                nc.vector.tensor_scalar(y.z[:], y.z[:], 1e-6, None, ALU.add).then_inc(s, 1)
                after("eps6")
                nc.vector.reciprocal(y.z[:], y.z[:]).then_inc(s, 1)
                dve.wait_ge(pe.sem, pe.after(blk, f"{i}kv"))
                nc.vector.tensor_tensor(y.kvm[:], y.a[:, 0:D], headmask[:], ALU.mult).then_inc(s, 1)
                yield
                yield
                dve.wait_ge(pe.sem, pe.after(blk, f"{i}o"))
                after("z")
                nc.vector.tensor_tensor(sum_t[:, y.q].rearrange("p t (h e) -> p (t h) e", e=HD),
                                        y.a[:, 0:N].rearrange("p (h e) -> p h e", e=HD),
                                        y.z[:].unsqueeze(2).to_broadcast([P, H * HEADS, HD]), ALU.mult).then_inc(s, 1)
                after("oz")
                nc.vector.tensor_tensor(sum_t[:, y.q], sum_t[:, y.q], y.h_t, ALU.add).then_inc(s, 1)
                after("sum")
                norm_stats(dve, m, blk, str(i), sum_t[:, y.q], y.q, 1e-12)
                yield
                yield
                norm_apply(dve, m, blk, str(i), sum_t[:, y.q], y.h_t, y.q, pool, (gains[:, 1 + i], shifts[:, 1 + i]))
                yield

            @staticmethod
            def ffn(dve, blk, y):
                m = ffn_vec[y.q]
                s = m.sem
                for _ in range(9):
                    yield
                dve.wait_ge(ffn_pe[y.q].sem, ffn_pe[y.q].after(blk, "fT"))
                nc.vector.tensor_tensor(sum_t[:, y.q], tok(y.a, H), y.h_t, ALU.add).then_inc(s, 1)
                dve.wait_ge(s, m.after(blk, "sum"))
                norm_stats(dve, m, blk, "i", sum_t[:, y.q], y.q, 1e-12)
                yield
                yield
                norm_apply(dve, m, blk, "i", sum_t[:, y.q], y.h_t, y.q, ffn_pool[y.q], (gains[:, L + 1], shifts[:, L + 1]))
                dve.wait_ge(s, m.after(blk, "ishift"))
                nc.vector.tensor_tensor(sum_t[:, y.q], y.h_t, x2_t[:, y.ts, :], ALU.add).then_inc(s, 1)
                dve.wait_ge(s, m.after(blk, "sum2"))
                norm_stats(dve, m, blk, "o", sum_t[:, y.q], y.q, 1e-5)
                yield
                yield
                norm_apply(dve, m, blk, "o", sum_t[:, y.q], x3_t[:, y.ts, :], y.q, ffn_pool[y.q])
                yield

            @staticmethod
            def moe(dve, blk):
                yield
                for k in range(E // 2):
                    dve.wait_ge(moe_wB.sem, moe_wB.after(blk, "wB", 2 * k + 1))
                    nc.vector.tensor_copy(wB[:, 2 * k + 1, :], gate[1][:]).then_inc(moe_vec.sem, 1)
                    yield
                for s in range(STEPS + 2):
                    yield
                    if 1 <= s <= STEPS:
                        r = s - 1
                        e, j = divmod(r, FC)
                        dve.wait_ge(moe_up.sem, moe_up.after(blk, "up", r))
                        dve.wait_ge(moe_pool.sem, moe_pool.after(blk, "gw", r))
                        if r >= 2:
                            dve.wait_ge(moe_y.sem, moe_y.after(blk, "y", r - 2))
                        nc.vector.scalar_tensor_tensor(out=p[:, r % 2, :], in0=up[:], scalar=col("e_b1", e * 2 * FC + j),
                                                       in1=gw[:, r % 2, :], op0=ALU.add, op1=ALU.mult).then_inc(moe_vec.sem, 1)
                    yield

            @staticmethod
            def moe_out(dve, blk):
                s = moe_vec.sem
                yield
                yield
                dve.wait_ge(moe_y.sem, moe_y.after(blk, "yT"))
                nc.vector.tensor_tensor(sumx[:], tok(gate[0], T), x1_t[:], ALU.add).then_inc(s, 1)
                dve.wait_ge(s, moe_vec.after(blk, "sum"))
                norm_stats(dve, moe_vec, blk, "", sumx, X, 1e-5)
                yield
                yield
                norm_apply(dve, moe_vec, blk, "", sumx, x2_t, X, moe_pool)
                yield

            @staticmethod
            def ter(dve, blk, done):
                s = ter_vec.sem
                for _ in range(4):
                    yield
                for c in range(FC):
                    dve.wait_ge(ter_pe.sem, ter_pe.after(blk, "gu", c))
                    dve.wait_ge(ter_act.sem, ter_act.after(blk, "silu", c))
                    nc.vector.scalar_tensor_tensor(out=tA[:, c, :], in0=(up, ybank)[c % 2][:], scalar=col("w2_s", c),
                                                   in1=u[:, c % 2, :], op0=ALU.mult, op1=ALU.mult).then_inc(s, 1)
                    yield
                for _ in range(2 * FC + 4):
                    yield
                dve.wait_ge(ter_pe.sem, ter_pe.after(blk, "yT"))
                dve.wait_ge(moe_vec.sem, moe_vec.before(done + 1))
                nc.vector.tensor_tensor(sumx[:], tok(up, T), x3_t[:], ALU.add).then_inc(s, 1)
                dve.wait_ge(s, ter_vec.after(blk, "sum"))
                norm_stats(dve, ter_vec, blk, "", sumx, X, 1e-5)
                yield
                yield
                dve.wait_ge(out_put.sem, out_put.before(blk))
                norm_apply(dve, ter_vec, blk, "", sumx, o_t, X, ter_pool)
                yield

        class Pool:
            @staticmethod
            def mix(pool, blk, y):
                m = mix_pool[y.q]
                for _ in range(5):
                    yield
                pool.wait_ge(begun, 1)
                pool.wait_ge(mix_vec[y.q].sem, mix_vec[y.q].after(blk, "clip"))
                nc.gpsimd.tensor_tensor(y.rn[:].rearrange("p t c -> p (t c)"), y.ssq[:].rearrange("p t c -> p (t c)"),
                                        minus_half[:, 0:2 * H], ALU.pow).then_inc(m.sem, 1)
                yield
                for _ in range(3):
                    yield
                norm_power(pool, m, blk, "", mix_vec[y.q], y.q, H)
                yield
                yield

            @staticmethod
            def route(pool, blk, y):
                for _ in range(4):
                    yield
                norm_power(pool, route_pool[y.q], blk, "", route_vec[y.q], y.q, H)
                for _ in range(11):
                    yield

            @staticmethod
            def conv(pool, blk, y):
                m = conv_pool[y.q]
                wait_apart(pool, conv_pe[y.q].sem, conv_pe[y.q].after(blk, "x2T"))
                for side in range(2):
                    at = side * (PAD + N)
                    nc.gpsimd.memset(y.c1F[:, :, at:at + PAD], 0.0).then_inc(m.sem, 1)
                yield
                for _ in range(14):
                    yield
                norm_power(pool, m, blk, "", conv_vec[y.q], y.q, H)
                yield
                yield

            @staticmethod
            def att(pool, blk, y, i):
                m = att_pool[y.q]
                for _ in range(4):
                    yield
                wait_apart(pool, att_act[y.q].sem, att_act[y.q].after(blk, f"{i}v", H - 1))
                nc.gpsimd.tensor_scalar(y.qk, y.qk, 0.21, None, ALU.add).then_inc(m.sem, 1)
                yield
                pool.wait_ge(m.sem, m.after(blk, f"{i}plus"))
                nc.gpsimd.tensor_tensor(y.big, y.qk, cos[:].unsqueeze(2).to_broadcast([P, H, 2, D]), ALU.mult).then_inc(m.sem, 1)
                yield
                for _ in range(5):
                    yield
                norm_power(pool, m, blk, str(i), att_vec[y.q], y.q, H)
                yield
                yield

            @staticmethod
            def ffn(pool, blk, y):
                for _ in range(10):
                    yield
                norm_power(pool, ffn_pool[y.q], blk, "i", ffn_vec[y.q], y.q, H)
                yield
                yield
                norm_power(pool, ffn_pool[y.q], blk, "o", ffn_vec[y.q], y.q, H)
                yield
                yield

            @staticmethod
            def moe(pool, blk):
                for _ in range(5):
                    yield
                pool.wait_ge(moe_vec.sem, moe_vec.after(blk, "wB", E // 2 - 1))
                for s in range(STEPS + 2):
                    if 1 <= s <= STEPS:
                        r = s - 1
                        pool.wait_ge(moe_act.sem, moe_act.after(blk, "gelu", r))
                        if r >= 2:
                            pool.wait_ge(moe_vec.sem, moe_vec.after(blk, "p", r - 2))
                        nc.gpsimd.tensor_tensor(gw[:, r % 2, :], g[:, r % 2, :], wB[:, r // FC, :],
                                                ALU.mult).then_inc(moe_pool.sem, 1)
                    yield
                    yield

            @staticmethod
            def moe_out(pool, blk):
                for _ in range(3):
                    yield
                norm_power(pool, moe_pool, blk, "", moe_vec, X, T)
                yield
                yield

            @staticmethod
            def ter(pool, blk, done):
                for _ in range(22):
                    yield
                norm_power(pool, ter_pool, blk, "", ter_vec, X, T)
                for _ in range(3):
                    yield

        def head(e, eng, blk, first, end):
            return [(chain(e.mix(eng, blk, y), e.route(eng, blk, y)), HEAD_SLOTS, first + y.q * LAG, end - (1 - y.q) * LAG)
                    for y in seqs]

        def body(e, eng, blk, first, end):
            return [(chain(e.conv(eng, blk, y), *[e.att(eng, blk, y, i) for i in range(L)], e.ffn(eng, blk, y)), BODY_SLOTS,
                     first + y.q * LAG, end - (1 - y.q) * LAG) for y in seqs]

        LAG = 3

        def run(e, eng, start, between, finish):
            start()
            weave(*head(e, eng, 0, 0, HEAD_SLOTS + LAG))
            extra = [(between(), TERNARY_SLOTS, 0, MOE_SLOTS)] if between else []
            weave((e.moe(eng, 0), MOE_SLOTS, 0, MOE_SLOTS), *extra)
            weave((e.moe_out(eng, 0), MOE_OUT_SLOTS, 0, MOE_OUT_SLOTS), *head(e, eng, 1, 0, HEAD_SLOTS + LAG))

            def steady(blk, with_head):
                rounds = max(MOE_SLOTS, BODY_SLOTS + LAG)
                weave((e.moe(eng, blk), MOE_SLOTS, 0, rounds), *body(e, eng, blk - 1, 0, rounds))
                rounds = MOE_OUT_SLOTS + TER_SLOTS
                weave((chain(e.moe_out(eng, blk), e.ter(eng, blk - 1, blk)), rounds, 0, rounds),
                      *(head(e, eng, blk + 1, 0, rounds) if with_head else []))

            with eng.Fori(1, BLOCKS - 1) as blk:
                steady(blk, True)
            steady(BLOCKS - 1, False)
            weave(*body(e, eng, BLOCKS - 1, 0, BODY_SLOTS + LAG))
            weave((e.ter(eng, BLOCKS - 1, BLOCKS - 1), TER_SLOTS, 0, TER_SLOTS))
            finish()

        def nothing():
            pass

        @block.sync
        def _(sp):
            begin(sp, x_got, out_put)

            def load_x(blk):
                for q in range(SEQS):
                    sp.wait_ge(mix_vec[q].sem, mix_vec[q].before(blk))
                sp.dma_start(x_t[:], x_in[bass.ds(blk * W, W), :].rearrange("(t p) d -> p t d", p=P)).then_inc(x_got.sem, 16)

            def put(blk):
                sp.wait_ge(ter_vec.sem, ter_vec.before(blk + 1))
                sp.dma_start(out[bass.ds(blk * W, W), :].rearrange("(t p) d -> p t d", p=P), o_t[:]).then_inc(out_put.sem, 16)

            load_x(0)
            for dst, src in early_loads:
                sp.dma_start(dst, src).then_inc(early, 16)
            for dst, src in later_loads:
                sp.dma_start(dst, src).then_inc(later, 16)
            for q in range(SEQS):
                sp.wait_ge(route_act[q].sem, route_act[q].before(1))
            for r in range(3):
                if r == 2:
                    sp.wait_ge(set_pe, 2 + ROUND1)
                for dst, name in loads[r]:
                    sp.dma_start(dst, a[name].rearrange("(c p) i -> p c i", p=P)).then_inc(staged[r], 16)
            load_x(1)
            with sp.Fori(1, BLOCKS - 1) as blk:
                load_x(blk + 1)
                put(blk - 1)
            put(BLOCKS - 2)
            put(BLOCKS - 1)
            sp.wait_ge(out_put.sem, out_put.before(BLOCKS))

        @block.tensor
        def _(pe):
            begin(pe, *mix_pe, *route_pe, *conv_pe, *att_pe, *ffn_pe, moe_wB, moe_gate, moe_up, moe_y, ter_pe)
            run(Pe, pe, lambda: Pe.setup(pe), lambda: Pe.ternary(pe), nothing)

        @block.scalar
        def _(act):
            begin(act, *mix_act, *route_act, *conv_act, *att_act, *ffn_act, moe_act, ter_act)
            for e in range(E):
                act.dma_start(e_w1[:, e, :], a["L0_ffn_W1"][e]).then_inc(e_got[e], 16)
                act.dma_start(e_w2[:, e, :, :], a["L0_ffn_W2"][e].rearrange("(c p) d -> p c d", p=P)).then_inc(e_got[e], 16)
            run(Act, act, lambda: Act.setup(act), lambda: Act.ternary(act), nothing)

        @block.vector
        def _(dve):
            begin(dve, *mix_vec, *route_vec, *conv_vec, *att_vec, *ffn_vec, moe_vec, ter_vec)
            run(Vec, dve, lambda: Vec.setup(dve), None, nothing)

        @block.gpsimd
        def _(pool):
            begin(pool, *mix_pool, *route_pool, *conv_pool, *att_pool, *ffn_pool, moe_pool, ter_pool)
            run(Pool, pool, nothing, None, nothing)


_INS = ["L0_attn_x", "L0_attn_W_q", "L0_attn_W_k", "L0_attn_W_v", "L0_ffn_Wr1", "L0_ffn_br1", "L0_ffn_ln_scale",
        "L0_ffn_ln_bias", "L0_ffn_Wr2", "L0_ffn_br2", "L0_ffn_W1", "L0_ffn_b1", "L0_ffn_W2", "L0_ffn_b2",
        "L1_attn_conv1_w", "L1_attn_conv1_b", "L1_attn_conv2_w", "L1_attn_conv2_b", "L1_attn_ln0_g", "L1_attn_ln0_b",
        "L1_attn_Wq", "L1_attn_bq", "L1_attn_Wk", "L1_attn_bk", "L1_attn_Wv", "L1_attn_bv", "L1_attn_lnA_g",
        "L1_attn_lnA_b", "L1_attn_W1", "L1_attn_b1", "L1_attn_W2", "L1_attn_b2", "L1_attn_ln2_g", "L1_attn_ln2_b",
        "L1_ffn_w1_w", "L1_ffn_w1_s", "L1_ffn_w2_w", "L1_ffn_w2_s", "L1_ffn_h1_w", "L1_ffn_h1_s", "L1_ffn_h2_w",
        "L1_ffn_h2_s", "L1_ffn_w3_w", "L1_ffn_w3_s"]


def constants():
    f = np.float32
    inv = f(1.0) / f(10000.0) ** (np.arange(0, D, 2, dtype=f) / f(D))
    freqs = np.repeat(np.arange(N, dtype=f)[:, None] * inv[None, :], 2, axis=-1)
    sign = np.where(np.arange(D) % 2 == 0, f(-1), f(1))
    tiles = lambda m: np.ascontiguousarray(m.reshape(N // P, P, D).transpose(1, 0, 2)).astype(f)
    head = np.arange(D) // HD
    e = np.arange(E)
    return {
        "c_ident": np.eye(P, dtype=f),
        "c_mean_of": np.full((P, P), 1.0 / N, f),
        "c_headmask": np.where(head[:, None] == head[None, :], f(1.0 / N), f(0)).astype(f),
        "c_cos": tiles(np.cos(freqs)),
        "c_sin": tiles(np.sin(freqs) * sign),
        "c_earlier": np.broadcast_to((e[None, :] < e[:, None]).astype(f), (P, E, E)).copy(),
    }


def kernel(**inputs):
    import concourse.bacc as _bacc
    from concourse.bass_utils import run_bass_kernel_spmd as _run

    nc = _bacc.Bacc("TRN2", target_bir_lowering=False, num_devices=1)
    arrays, aps = {}, {}
    for name, value in {**{n: inputs[n] for n in _INS}, **constants()}.items():
        v = np.ascontiguousarray(value)
        arrays[f"in_{name}_dram"] = v
        aps[name] = nc.dram_tensor(f"in_{name}_dram", v.shape, mybir.dt.from_np(v.dtype), kind="ExternalInput").ap()
    out = nc.dram_tensor("out_0_dram", (B, N, D), F32, kind="ExternalOutput").ap()
    build(nc, aps["L0_attn_x"].rearrange("b n d -> (b n) d"), out.rearrange("b n d -> (b n) d"), aps)
    r = _run(nc, [arrays], core_ids=[0])
    return r.results[0]["out_0_dram"]
```

```python
from contextlib import ExitStack

import numpy as np

import concourse.bass as bass
from concourse import mybir

F32 = mybir.dt.float32
F32R = mybir.dt.float32r
ALU = mybir.AluOpType
ACT = mybir.ActivationFunctionType
AX = mybir.AxisListType

P = 128
B, N, D = 8, 256, 128
SEQS = 2
H = N // P
T = SEQS * H
W = T * P
BLOCKS = B // SEQS
E, F = 8, 512
FC = F // P
R = D // 2
L = 4
HEADS = 16
HD = D // HEADS
TAPS, PAD = 5, 2
STEPS = E * FC

ROWS = {}
_at = 0
for _name, _n in (("e_b1", 2 * FC * E), ("f_b1", FC), ("f_b2", 1), ("c2_b", 1), ("w1_s", FC), ("w2_s", FC),
                  ("h1_s", FC), ("h2_s", FC), ("w3_s", 1)):
    ROWS[_name] = (_at, _n)
    _at += _n
NROWS = _at


class Steps:

    def __init__(self, sem, *steps, unit=1):
        self.sem, self.unit, self.first, self.n = sem, unit, {}, 0
        for name, count in steps:
            self.first[name] = self.n
            self.n += count

    def after(self, blk, name, k=0):
        return self.before(blk) + (self.first[name] + k + 1) * self.unit

    def before(self, blk):
        return blk * (self.n * self.unit) + 1


def norm_steps(name, tiles, affine=False):
    return ([(name + "stats", tiles), (name + "aggr", tiles), (name + "eps", 1)] + [(name + "gain", tiles)] * affine
            + [(name + "apply", tiles)])


MIX_SLOTS = [0.6, 0.45, 1.3, 0.9, 1.5, 0.8, 0.6, 0.5, 1.8, 0.8, 0.5]
ROUTE_SLOTS = [0.6, 0.45, 0.5, 1., 0.8, 0.9, 1.77, 0.5, 0.45, 0.4, 2.6, 0.85, 1.2, 0.5, 0.45]
CONV_SLOTS = [1.97, 0.61] + [2.2] * TAPS + [3.2] + [2.56] * 4 + [0.4, 0.6, 1.64, 0.8, 1.2]
ATT_SLOTS = [0.6, 0.45, 0.8, 1.23, 2.3, 0.8, 1.51, 0.61, 0.23, 1.5, 0.73, 2.16]
FFN_SLOTS = [0.6, 0.81, 0.85, 2.3, 0.85, 2.3, 1.19, 0.6, 0.64, 1.4, 0.8, 2.8, 0.8, 0.8]
MOE_SLOTS = [1.28] * (2 * (STEPS + 2))
MOE_OUT_SLOTS = [0.65, 0.63, 2.61, 1., 0.9]
TER_SLOTS = [0.9, 0.65] + [1.7] * FC + [0.9] + [1.7] * (4 * FC) + [3.4, 0.65, 0.9, 2.2, 1.35, 0.9]
BODY_SLOTS = CONV_SLOTS + ATT_SLOTS * L + FFN_SLOTS
HEAD_SLOTS = MIX_SLOTS + ROUTE_SLOTS


def weave(*threads):
    order = []
    for i, (_, slots, start, end) in enumerate(threads):
        at, scale = start, (end - start) / sum(slots)
        for length in slots:
            order.append((round(at, 6), i))
            at += length * scale
    for _, i in sorted(order):
        next(threads[i][0], None)
    for gen, _, _, _ in threads:
        assert next(gen, "end") == "end", "a stage has more slots than it says"


def chain(*gens):
    for gen in gens:
        yield from gen


def build(nc, x_in, out, w_rows, a):
    ctx = ExitStack()
    with ctx:
        def sb(name, shape, dt=F32):
            return ctx.enter_context(nc.sbuf_tensor(name, shape, dt))

        def sem(name):
            return ctx.enter_context(nc.semaphore(name))

        def bank(name):
            return ctx.enter_context(nc.psum_tensor(name, [P, 512], F32))

        gate = [bank(f"gate{i}") for i in range(2)]
        up = bank("up")
        ybank = bank("ybank")
        gate_bank, up_banks = gate[0], [gate[1], up]
        ab = [[bank(f"seq{q}_{i}") for i in range(2)] for q in range(SEQS)]

        ident = sb("ident", [P, P])
        mean_of = sb("mean_of", [P, P])
        headmask = sb("headmask", [P, P])
        cos = sb("cos", [P, H, D])
        sin = sb("sin", [P, H, D])
        earlier = sb("earlier", [P, E, E])
        ones = sb("ones", [1, P])
        plus = sb("plus", [1, D])
        minus_half = sb("minus_half", [P, 2 * T])
        cols = sb("cols", [P, NROWS])
        wqkv0 = sb("wqkv0", [P, 3 * D])
        wr1 = sb("wr1", [P, R])
        wr2 = sb("wr2", [R, E])
        e_w1lo = sb("e_w1lo", [P, E, 2 * F], F32R)
        e_w1hi = sb("e_w1hi", [P, E, 2 * F], F32R)
        e_w2 = sb("e_w2", [P, E, FC, D])
        e_b2 = sb("e_b2", [E, D])
        br1 = sb("br1", [P, R])
        r_g = sb("r_g", [P, R])
        r_b = sb("r_b", [P, R])
        br2 = sb("br2", [P, E])
        c1_w = sb("c1_w", [P, 4, TAPS])
        c1_b = sb("c1_b", [P, 4])
        c2_w = sb("c2_w", [P, 4, TAPS])
        gains = sb("gains", [P, L + 2, D])
        shifts = sb("shifts", [P, L + 2, D])
        a_w = sb("a_w", [P, L, 3 * D])
        a_bs = sb("a_bs", [32 + L, 3 * D], F32R)
        a_sel = sb("a_sel", [32 + L, L], F32R)
        f_w1 = sb("f_w1", [P, F])
        f_w2 = sb("f_w2", [P, FC, D])
        t_w12 = sb("t_w12", [P, 2, F])
        t_h = sb("t_h", [P, 2, FC, F])
        t_w3 = sb("t_w3", [P, FC, D])

        x_t = sb("x_t", [P, T, D])
        x1_sets = [tuple(sb(n + i, shape, dt) for n, shape, dt in (
            ("x1_t", [P, T, D], F32), ("x1hi", [P, W], F32R), ("x1lo", [P, W], F32R), ("wT", [E, W], F32))) for i in ("0", "")]
        x2_t = sb("x2_t", [P, T, D])
        r_t = sb("r_t", [P, T, D])
        x3_t = sb("x3_t", [P, 2 * T, D])
        xroom = sb("xroom", [P, 4, 2, W])
        g, gw, p, wB = (xroom[:, i] for i in range(4))
        yF = p[:, 0]
        tA, tB = (xroom[:, 2 * i:2 * i + 2].rearrange("p a c w -> p (a c) w") for i in range(2))
        u, x3F, tyF = tB[:, 0:2], tB[:, 2], tB[:, 3]
        o_t = sb("o_t", [P, T, D])
        sumx = sb("sumx", [P, T, D])

        ROOM = 8 * N
        room = sb("room", [P, SEQS, ROOM])
        hh = sb("hh", [P, SEQS, 2, H * D])
        x2F = sb("x2F", [P, SEQS, N + 2 * PAD])
        sum_t = sb("sum_t", [P, SEQS, H, D])

        def cut(memory):
            at = 0

            def part(n):
                nonlocal at
                at += n
                assert at <= memory.shape[1]
                return memory[:, at - n:at]
            return part

        def token_major(v):
            return v.rearrange("p (t d) -> p t d", t=H)

        class Seq:

            def __init__(self, q):
                self.q, self.thread, self.ts = q, q, slice(q * H, (q + 1) * H)
                self.a, self.b = ab[q]
                self.room = room[:, q]
                self.h_t = token_major(hh[:, q, 0])
                self.hF = hh[:, q, 1]
                self.c2 = hh[:, q]
                self.sum = sum_t[:, q]
                part = cut(self.room)
                self.qk, self.rot, self.big = (part(2 * N).rearrange("p (c t d) -> p c t d", t=H, c=2) for _ in range(3))
                self.vt, self.den = (token_major(part(N)) for _ in range(2))
                self.qF = self.big[:, 0].rearrange("p t d -> p (t d)")
                part = cut(self.room)
                self.c1F = part(4 * (N + 2 * PAD)).rearrange("p (j n) -> p j n", j=4)
                self.c1 = self.c1F[:, :, PAD:PAD + N]
                part = cut(self.room)
                self.ffh = part(FC * N).rearrange("p (c n) -> p c n", c=FC)
                self.z = sb(f"z{q}", [P, H * HEADS])
                self.kvm = sb(f"kvm{q}", [P, D])

        class Head:

            def __init__(self, q, thread, banks, memory, hF, total, small):
                self.q, self.thread, self.ts = q, thread, slice(q * H, (q + 1) * H)
                self.a, self.b = banks
                self.hF, self.sum = hF, total
                part = cut(memory)
                self.qkv = part(3 * N).rearrange("p (t c d) -> p t c d", t=H, c=3)
                self.sq = part(2 * N).rearrange("p (t c d) -> p t c d", t=H, c=2)
                self.kvt = token_major(part(N))
                part = cut(memory)
                self.hr, self.hg = (token_major(part(H * R)) for _ in range(2))
                self.hT = part(N)
                self.cmp1, self.cmp2 = (part(H * E * E).rearrange("p (t e f) -> p t e f", t=H, e=E) for _ in range(2))
                self.ssq, self.rn, self.lg, self.rank, self.lex, self.wts, self.lmax = small

        seqs = [Seq(q) for q in range(SEQS)]
        small = [[sb(f"{n}{q}", shape) for n, shape in (
            ("ssq", [P, H, 2]), ("rn", [P, H, 2]), ("lg", [P, H, E]), ("rank", [P, H, E]), ("lex", [P, H, E]),
            ("wts", [P, H, E]), ("lmax", [P, H]))] for q in range(SEQS)]
        early_heads = [Head(q, q, ab[q], room[:, q], y.hF, y.sum, small[q]) for q, y in enumerate(seqs)]
        late_heads = []
        for q in range(SEQS):
            part = cut(xroom[:, 2 * q:2 * q + 2].rearrange("p i a w -> p (i a w)"))
            late_heads.append(Head(q, 3 + q, (gate, [up, ybank])[q], part(6 * N), part(N), token_major(part(N)), small[q]))

        stat = [(sb(f"st{i}", [P, T, 6]), sb(f"mv{i}", [P, T, 2]), sb(f"ve{i}", [P, T]), sb(f"rs{i}", [P, T])) for i in range(3 + SEQS)]
        X = 2

        raw = room[:].rearrange("p q n -> p (q n)")
        wqkv0_raw = x3_t[:, 0:3, :]
        rows = x3_t[:, 3, :]
        e_raw = [v[:, i * 2 * F:(i + 1) * 2 * F]
                 for v in (xroom[:].rearrange("p i a w -> p (i a w)"), t_h[:].rearrange("p a k f -> p (a k f)")) for i in range(E // 2)]
        a_b = sumx[:].rearrange("p t d -> p (t d)")[:, 0:3 * D]

        def col(name, k=0):
            return cols[:, ROWS[name][0] + k:ROWS[name][0] + k + 1]

        x_got = Steps(sem("x_got"), ("x", 1), unit=16)
        w_put = Steps(sem("w_put"), ("w", 1), unit=16)
        out_put = Steps(sem("out_put"), ("out", 1), unit=16)

        def pair(name, *steps):
            return [Steps(sem(f"{name}{q}"), *steps) for q in range(SEQS)]

        mix_pe = pair("mix_pe", ("xT", 1), ("qkv", H), ("mean", 1))
        mix_act = pair("mix_act", ("xF", 1), ("qkv", H))
        mix_vec = pair("mix_vec", ("square", 1), ("ssq", 1), ("clip", 1), ("kv", H), ("q", H), ("sum", 1), *norm_steps("", H))
        mix_pool = pair("mix_pool", ("len", 1), ("rstd", 1))
        route_pe = pair("route_pe", ("x1T", 1), ("h", 1), ("hT", 1), ("logit", 1), ("wT", 1))
        route_act = pair("route_act", ("x1F", 1), ("x1hi", 1), ("gelu", 1), ("hT", 1), ("exp", 1), ("wT", 1))
        route_vec = pair("route_vec", ("h", 1), *norm_steps("", H, True), ("logit", 1), ("above", 1), ("tie", 1),
                         ("tie_earlier", 1), ("beats", 1), ("rank", 1), ("chosen", 1), ("max", 1), ("less_max", 1),
                         ("keep", 1), ("total", 1), ("recip", 1), ("weight", 1))
        route_pool = pair("route_pool", ("x1lo", 1), ("rstd", 1))
        conv_pe = pair("conv_pe", ("x2T", 1), ("c2T", 1))
        conv_act = pair("conv_act", ("x2F", 1), ("gelu", 4))
        conv_vec = pair("conv_vec", ("tap1", 4 * TAPS), ("tap2", 4 * TAPS), ("c2", 1), ("sum", 1), *norm_steps("", H, True))
        conv_pool = pair("conv_pool", ("pad", 2), ("x2", 1), ("rstd", 1))
        att_pe = pair("att_pe", *[(f"{i}{s}", n) for i in range(L) for s, n in (
            ("hT", 1), ("qkv", H), ("kmean", 1), ("kv", 1), ("qT", 1), ("o", 1))])
        att_act = pair("att_act", *[(f"{i}{s}", n) for i in range(L) for s, n in (("hF", 1), ("v", H), ("qF", 1))])
        att_vec = pair("att_vec", *[s for i in range(L) for s in (
            (f"{i}swap", 2), (f"{i}cos", 1), (f"{i}rot", 1), (f"{i}den", 1), (f"{i}kvm", 1), (f"{i}head", 1),
            (f"{i}eps6", 1), (f"{i}z", 1), (f"{i}oz", 1), (f"{i}sum", 1), *norm_steps(str(i), H, True))])
        att_pool = pair("att_pool", *[(f"{i}{s}", n) for i in range(L) for s, n in (("rstd", 1),)])
        ffn_pe = pair("ffn_pe", ("hT", 1), ("up", FC), ("down", 1), ("fT", 1))
        ffn_act = pair("ffn_act", ("hF", 1), ("gelu", FC), ("fF", 1))
        ffn_vec = pair("ffn_vec", ("sum", 1), *norm_steps("i", H, True), ("sum2", 1), *norm_steps("o", H))
        ffn_pool = pair("ffn_pool", ("irstd", 1), ("orstd", 1))

        moe_wB = [Steps(sem(f"moe_wB{i}"), ("wB", E // 2), unit=16) for i in range(2)]
        moe_gate = Steps(sem("moe_gate"), ("gate", STEPS))
        moe_up = Steps(sem("moe_up"), ("up", STEPS))
        moe_y = Steps(sem("moe_y"), ("y", STEPS), ("yT", 1))
        moe_act = Steps(sem("moe_act"), ("gelu", STEPS), ("yF", 1))
        moe_pool = Steps(sem("moe_pool"), ("gw", STEPS), ("rstd", 1))
        moe_vec = Steps(sem("moe_vec"), ("p", STEPS), ("sum", 1), *norm_steps("", T))
        ter_pe = Steps(sem("ter_pe"), ("x3T", 1), ("gu", FC), ("h1", FC), ("h2", FC), ("w3", 1), ("yT", 1))
        ter_act = Steps(sem("ter_act"), ("x3F", 1), ("silu", FC), ("h1", FC), ("h2", FC), ("yF", 1))
        ter_vec = Steps(sem("ter_vec"), ("h", FC), ("sum", 1), *norm_steps("", T))
        ter_pool = Steps(sem("ter_pool"), ("rstd", 1))

        def first(blk):
            return isinstance(blk, int) and blk == 0

        def x1_of(blk):
            return x1_sets[0 if first(blk) else 1]

        def begin(eng, *counts):
            for c in counts:
                eng.sem_inc(c.sem, 1)

        begun = sem("begun")
        passed = sem("passed")
        firsts = sem("firsts")
        early = sem("early")
        vectors = sem("vectors")
        later = sem("later")
        e_got = [sem(f"e_got{e}") for e in range(E)]
        w2_got = [sem(f"w2_got{e}") for e in range(E)]
        e_high, e_low = sem("e_high"), sem("e_low")
        staged = [sem(f"staged{i}") for i in range(3)]
        set_pe, set_act = sem("set_pe"), sem("set_act")

        block = ctx.enter_context(nc.Block())

        def row(v):
            return v.rearrange("(a n) -> a n", a=1).partition_broadcast(P)

        def rows_of(name):
            at, n = ROWS[name]
            return rows[at:at + n, :]

        first_loads = [
            (ident[:], a["c_ident"]), (wqkv0_raw[:, 0, :], a["L0_attn_W_q"]), (wqkv0_raw[:, 1, :], a["L0_attn_W_k"]),
            (wqkv0_raw[:, 2, :], a["L0_attn_W_v"]), (mean_of[:], a["c_mean_of"]),
        ]
        early_loads = [
            (wr1[:], a["L0_ffn_Wr1"]),
            (wr2[:], a["L0_ffn_Wr2"]), (br1[:], row(a["L0_ffn_br1"])), (r_g[:], row(a["L0_ffn_ln_scale"])),
            (r_b[:], row(a["L0_ffn_ln_bias"])), (br2[:], row(a["L0_ffn_br2"])), (earlier[:], a["c_earlier"]),
            (e_b2[:], a["L0_ffn_b2"]),
        ]
        vector_loads = [
            (rows_of("e_b1"), a["L0_ffn_b1"].rearrange("e (c p) -> (e c) p", p=P)),
        ] + [(rows_of(n), a[v].rearrange("(c p) -> c p", p=P)) for n, v in (
            ("f_b1", "L1_attn_b1"), ("f_b2", "L1_attn_b2"), ("c2_b", "L1_attn_conv2_b"), ("w1_s", "L1_ffn_w1_s"),
            ("w2_s", "L1_ffn_w2_s"), ("h1_s", "L1_ffn_h1_s"), ("h2_s", "L1_ffn_h2_s"), ("w3_s", "L1_ffn_w3_s"))
        ] + [(a_b[at:at + L, i * D:(i + 1) * D], a[v]) for at in (0, 32) for i, v in enumerate(
            ("L1_attn_bq", "L1_attn_bk", "L1_attn_bv"))]
        later_loads = [
            (c1_w[:], a["L1_attn_conv1_w"].rearrange("(c j) o k -> c j (o k)", j=4)),
            (c1_b[:], a["L1_attn_conv1_b"].rearrange("(c j) -> c j", j=4)), (c2_w[:], a["L1_attn_conv2_w"]),
            (cos[:], a["c_cos"]), (sin[:], a["c_sin"]), (headmask[:], a["c_headmask"]),
            (gains[:, 0, :], row(a["L1_attn_ln0_g"])), (shifts[:, 0, :], row(a["L1_attn_ln0_b"])),
            (gains[:, L + 1, :], row(a["L1_attn_ln2_g"])), (shifts[:, L + 1, :], row(a["L1_attn_ln2_b"])),
            (gains[:, 1:L + 1, :], a["L1_attn_lnA_g"].rearrange("(a l) d -> a l d", a=1).partition_broadcast(P)),
            (shifts[:, 1:L + 1, :], a["L1_attn_lnA_b"].rearrange("(a l) d -> a l d", a=1).partition_broadcast(P)),
            (a_w[:, :, 0:D], a["L1_attn_Wq"].rearrange("l i o -> i l o")),
            (a_w[:, :, D:2 * D], a["L1_attn_Wk"].rearrange("l i o -> i l o")),
            (a_w[:, :, 2 * D:3 * D], a["L1_attn_Wv"].rearrange("l i o -> i l o")),
            (f_w1[:], a["L1_attn_W1"]), (f_w2[:], a["L1_attn_W2"].rearrange("(c p) d -> p c d", p=P)),
        ]

        def chunked(v):
            return v.rearrange("p (c i) -> p c i", i=F)

        raw_w3 = o_t[:].rearrange("p t d -> p (t d)")
        raw_w = [raw[:, 0:FC * P], raw[:, FC * P:2 * FC * P]]
        raw_h = [raw[:, 2 * FC * P:2 * FC * P + FC * F], raw[:, 0:FC * F]]
        loads = [[(raw_w[w].rearrange("p (c i) -> p c i", c=FC), f"L1_ffn_w{w + 1}_w") for w in range(2)]
                 + [(chunked(raw_w3), "L1_ffn_w3_w")],
                 [(chunked(raw_h[0]), "L1_ffn_h1_w")], [(chunked(raw_h[1]), "L1_ffn_h2_w")]]
        groups = []
        for w in range(2):
            groups.append((0, [raw_w[w][:, c * P:(c + 1) * P] for c in range(FC)], t_w12[:, w, :]))
        groups.append((0, [raw_w3[:, k * P:(k + 1) * P] for k in range(FC)], t_w3[:].rearrange("p k d -> p (k d)")))
        for w in range(2):
            for k in range(FC):
                groups.append((w + 1, [raw_h[w][:, c * F + k * P:c * F + (k + 1) * P] for c in range(FC)], t_h[:, w, k, :]))
        ROUND0, ROUND1 = 3, 3 + FC
        TERNARY_SLOTS = [1.] * (len(groups) + 1)

        def wait_apart(eng, s, value):
            eng.wait_ge(s, value)
            eng.sem_inc(passed, 1)

        def norm_stats(dve, steps, blk, name, src, thread, eps, dst=None, gain=None):
            st, mv, ve, _ = stat[thread]
            s, n = steps.sem, src.shape[1]
            for t in range(n):
                nc.vector.bn_stats(st[:, t, :], src[:, t, :]).then_inc(s, 1)
            wait_apart(dve, s, steps.after(blk, name + "stats", n - 1))
            for t in range(n):
                nc.vector.bn_aggr(mv[:, t, :], st[:, t, :]).then_inc(s, 1)
            dve.wait_ge(s, steps.after(blk, name + "aggr", n - 1))
            nc.vector.tensor_scalar(ve[:, 0:n], mv[:, 0:n, 1], eps, None, ALU.add).then_inc(s, 1)
            if gain is not None:
                for t in range(n):
                    nc.vector.scalar_tensor_tensor(out=dst[:, t, :], in0=src[:, t, :], scalar=mv[:, t, 0:1], in1=gain,
                                                   op0=ALU.subtract, op1=ALU.mult).then_inc(s, 1)

        def norm_power(pool, steps, blk, name, vec, thread, n):
            _, _, ve, rs = stat[thread]
            pool.wait_ge(vec.sem, vec.after(blk, name + "eps"))
            nc.gpsimd.tensor_tensor(rs[:, 0:n], ve[:, 0:n], minus_half[:, 0:n], ALU.pow).then_inc(steps.sem, 1)

        def norm_apply(dve, steps, blk, name, src, dst, thread, power, shift=None):
            _, mv, _, rs = stat[thread]
            s, n = steps.sem, src.shape[1]
            dve.wait_ge(power.sem, power.after(blk, name + "rstd"))
            for t in range(n):
                if shift is None:
                    nc.vector.tensor_scalar(dst[:, t, :], src[:, t, :], mv[:, t, 0:1], rs[:, t:t + 1],
                                            ALU.subtract, ALU.mult).then_inc(s, 1)
                else:
                    dve.wait_ge(s, steps.after(blk, name + "gain", t))
                    nc.vector.scalar_tensor_tensor(out=dst[:, t, :], in0=dst[:, t, :], scalar=rs[:, t:t + 1], in1=shift,
                                                   op0=ALU.mult, op1=ALU.add).then_inc(s, 1)

        def turn(src, bank):
            for t in range(src.shape[1]):
                mm = nc.tensor.transpose(bank[0:src.shape[2], t * P:(t + 1) * P], src[:, t, :], ident[:])
            return mm

        def turn_back(srcF, bank):
            for t in range(srcF.shape[1] // P):
                mm = nc.tensor.transpose(bank[:, t * P:(t + 1) * P], srcF[:, t * P:(t + 1) * P], ident[:])
            return mm

        def tok(bank, tiles):
            return bank[:, 0:tiles * D].rearrange("p (t d) -> p t d", t=tiles)

        class Pe:
            @staticmethod
            def setup(pe):
                pe.wait_ge(firsts, 16 * len(first_loads))
                for i in range(3):
                    mm = nc.tensor.transpose(gate[0][:, i * P:(i + 1) * P], wqkv0_raw[:, i, :], ident[:])
                mm.then_inc(set_pe, 1)

            @staticmethod
            def columns(pe):
                pe.wait_ge(vectors, 16 * len(vector_loads))
                nc.tensor.transpose(gate[1][:, 0:NROWS], rows[0:NROWS, :], ident[0:NROWS, 0:NROWS]).then_inc(set_pe, 1)
                yield
                yield

            @staticmethod
            def ternary(pe):
                banks = [up, ab[0][0]]
                for n, (r, blocks, _) in enumerate(groups):
                    pe.wait_ge(staged[r], 16 * len(loads[r]))
                    if n >= 2:
                        pe.wait_ge(set_act, 2 + n - 1)
                    for c, src in enumerate(blocks):
                        mm = nc.tensor.transpose(ab[n % 2][1][:, c * P:(c + 1) * P], src, ident[:])
                    mm.then_inc(set_pe, 1)
                    yield
                yield

            @staticmethod
            def mix(pe, blk, y):
                m, act, vec = mix_pe[y.q], mix_act[y.q], mix_vec[y.q]
                pe.wait_ge(x_got.sem, x_got.after(blk, "x"))
                if isinstance(blk, int) and blk == 1:
                    pe.wait_ge(set_act, 2 + len(groups))
                elif not isinstance(blk, int):
                    pe.wait_ge(moe_vec.sem, moe_vec.after(blk - 1, "sum"))
                turn(x_t[:, y.ts, :], y.a).then_inc(m.sem, 1)
                yield
                yield
                pe.wait_ge(set_act, 1)
                pe.wait_ge(act.sem, act.after(blk, "xF"))
                for t in range(H):
                    nc.tensor.matmul((y.b, y.a)[t][:, 0:3 * D], y.hF[:, t * P:(t + 1) * P], wqkv0[:],
                                     start=True, stop=True).then_inc(m.sem, 1)
                yield
                for _ in range(4):
                    yield
                pe.wait_ge(vec.sem, vec.after(blk, "kv", H - 1))
                for t in range(H):
                    mm = nc.tensor.matmul(y.b[:, 0:D], mean_of[:], y.kvt[:, t, :], start=(t == 0), stop=(t == H - 1))
                mm.then_inc(m.sem, 1)
                yield
                for _ in range(3):
                    yield

            @staticmethod
            def route(pe, blk, y):
                m, act, vec = route_pe[y.q], route_act[y.q], route_vec[y.q]
                pe.wait_ge(mix_vec[y.q].sem, mix_vec[y.q].after(blk, "apply", H - 1))
                turn(x1_of(blk)[0][:, y.ts, :], y.a).then_inc(m.sem, 1)
                yield
                yield
                if first(blk):
                    pe.wait_ge(early, 16 * len(early_loads))
                pe.wait_ge(act.sem, act.after(blk, "x1F"))
                for t in range(H):
                    mm = nc.tensor.matmul(y.b[:, t * R:(t + 1) * R], y.hF[:, t * P:(t + 1) * P], wr1[:], start=True, stop=True)
                mm.then_inc(m.sem, 1)
                yield
                for _ in range(4):
                    yield
                wait_apart(pe, act.sem, act.after(blk, "gelu"))
                turn(y.hg, y.a).then_inc(m.sem, 1)
                yield
                yield
                pe.wait_ge(act.sem, act.after(blk, "hT"))
                for t in range(H):
                    mm = nc.tensor.matmul(y.b[:, t * E:(t + 1) * E], y.hT[0:R, t * P:(t + 1) * P], wr2[:], start=True, stop=True)
                mm.then_inc(m.sem, 1)
                yield
                for _ in range(3):
                    yield
                pe.wait_ge(vec.sem, vec.after(blk, "weight"))
                turn(y.wts[:], y.a).then_inc(m.sem, 1)
                yield
                yield

            @staticmethod
            def conv(pe, blk, y):
                m, vec = conv_pe[y.q], conv_vec[y.q]
                pe.wait_ge(moe_vec.sem, moe_vec.after(blk, "apply", T - 1))
                pe.wait_ge(route_act[y.q].sem, route_act[y.q].after(1, "wT"))
                pe.wait_ge(ffn_vec[y.q].sem, ffn_vec[y.q].before(blk))
                turn(x2_t[:, y.ts, :], y.a).then_inc(m.sem, 1)
                yield
                for _ in range(12):
                    yield
                pe.wait_ge(vec.sem, vec.after(blk, "c2"))
                turn_back(y.c2[:, 0], y.a).then_inc(m.sem, 1)
                yield
                for _ in range(3):
                    yield

            @staticmethod
            def att(pe, blk, y, i):
                m, act, vec = att_pe[y.q], att_act[y.q], att_vec[y.q]
                if i == 0:
                    pe.wait_ge(conv_vec[y.q].sem, conv_vec[y.q].before(blk + 1))
                else:
                    pe.wait_ge(vec.sem, vec.after(blk, f"{i - 1}apply", H - 1))
                turn(y.h_t, y.a).then_inc(m.sem, 1)
                yield
                yield
                pe.wait_ge(later, 16 * len(later_loads))
                pe.wait_ge(begun, SETUP_STEPS)
                pe.wait_ge(act.sem, act.after(blk, f"{i}hF"))
                for t in range(H):
                    bank = (y.b, y.a)[t]
                    nc.tensor.matmul(bank[:, 0:3 * D], y.hF[:, t * P:(t + 1) * P], a_w[:, i, :], start=True, stop=False)
                    nc.tensor.matmul(bank[:, 0:3 * D], a_sel[:, i:i + 1].to_broadcast([32 + L, P]), a_bs[:],
                                     start=False, stop=True).then_inc(m.sem, 1)
                yield
                yield
                pe.wait_ge(act.sem, act.after(blk, f"{i}v", H - 1))
                nc.tensor.matmul(y.b[:, 0:D], ones[:], plus[:], start=True, stop=False)
                for t in range(H):
                    mm = nc.tensor.matmul(y.b[:, 0:D], mean_of[:], y.qk[:, 1, t, :], start=False, stop=(t == H - 1))
                mm.then_inc(m.sem, 1)
                yield
                yield
                pe.wait_ge(vec.sem, vec.after(blk, f"{i}rot"))
                for t in range(H):
                    mm = nc.tensor.matmul(y.a[:, 0:D], y.rot[:, 1, t, :], y.vt[:, t, :], start=(t == 0), stop=(t == H - 1))
                mm.then_inc(m.sem, 1)
                pe.wait_ge(vec.sem, vec.after(blk, f"{i}den"))
                turn(y.rot[:, 0], y.b).then_inc(m.sem, 1)
                yield
                yield
                pe.wait_ge(act.sem, act.after(blk, f"{i}qF"))
                pe.wait_ge(vec.sem, vec.after(blk, f"{i}kvm"))
                for t in range(H):
                    mm = nc.tensor.matmul(y.a[:, t * P:(t + 1) * P], y.qF[:, t * P:(t + 1) * P], y.kvm[:], start=True, stop=True)
                mm.then_inc(m.sem, 1)
                yield
                for _ in range(3):
                    yield

            @staticmethod
            def ffn(pe, blk, y):
                m, act = ffn_pe[y.q], ffn_act[y.q]
                pe.wait_ge(att_vec[y.q].sem, att_vec[y.q].before(blk + 1))
                turn(y.h_t, y.a).then_inc(m.sem, 1)
                yield
                yield
                for j in range(FC):
                    pe.wait_ge(act.sem, act.after(blk, "hF") if j < 2 else act.after(blk, "gelu", j - 2))
                    nc.tensor.matmul((y.b, y.a)[j % 2][:, 0:N], f_w1[:, j * P:(j + 1) * P], y.hF, start=True, stop=True).then_inc(m.sem, 1)
                    if j % 2:
                        yield
                        yield
                for j in range(FC):
                    pe.wait_ge(act.sem, act.after(blk, "gelu", FC - 1))
                    mm = nc.tensor.matmul(y.b[:, 0:N], f_w2[:, j, :], y.ffh[:, j, :], start=(j == 0), stop=(j == FC - 1))
                mm.then_inc(m.sem, 1)
                yield
                yield
                pe.wait_ge(act.sem, act.after(blk, "fF"))
                turn_back(y.hF, y.a).then_inc(m.sem, 1)
                yield
                for _ in range(5):
                    yield

            @staticmethod
            def moe(pe, blk):
                for q in range(SEQS):
                    pe.wait_ge(route_act[q].sem, route_act[q].after(blk, "wT"))
                    pe.wait_ge(route_pool[q].sem, route_pool[q].after(blk, "x1lo"))
                if isinstance(blk, int) and blk == 0:
                    pe.wait_ge(set_act, 2)
                else:
                    pe.wait_ge(moe_vec.sem, moe_vec.after(blk - 1, "sum"))
                    if isinstance(blk, int):
                        pe.wait_ge(ter_vec.sem, ter_vec.after(0, "sum"))
                _, x1hi, x1lo, wT = x1_of(blk)

                def product(bank, at, e):
                    for k, (w, x) in enumerate(((e_w1hi, x1hi), (e_w1lo, x1hi), (e_w1hi, x1lo))):
                        mm = nc.tensor.matmul(bank, w[:, e, at:at + P], x[:], start=(k == 0), stop=(k == 2))
                    return mm

                for s in range(STEPS + 2):
                    if s < STEPS:
                        e, j = divmod(s, FC)
                        if j == 0:
                            if isinstance(blk, int) and blk == 0:
                                pe.wait_ge(e_low, max(e + 1, E // 2))
                        if s >= 1:
                            pe.wait_ge(moe_act.sem, moe_act.after(blk, "gelu", s - 1))
                        product(gate_bank[:], F + j * P, e).then_inc(moe_gate.sem, 1)
                    if s == 0:
                        nc.tensor.matmul(ybank[:], e_b2[:], wT[:], start=True, stop=False)
                    if s >= 2:
                        r = s - 2
                        if r % FC == 0 and isinstance(blk, int) and blk == 0:
                            pe.wait_ge(w2_got[r // FC], 16)
                        pe.wait_ge(moe_vec.sem, moe_vec.after(blk, "p", r))
                        nc.tensor.matmul(ybank[:], e_w2[:, r // FC, r % FC, :], p[:, r % 2, :],
                                         start=False, stop=(r == STEPS - 1)).then_inc(moe_y.sem, 1)
                    yield
                    if s < STEPS:
                        if s >= 2:
                            pe.wait_ge(moe_vec.sem, moe_vec.after(blk, "p", s - 2))
                        product(up_banks[s % 2][:], j * P, e).then_inc(moe_up.sem, 1)
                    yield

            @staticmethod
            def moe_out(pe, blk):
                yield
                pe.wait_ge(moe_act.sem, moe_act.after(blk, "yF"))
                turn_back(yF, gate[0]).then_inc(moe_y.sem, 1)
                yield
                for _ in range(3):
                    yield

            @staticmethod
            def ter(pe, blk, done):
                m, act, vec = ter_pe, ter_act, ter_vec
                for q in range(SEQS):
                    pe.wait_ge(ffn_vec[q].sem, ffn_vec[q].before(blk + 1))
                for q in range(SEQS):
                    pe.wait_ge(route_act[q].sem, route_act[q].after(BLOCKS - 1, "wT"))
                    pe.wait_ge(route_pool[q].sem, route_pool[q].after(BLOCKS - 1, "x1lo"))
                turn(x3_t[:, blk % 2 * T:(blk % 2 + 1) * T, :], gate[1]).then_inc(m.sem, 1)
                yield
                yield
                pe.wait_ge(moe_vec.sem, moe_vec.after(done, "sum"))
                pe.wait_ge(act.sem, act.after(blk, "x3F"))
                for c in range(FC):
                    if c >= 2:
                        pe.wait_ge(act.sem, act.after(blk, "silu", c - 2))
                        pe.wait_ge(vec.sem, vec.after(blk, "h", c - 2))
                    nc.tensor.matmul(gate[c % 2][:], t_w12[:, 0, c * P:(c + 1) * P], x3F, start=True, stop=True)
                    nc.tensor.matmul((up, ybank)[c % 2][:], t_w12[:, 1, c * P:(c + 1) * P], x3F,
                                     start=True, stop=True).then_inc(m.sem, 1)
                    yield
                yield
                for w, (src, name) in enumerate(((tA, "h1"), (tB, "h2"))):
                    for c in range(FC):
                        before = act.after(blk, ("silu", "h1")[w], FC - 2 + c) if c < 2 else act.after(blk, name, c - 2)
                        pe.wait_ge(act.sem, before)
                        for k in range(FC):
                            if c == 0 and w == 0:
                                pe.wait_ge(vec.sem, vec.after(blk, "h", k))
                            elif c == 0:
                                pe.wait_ge(act.sem, act.after(blk, "h1", k))
                            mm = nc.tensor.matmul(gate[c % 2][:], t_h[:, w, k, c * P:(c + 1) * P], src[:, k, :],
                                                  start=(k == 0), stop=(k == FC - 1))
                            if k == 1:
                                yield
                        mm.then_inc(m.sem, 1)
                        yield
                for k in range(FC):
                    pe.wait_ge(act.sem, act.after(blk, "h2", k))
                    mm = nc.tensor.matmul(ybank[:], t_w3[:, k, :], tA[:, k, :], start=(k == 0), stop=(k == FC - 1))
                mm.then_inc(m.sem, 1)
                yield
                yield
                pe.wait_ge(act.sem, act.after(blk, "yF"))
                turn_back(tyF, up).then_inc(m.sem, 1)
                yield
                for _ in range(3):
                    yield

        class Act:
            @staticmethod
            def setup(act):
                act.wait_ge(set_pe, 1)
                nc.scalar.copy(wqkv0[:], gate[0][:, 0:3 * D]).then_inc(set_act, 1)

            @staticmethod
            def columns(act):
                yield
                act.wait_ge(set_pe, 2)
                nc.scalar.copy(cols[:], gate[1][:, 0:NROWS]).then_inc(set_act, 1)
                yield

            @staticmethod
            def split(act):
                for e in range(E):
                    act.wait_ge(e_got[e], 16)
                    nc.scalar.copy(e_w1hi[:, e, :], e_raw[e]).then_inc(e_high, 1)
                    yield

            @staticmethod
            def ternary(act):
                yield
                for n, (_, _, dst) in enumerate(groups):
                    if n == ROUND0:
                        act.wait_ge(e_low, E)
                    act.wait_ge(set_pe, 2 + n + 1)
                    nc.scalar.copy(dst, ab[n % 2][1][:]).then_inc(set_act, 1)
                    yield

            @staticmethod
            def mix(act, blk, y):
                m, pe = mix_act[y.q], mix_pe[y.q]
                yield
                act.wait_ge(pe.sem, pe.after(blk, "xT"))
                nc.scalar.copy(y.hF, y.a[:, 0:N]).then_inc(m.sem, 1)
                yield
                yield
                for t in range(H):
                    act.wait_ge(pe.sem, pe.after(blk, "qkv", t))
                    nc.scalar.copy(y.qkv[:, t].rearrange("p c d -> p (c d)"), (y.b, y.a)[t][:, 0:3 * D]).then_inc(m.sem, 1)
                yield
                for _ in range(7):
                    yield

            @staticmethod
            def route(act, blk, y):
                m, pe, vec = route_act[y.q], route_pe[y.q], route_vec[y.q]
                yield
                act.wait_ge(pe.sem, pe.after(blk, "x1T"))
                nc.scalar.copy(y.hF, y.a[:, 0:N]).then_inc(m.sem, 1)
                nc.scalar.copy(x1_of(blk)[1][:, y.q * N:(y.q + 1) * N], y.a[:, 0:N]).then_inc(m.sem, 1)
                yield
                for _ in range(4):
                    yield
                act.wait_ge(vec.sem, vec.after(blk, "apply", H - 1))
                nc.scalar.activation(y.hg, y.hg, ACT.Gelu_apprx_tanh).then_inc(m.sem, 1)
                yield
                yield
                act.wait_ge(pe.sem, pe.after(blk, "hT"))
                nc.scalar.copy(y.hT[0:R, :], y.a[0:R, 0:N]).then_inc(m.sem, 1)
                yield
                yield
                yield
                act.wait_ge(vec.sem, vec.after(blk, "less_max"))
                nc.scalar.activation(y.lex[:], y.lex[:], ACT.Exp).then_inc(m.sem, 1)
                yield
                yield
                yield
                act.wait_ge(pe.sem, pe.after(blk, "wT"))
                nc.scalar.copy(x1_of(blk)[3][:, y.q * N:(y.q + 1) * N], y.a[0:E, 0:N]).then_inc(m.sem, 1)
                yield

            @staticmethod
            def conv(act, blk, y):
                m, pe, vec = conv_act[y.q], conv_pe[y.q], conv_vec[y.q]
                yield
                act.wait_ge(pe.sem, pe.after(blk, "x2T"))
                nc.scalar.copy(x2F[:, y.q, PAD:PAD + N], y.a[:, 0:N]).then_inc(m.sem, 1)
                yield
                for _ in range(5):
                    yield
                act.wait_ge(conv_pool[y.q].sem, conv_pool[y.q].after(blk, "pad", 1))
                for j in range(4):
                    act.wait_ge(vec.sem, vec.after(blk, "tap1", 4 * (TAPS - 1) + j))
                    nc.scalar.activation(y.c1F[:, j, PAD:PAD + N], y.c1[:, j], ACT.Gelu, bias=c1_b[:, j:j + 1]).then_inc(m.sem, 1)
                yield
                for _ in range(9):
                    yield

            @staticmethod
            def att(act, blk, y, i):
                m, pe = att_act[y.q], att_pe[y.q]
                yield
                act.wait_ge(pe.sem, pe.after(blk, f"{i}hT"))
                nc.scalar.copy(y.hF, y.a[:, 0:N]).then_inc(m.sem, 1)
                yield
                yield
                for t in range(H):
                    bank = (y.b, y.a)[t]
                    act.wait_ge(pe.sem, pe.after(blk, f"{i}qkv", t))
                    nc.scalar.activation(y.qk[:, :, t, :], bank[:, 0:2 * D].rearrange("p (c d) -> p c d", c=2), ACT.Gelu)
                    nc.scalar.copy(y.vt[:, t, :], bank[:, 2 * D:3 * D]).then_inc(m.sem, 1)
                yield
                for _ in range(3):
                    yield
                act.wait_ge(pe.sem, pe.after(blk, f"{i}qT"))
                nc.scalar.copy(y.qF, y.b[:, 0:N]).then_inc(m.sem, 1)
                yield
                for _ in range(4):
                    yield

            @staticmethod
            def ffn(act, blk, y):
                m, pe = ffn_act[y.q], ffn_pe[y.q]
                yield
                act.wait_ge(pe.sem, pe.after(blk, "hT"))
                nc.scalar.copy(y.hF, y.a[:, 0:N]).then_inc(m.sem, 1)
                yield
                for j in range(FC):
                    if j % 2 == 0:
                        yield
                    act.wait_ge(pe.sem, pe.after(blk, "up", j))
                    nc.scalar.activation(y.ffh[:, j, :], (y.b, y.a)[j % 2][:, 0:N], ACT.Gelu, bias=col("f_b1", j)).then_inc(m.sem, 1)
                    if j % 2:
                        yield
                yield
                act.wait_ge(pe.sem, pe.after(blk, "down"))
                nc.scalar.activation(y.hF, y.b[:, 0:N], ACT.Identity, bias=col("f_b2")).then_inc(m.sem, 1)
                yield
                for _ in range(6):
                    yield

            @staticmethod
            def moe(act, blk):
                for s in range(STEPS + 2):
                    yield
                    if s < STEPS:
                        e, j = divmod(s, FC)
                        act.wait_ge(moe_gate.sem, moe_gate.after(blk, "gate", s))
                        if s >= 2:
                            act.wait_ge(moe_pool.sem, moe_pool.after(blk, "gw", s - 2))
                        nc.scalar.activation(g[:, s % 2, :], gate_bank[:], ACT.Gelu_apprx_tanh,
                                             bias=col("e_b1", e * 2 * FC + FC + j)).then_inc(moe_act.sem, 1)
                    yield

            @staticmethod
            def moe_out(act, blk):
                act.wait_ge(moe_y.sem, moe_y.after(blk, "y", STEPS - 1))
                nc.scalar.copy(yF, ybank[:]).then_inc(moe_act.sem, 1)
                yield
                for _ in range(4):
                    yield

            @staticmethod
            def ter(act, blk, done):
                m, pe, vec = ter_act, ter_pe, ter_vec
                yield
                act.wait_ge(pe.sem, pe.after(blk, "x3T"))
                nc.scalar.copy(x3F, gate[1][:]).then_inc(m.sem, 1)
                yield
                yield
                for c in range(FC):
                    act.wait_ge(pe.sem, pe.after(blk, "gu", c))
                    if c >= 2:
                        act.wait_ge(vec.sem, vec.after(blk, "h", c - 2))
                    nc.scalar.activation(u[:, c % 2, :], gate[c % 2][:], ACT.Silu, scale=col("w1_s", c)).then_inc(m.sem, 1)
                    yield
                yield
                for name, scale, dst in (("h1", "h1_s", tB), ("h2", "h2_s", tA)):
                    for c in range(FC):
                        yield
                        act.wait_ge(pe.sem, pe.after(blk, name, c))
                        nc.scalar.activation(dst[:, c, :], gate[c % 2][:], ACT.Gelu, scale=col(scale, c)).then_inc(m.sem, 1)
                        yield
                act.wait_ge(pe.sem, pe.after(blk, "w3"))
                nc.scalar.activation(tyF, ybank[:], ACT.Identity, scale=col("w3_s")).then_inc(m.sem, 1)
                yield
                for _ in range(4):
                    yield

        SETUP_STEPS = 11

        class Vec:
            @staticmethod
            def setup(dve):
                nc.vector.memset(minus_half[:], -0.5).then_inc(begun, 1)
                nc.vector.memset(x2F[:], 0.0).then_inc(begun, 1)
                nc.vector.memset(ones[:], 1.0).then_inc(begun, 1)
                nc.vector.memset(plus[:], 0.21).then_inc(begun, 1)
                nc.vector.memset(a_bs[:].bitcast(F32), 0.0).then_inc(begun, 1)
                nc.vector.memset(a_sel[:].bitcast(F32), 0.0).then_inc(begun, 1)

            @staticmethod
            def columns(dve):
                dve.wait_ge(vectors, 16 * len(vector_loads))
                dve.wait_ge(begun, 6)
                for at in (0, 32):
                    nc.vector.tensor_copy(a_bs[at:at + L, :], a_b[at:at + L, :]).then_inc(begun, 1)
                    nc.vector.tensor_copy(a_sel[at:at + L, :], ident[at:at + L, at:at + L]).then_inc(begun, 1)
                dve.wait_ge(begun, 10)
                nc.vector.tensor_tensor(a_bs[32:32 + L, :], a_b[32:32 + L, :], a_bs[32:32 + L, :].bitcast(F32),
                                        ALU.subtract).then_inc(begun, 1)
                yield
                yield

            @staticmethod
            def mix(dve, blk, y):
                m = mix_vec[y.q]
                s = m.sem
                for _ in range(4):
                    yield
                qk0 = y.qkv[:, :, 0:2, :]
                dve.wait_ge(mix_act[y.q].sem, mix_act[y.q].after(blk, "qkv", H - 1))
                nc.vector.tensor_tensor(y.sq, qk0, qk0, ALU.mult).then_inc(s, 1)
                dve.wait_ge(s, m.after(blk, "square"))
                nc.vector.tensor_reduce(y.ssq[:], y.sq, AX.X, ALU.add).then_inc(s, 1)
                dve.wait_ge(s, m.after(blk, "ssq"))
                nc.vector.tensor_scalar(y.ssq[:], y.ssq[:], 1e-24, None, ALU.max).then_inc(s, 1)
                yield
                yield
                dve.wait_ge(mix_pool[y.q].sem, mix_pool[y.q].after(blk, "len"))
                for t in range(H):
                    nc.vector.scalar_tensor_tensor(out=y.kvt[:, t, :], in0=y.qkv[:, t, 1, :], scalar=y.rn[:, t, 1:2],
                                                   in1=y.qkv[:, t, 2, :], op0=ALU.mult, op1=ALU.mult).then_inc(s, 1)
                yield
                yield
                dve.wait_ge(mix_pe[y.q].sem, mix_pe[y.q].after(blk, "mean"))
                for t in range(H):
                    nc.vector.scalar_tensor_tensor(out=y.sum[:, t, :], in0=y.qkv[:, t, 0, :], scalar=y.rn[:, t, 0:1],
                                                   in1=y.b[:, 0:D], op0=ALU.mult, op1=ALU.mult).then_inc(s, 1)
                dve.wait_ge(s, m.after(blk, "q", H - 1))
                nc.vector.tensor_tensor(y.sum, y.sum, x_t[:, y.ts, :], ALU.add).then_inc(s, 1)
                dve.wait_ge(s, m.after(blk, "sum"))
                norm_stats(dve, m, blk, "", y.sum, y.thread, 1e-5)
                yield
                yield
                if not (isinstance(blk, int) and blk <= 1):
                    dve.wait_ge(moe_vec.sem, moe_vec.after(blk - 1, "sum"))
                norm_apply(dve, m, blk, "", y.sum, x1_of(blk)[0][:, y.ts, :], y.thread, mix_pool[y.q])
                yield

            @staticmethod
            def route(dve, blk, y):
                m, pe = route_vec[y.q], route_pe[y.q]
                s = m.sem

                def after(name):
                    dve.wait_ge(s, m.after(blk, name))

                for _ in range(3):
                    yield
                if first(blk):
                    dve.wait_ge(early, 16 * len(early_loads))
                dve.wait_ge(pe.sem, pe.after(blk, "h"))
                nc.vector.tensor_tensor(y.hr, y.b[:, 0:H * R].rearrange("p (t d) -> p t d", t=H),
                                        br1[:].unsqueeze(1).to_broadcast([P, H, R]), ALU.add).then_inc(s, 1)
                after("h")
                norm_stats(dve, m, blk, "", y.hr, y.thread, 1e-6, y.hg, r_g[:])
                yield
                yield
                norm_apply(dve, m, blk, "", y.hr, y.hg, y.thread, route_pool[y.q], r_b[:])
                yield
                for _ in range(4):
                    yield
                dve.wait_ge(pe.sem, pe.after(blk, "logit"))
                nc.vector.tensor_tensor(y.lg[:], y.b[:, 0:H * E].rearrange("p (t e) -> p t e", t=H),
                                        br2[:].unsqueeze(1).to_broadcast([P, H, E]), ALU.add).then_inc(s, 1)
                full, small = [P, H, E, E], [P, H, E]
                other, own = y.lg[:].unsqueeze(2).to_broadcast(full), y.lg[:].unsqueeze(3).to_broadcast(full)
                after("logit")
                nc.vector.tensor_tensor(y.cmp1, other, own, ALU.is_gt).then_inc(s, 1)
                nc.vector.tensor_tensor(y.cmp2, other, own, ALU.is_equal).then_inc(s, 1)
                after("tie")
                nc.vector.tensor_tensor(y.cmp2, y.cmp2, earlier[:].unsqueeze(1).to_broadcast(full), ALU.mult).then_inc(s, 1)
                after("tie_earlier")
                nc.vector.tensor_tensor(y.cmp1, y.cmp1, y.cmp2, ALU.add).then_inc(s, 1)
                after("beats")
                nc.vector.tensor_reduce(y.rank[:], y.cmp1, AX.X, ALU.add).then_inc(s, 1)
                after("rank")
                nc.vector.tensor_scalar(y.rank[:], y.rank[:], 1.5, None, ALU.is_lt).then_inc(s, 1)
                nc.vector.tensor_reduce(y.lmax[:], y.lg[:], AX.X, ALU.max).then_inc(s, 1)
                after("max")
                nc.vector.tensor_tensor(y.lex[:], y.lg[:], y.lmax[:].unsqueeze(2).to_broadcast(small), ALU.subtract).then_inc(s, 1)
                yield
                yield
                dve.wait_ge(route_act[y.q].sem, route_act[y.q].after(blk, "exp"))
                nc.vector.tensor_tensor(y.lex[:], y.lex[:], y.rank[:], ALU.mult).then_inc(s, 1)
                after("keep")
                nc.vector.tensor_reduce(y.lmax[:], y.lex[:], AX.X, ALU.add).then_inc(s, 1)
                after("total")
                nc.vector.reciprocal(y.lmax[:], y.lmax[:]).then_inc(s, 1)
                after("recip")
                nc.vector.tensor_tensor(y.wts[:], y.lex[:], y.lmax[:].unsqueeze(2).to_broadcast(small), ALU.mult).then_inc(s, 1)
                yield
                yield

            @staticmethod
            def conv(dve, blk, y):
                m = conv_vec[y.q]
                s = m.sem
                yield
                yield
                dve.wait_ge(conv_act[y.q].sem, conv_act[y.q].after(blk, "x2F"))
                dve.wait_ge(later, 16 * len(later_loads))
                for k in range(TAPS):
                    for j in range(4):
                        src, w = x2F[:, y.q, k:k + N], c1_w[:, j, k:k + 1]
                        if k == 0:
                            nc.vector.tensor_scalar(y.c1[:, j], src, w, None, ALU.mult).then_inc(s, 1)
                        else:
                            dve.wait_ge(s, m.after(blk, "tap1", 4 * (k - 1) + j))
                            nc.vector.scalar_tensor_tensor(out=y.c1[:, j], in0=src, scalar=w, in1=y.c1[:, j],
                                                           op0=ALU.mult, op1=ALU.add).then_inc(s, 1)
                    yield
                yield
                for j in range(4):
                    dve.wait_ge(conv_act[y.q].sem, conv_act[y.q].after(blk, "gelu", j))
                    for k in range(TAPS):
                        n = j * TAPS + k
                        src, w = y.c1F[:, j, k:k + N], c2_w[:, j, k:k + 1]
                        if n == 0:
                            nc.vector.tensor_scalar(y.c2[:, 0], src, w, col("c2_b"), ALU.mult, ALU.add).then_inc(s, 1)
                        elif n == 1:
                            nc.vector.tensor_scalar(y.c2[:, 1], src, w, None, ALU.mult).then_inc(s, 1)
                        else:
                            dve.wait_ge(s, m.after(blk, "tap2", n - 2))
                            nc.vector.scalar_tensor_tensor(out=y.c2[:, n % 2], in0=src, scalar=w, in1=y.c2[:, n % 2],
                                                           op0=ALU.mult, op1=ALU.add).then_inc(s, 1)
                    yield
                dve.wait_ge(s, m.after(blk, "tap2", 4 * TAPS - 1))
                nc.vector.tensor_tensor(y.c2[:, 0], y.c2[:, 0], y.c2[:, 1], ALU.add).then_inc(s, 1)
                yield
                yield
                dve.wait_ge(conv_pe[y.q].sem, conv_pe[y.q].after(blk, "c2T"))
                nc.vector.tensor_tensor(y.sum, tok(y.a, H), x2_t[:, y.ts, :], ALU.add).then_inc(s, 1)
                dve.wait_ge(s, m.after(blk, "sum"))
                norm_stats(dve, m, blk, "", y.sum, y.thread, 1e-12, y.h_t, gains[:, 0])
                yield
                yield
                norm_apply(dve, m, blk, "", y.sum, y.h_t, y.thread, conv_pool[y.q], shifts[:, 0])
                yield

            @staticmethod
            def att(dve, blk, y, i):
                m, pe, pool = att_vec[y.q], att_pe[y.q], att_pool[y.q]
                s = m.sem

                def after(name, k=0):
                    dve.wait_ge(s, m.after(blk, f"{i}{name}", k))

                for _ in range(4):
                    yield
                dve.wait_ge(att_act[y.q].sem, att_act[y.q].after(blk, f"{i}v", H - 1))
                flat = "p c t d -> p c (t d)"
                qk, rot = y.qk.rearrange(flat), y.rot.rearrange(flat)
                cos_f, sin_f = (v[:].rearrange("p t d -> p (t d)") for v in (cos, sin))
                for odd in range(2):
                    nc.vector.scalar_tensor_tensor(out=rot[:, :, odd::2], in0=qk[:, :, 1 - odd::2], scalar=0.21,
                                                   in1=sin_f[:, odd::2].unsqueeze(1).to_broadcast([P, 2, N // 2]),
                                                   op0=ALU.add, op1=ALU.mult).then_inc(s, 1)
                nc.vector.scalar_tensor_tensor(out=y.big.rearrange(flat), in0=qk, scalar=0.21,
                                               in1=cos_f.unsqueeze(1).to_broadcast([P, 2, N]),
                                               op0=ALU.add, op1=ALU.mult).then_inc(s, 1)
                after("cos")
                nc.vector.tensor_tensor(y.rot, y.rot, y.big, ALU.add).then_inc(s, 1)
                yield
                dve.wait_ge(pe.sem, pe.after(blk, f"{i}kmean"))
                nc.vector.scalar_tensor_tensor(out=y.den, in0=y.qk[:, 0], scalar=0.21,
                                               in1=y.b[:, 0:D].unsqueeze(1).to_broadcast([P, H, D]),
                                               op0=ALU.add, op1=ALU.mult).then_inc(s, 1)
                yield
                dve.wait_ge(pe.sem, pe.after(blk, f"{i}kv"))
                nc.vector.tensor_tensor(y.kvm[:], y.a[:, 0:D], headmask[:], ALU.mult).then_inc(s, 1)
                after("den")
                nc.vector.tensor_reduce(y.z[:], y.den.rearrange("p t (h e) -> p (t h) e", e=HD), AX.X, ALU.add).then_inc(s, 1)
                yield
                after("head")
                nc.vector.tensor_scalar(y.z[:], y.z[:], 1e-6, None, ALU.add).then_inc(s, 1)
                after("eps6")
                nc.vector.reciprocal(y.z[:], y.z[:]).then_inc(s, 1)
                yield
                yield
                dve.wait_ge(pe.sem, pe.after(blk, f"{i}o"))
                after("z")
                nc.vector.tensor_tensor(y.sum.rearrange("p t (h e) -> p (t h) e", e=HD),
                                        y.a[:, 0:N].rearrange("p (h e) -> p h e", e=HD),
                                        y.z[:].unsqueeze(2).to_broadcast([P, H * HEADS, HD]), ALU.mult).then_inc(s, 1)
                after("oz")
                nc.vector.tensor_tensor(y.sum, y.sum, y.h_t, ALU.add).then_inc(s, 1)
                after("sum")
                norm_stats(dve, m, blk, str(i), y.sum, y.thread, 1e-12, y.h_t, gains[:, 1 + i])
                yield
                yield
                norm_apply(dve, m, blk, str(i), y.sum, y.h_t, y.thread, pool, shifts[:, 1 + i])
                yield

            @staticmethod
            def ffn(dve, blk, y):
                m = ffn_vec[y.q]
                s = m.sem
                for _ in range(9):
                    yield
                dve.wait_ge(ffn_pe[y.q].sem, ffn_pe[y.q].after(blk, "fT"))
                nc.vector.tensor_tensor(y.sum, tok(y.a, H), y.h_t, ALU.add).then_inc(s, 1)
                dve.wait_ge(s, m.after(blk, "sum"))
                norm_stats(dve, m, blk, "i", y.sum, y.thread, 1e-12, y.h_t, gains[:, L + 1])
                yield
                yield
                norm_apply(dve, m, blk, "i", y.sum, y.h_t, y.thread, ffn_pool[y.q], shifts[:, L + 1])
                dve.wait_ge(s, m.after(blk, "iapply", H - 1))
                dve.wait_ge(conv_pool[y.q].sem, conv_pool[y.q].after(blk, "x2"))
                nc.vector.tensor_tensor(y.sum, y.h_t, r_t[:, y.ts, :], ALU.add).then_inc(s, 1)
                dve.wait_ge(s, m.after(blk, "sum2"))
                norm_stats(dve, m, blk, "o", y.sum, y.thread, 1e-5)
                yield
                yield
                half = blk
                if isinstance(blk, int):
                    half = blk % 2
                    dve.wait_ge(ter_vec.sem, ter_vec.after(blk - 2, "sum"))
                norm_apply(dve, m, blk, "o", y.sum, x3_t[:, bass.ds(half * T + y.ts.start, H), :], y.thread, ffn_pool[y.q])
                yield

            @staticmethod
            def moe(dve, blk):
                for s in range(STEPS + 2):
                    yield
                    if 1 <= s <= STEPS:
                        r = s - 1
                        e, j = divmod(r, FC)
                        dve.wait_ge(moe_up.sem, moe_up.after(blk, "up", r))
                        dve.wait_ge(moe_pool.sem, moe_pool.after(blk, "gw", r))
                        if r >= 2:
                            dve.wait_ge(moe_y.sem, moe_y.after(blk, "y", r - 2))
                        nc.vector.scalar_tensor_tensor(out=p[:, r % 2, :], in0=up_banks[r % 2][:], scalar=col("e_b1", e * 2 * FC + j),
                                                       in1=gw[:, r % 2, :], op0=ALU.add, op1=ALU.mult).then_inc(moe_vec.sem, 1)
                    yield

            @staticmethod
            def moe_out(dve, blk):
                s = moe_vec.sem
                yield
                yield
                dve.wait_ge(moe_y.sem, moe_y.after(blk, "yT"))
                if isinstance(blk, int) and blk > 0:
                    dve.wait_ge(ter_vec.sem, ter_vec.before(1))
                nc.vector.tensor_tensor(sumx[:], tok(gate[0], T), x1_of(blk)[0][:], ALU.add).then_inc(s, 1)
                dve.wait_ge(s, moe_vec.after(blk, "sum"))
                norm_stats(dve, moe_vec, blk, "", sumx, X, 1e-5)
                yield
                yield
                if not (isinstance(blk, int) and blk == 0):
                    for q in range(SEQS):
                        dve.wait_ge(conv_vec[q].sem, conv_vec[q].after(blk - 1, "sum"))
                        dve.wait_ge(conv_pool[q].sem, conv_pool[q].after(blk - 1, "x2"))
                norm_apply(dve, moe_vec, blk, "", sumx, x2_t, X, moe_pool)
                yield

            @staticmethod
            def ter(dve, blk, done):
                s = ter_vec.sem
                for _ in range(4):
                    yield
                for c in range(FC):
                    dve.wait_ge(ter_pe.sem, ter_pe.after(blk, "gu", c))
                    dve.wait_ge(ter_act.sem, ter_act.after(blk, "silu", c))
                    nc.vector.scalar_tensor_tensor(out=tA[:, c, :], in0=(up, ybank)[c % 2][:], scalar=col("w2_s", c),
                                                   in1=u[:, c % 2, :], op0=ALU.mult, op1=ALU.mult).then_inc(s, 1)
                    yield
                for _ in range(4 * FC + 2):
                    yield
                dve.wait_ge(ter_pe.sem, ter_pe.after(blk, "yT"))
                dve.wait_ge(moe_vec.sem, moe_vec.before(done + 1))
                nc.vector.tensor_tensor(sumx[:], tok(up, T), x3_t[:, blk % 2 * T:(blk % 2 + 1) * T, :], ALU.add).then_inc(s, 1)
                dve.wait_ge(s, ter_vec.after(blk, "sum"))
                norm_stats(dve, ter_vec, blk, "", sumx, X, 1e-5)
                yield
                yield
                dve.wait_ge(out_put.sem, out_put.before(blk))
                norm_apply(dve, ter_vec, blk, "", sumx, o_t, X, ter_pool)
                yield

        class Pool:
            @staticmethod
            def columns(pool):
                yield
                yield

            @staticmethod
            def split(pool):
                for e in range(E):
                    pool.wait_ge(e_high, e + 1)
                    nc.gpsimd.tensor_tensor(e_w1lo[:, e, :], e_raw[e], e_w1hi[:, e, :].bitcast(F32),
                                            ALU.subtract).then_inc(e_low, 1)
                    yield

            @staticmethod
            def mix(pool, blk, y):
                m = mix_pool[y.q]
                for _ in range(5):
                    yield
                pool.wait_ge(begun, 1)
                pool.wait_ge(mix_vec[y.q].sem, mix_vec[y.q].after(blk, "clip"))
                nc.gpsimd.tensor_tensor(y.rn[:].rearrange("p t c -> p (t c)"), y.ssq[:].rearrange("p t c -> p (t c)"),
                                        minus_half[:, 0:2 * H], ALU.pow).then_inc(m.sem, 1)
                yield
                for _ in range(3):
                    yield
                norm_power(pool, m, blk, "", mix_vec[y.q], y.thread, H)
                yield
                yield

            @staticmethod
            def route(pool, blk, y):
                yield
                yield
                at = slice(y.q * N, (y.q + 1) * N)
                pool.wait_ge(route_act[y.q].sem, route_act[y.q].after(blk, "x1hi"))
                _, x1hi, x1lo, _ = x1_of(blk)
                nc.gpsimd.tensor_tensor(x1lo[:, at], y.hF, x1hi[:, at].bitcast(F32), ALU.subtract).then_inc(route_pool[y.q].sem, 1)
                yield
                yield
                norm_power(pool, route_pool[y.q], blk, "", route_vec[y.q], y.thread, H)
                for _ in range(11):
                    yield

            @staticmethod
            def conv(pool, blk, y):
                m = conv_pool[y.q]
                wait_apart(pool, conv_pe[y.q].sem, conv_pe[y.q].after(blk, "x2T"))
                for side in range(2):
                    at = side * (PAD + N)
                    nc.gpsimd.memset(y.c1F[:, :, at:at + PAD], 0.0).then_inc(m.sem, 1)
                wait_apart(pool, ffn_vec[y.q].sem, ffn_vec[y.q].before(blk))
                nc.gpsimd.tensor_copy(r_t[:, y.ts, :], x2_t[:, y.ts, :]).then_inc(m.sem, 1)
                yield
                for _ in range(14):
                    yield
                norm_power(pool, m, blk, "", conv_vec[y.q], y.thread, H)
                yield
                yield

            @staticmethod
            def att(pool, blk, y, i):
                m = att_pool[y.q]
                for _ in range(10):
                    yield
                norm_power(pool, m, blk, str(i), att_vec[y.q], y.thread, H)
                yield
                yield

            @staticmethod
            def ffn(pool, blk, y):
                for _ in range(10):
                    yield
                norm_power(pool, ffn_pool[y.q], blk, "i", ffn_vec[y.q], y.thread, H)
                yield
                yield
                norm_power(pool, ffn_pool[y.q], blk, "o", ffn_vec[y.q], y.thread, H)
                yield
                yield

            @staticmethod
            def moe(pool, blk):
                for s in range(STEPS + 2):
                    if 1 <= s <= STEPS:
                        r = s - 1
                        e = r // FC
                        if r % FC == 0:
                            pool.wait_ge(moe_wB[e % 2].sem, moe_wB[e % 2].after(blk, "wB", e // 2))
                        pool.wait_ge(moe_act.sem, moe_act.after(blk, "gelu", r))
                        if r >= 2:
                            pool.wait_ge(moe_vec.sem, moe_vec.after(blk, "p", r - 2))
                        nc.gpsimd.tensor_tensor(gw[:, r % 2, :], g[:, r % 2, :], wB[:, e % 2, :],
                                                ALU.mult).then_inc(moe_pool.sem, 1)
                    yield
                    yield

            @staticmethod
            def moe_out(pool, blk):
                for _ in range(3):
                    yield
                norm_power(pool, moe_pool, blk, "", moe_vec, X, T)
                yield
                yield

            @staticmethod
            def ter(pool, blk, done):
                for _ in range(19 + 2 * FC):
                    yield
                norm_power(pool, ter_pool, blk, "", ter_vec, X, T)
                yield
                yield

        LAG = 0.54

        HEAD, BODY, MOE, MOE_OUT, TER = (sum(v) for v in (HEAD_SLOTS, BODY_SLOTS, MOE_SLOTS, MOE_OUT_SLOTS, TER_SLOTS))
        COLUMNS = 22.5
        TERN0, TERN1, SPLIT0, SPLIT1, TER2 = 2.55, 48.15, 7., 41.4, 50.
        OUT_FROM, HEAD_FROM, END, BODY_END = 88.35, 102., 130., 130.
        MOE_FROM, OUT_FROM1, END1 = 50.6, 148.73, 145.

        def head(e, eng, blk, start, end):
            return [(chain(e.mix(eng, blk, y), e.route(eng, blk, y)), HEAD_SLOTS, start + y.q * LAG, end - (1 - y.q) * LAG)
                    for y in (early_heads if isinstance(blk, int) else late_heads)]

        def body(e, eng, blk, start, end):
            return [(chain(e.conv(eng, blk, y), *[e.att(eng, blk, y, i) for i in range(L)], e.ffn(eng, blk, y)), BODY_SLOTS,
                     start + y.q * LAG, end - (1 - y.q) * LAG) for y in seqs]

        def run(e, eng, start, split, turning):
            start()
            extra = [(split(), [1.] * E, SPLIT0, SPLIT1)] if split else []
            extra += [(turning(), TERNARY_SLOTS, HEAD + TERN0, HEAD + TERN1)] if turning else []
            x, end = HEAD + MOE, HEAD + MOE + MOE_OUT
            weave(*head(e, eng, 0, 0, HEAD), (e.moe(eng, 0), MOE_SLOTS, HEAD, x), (e.moe_out(eng, 0), MOE_OUT_SLOTS, x, end), *extra,
                  (e.columns(eng), [1., 1.], COLUMNS, COLUMNS + 2), *head(e, eng, 1, HEAD + TERN1, x))

            with eng.Fori(1, BLOCKS - 1) as blk:
                weave((e.moe(eng, blk), MOE_SLOTS, 0, OUT_FROM), (e.moe_out(eng, blk), MOE_OUT_SLOTS, OUT_FROM, HEAD_FROM),
                      *head(e, eng, blk + 1, HEAD_FROM, END), *body(e, eng, blk - 1, 0, BODY_END))
            last = BLOCKS - 1
            weave((e.ter(eng, 0, last - 1), TER_SLOTS, 0, MOE_FROM), (e.moe(eng, last), MOE_SLOTS, MOE_FROM, OUT_FROM1),
                  (e.moe_out(eng, last), MOE_OUT_SLOTS, OUT_FROM1, END1), *body(e, eng, last - 1, 0, END1))
            weave((e.ter(eng, 1, last), TER_SLOTS, 0, TER2), (e.ter(eng, 2, last), TER_SLOTS, TER2 + 3, BODY),
                  *body(e, eng, last, 0, BODY))
            weave((e.ter(eng, last, last), TER_SLOTS, 0, TER))

        def nothing():
            pass

        @block.sync
        def _(sp):
            begin(sp, x_got, w_put, out_put, *moe_wB)

            def load_x(blk):
                for q in range(SEQS):
                    sp.wait_ge(mix_vec[q].sem, mix_vec[q].before(blk))
                sp.dma_start(x_t[:], x_in[bass.ds(blk * W, W), :].rearrange("(t p) d -> p t d", p=P)).then_inc(x_got.sem, 16)

            def put(blk):
                sp.wait_ge(ter_vec.sem, ter_vec.before(blk + 1))
                sp.dma_start(out[bass.ds(blk * W, W), :].rearrange("(t p) d -> p t d", p=P), o_t[:]).then_inc(out_put.sem, 16)

            def experts(blk, first=0, last=E):
                for e in range(first, last):
                    if e == 0:
                        for q in range(SEQS):
                            sp.wait_ge(route_act[q].sem, route_act[q].after(blk, "wT"))
                        sp.dma_start(w_rows[bass.ds(blk * E, E), :], x1_of(blk)[3][:]).then_inc(w_put.sem, 16)
                        sp.wait_ge(w_put.sem, w_put.after(blk, "w"))
                        if isinstance(blk, int) and blk == 0:
                            sp.wait_ge(e_low, E // 2)
                        else:
                            sp.wait_ge(moe_vec.sem, moe_vec.after(blk - 1, "sum"))
                            for q in range(SEQS):
                                sp.wait_ge(route_pool[q].sem, route_pool[q].after(blk, "x1lo"))
                            if isinstance(blk, int):
                                sp.wait_ge(ter_vec.sem, ter_vec.after(0, "sum"))
                    elif e >= 2:
                        sp.wait_ge(moe_pool.sem, moe_pool.after(blk, "gw", (e - 1) * FC - 1))
                    sp.dma_start(wB[:, e % 2], row(w_rows[bass.ds(blk * E + e, 1), :].rearrange("a n -> (a n)"))).then_inc(moe_wB[e % 2].sem, 16)

            load_x(0)
            for loads_of, got in ((first_loads, firsts), (early_loads, early), (vector_loads, vectors)):
                for dst, src in loads_of:
                    sp.dma_start(dst, src).then_inc(got, 16)
            for e in range(E):
                sp.dma_start(e_raw[e], a["L0_ffn_W1"][e]).then_inc(e_got[e], 16)
            for e in range(E):
                sp.dma_start(e_w2[:, e, :, :], a["L0_ffn_W2"][e].rearrange("(c p) d -> p c d", p=P)).then_inc(w2_got[e], 16)
            for dst, src in later_loads:
                sp.dma_start(dst, src).then_inc(later, 16)

            for q in range(SEQS):
                sp.wait_ge(route_act[q].sem, route_act[q].before(1))

            def ternary(r):
                for dst, name in loads[r]:
                    sp.dma_start(dst, a[name].rearrange("(c p) i -> p c i", p=P)).then_inc(staged[r], 16)

            experts(0, 0, 2)
            ternary(0)
            ternary(1)
            load_x(1)
            experts(0, 2, 4)
            sp.wait_ge(set_pe, 2 + ROUND1)
            ternary(2)
            experts(0, 4)
            with sp.Fori(1, BLOCKS - 1) as blk:
                load_x(blk + 1)
                experts(blk)
            experts(BLOCKS - 1)
            with sp.Fori(0, BLOCKS) as blk:
                put(blk)
            sp.wait_ge(w_put.sem, w_put.before(BLOCKS))
            sp.wait_ge(out_put.sem, out_put.before(BLOCKS))

        @block.tensor
        def _(pe):
            begin(pe, *mix_pe, *route_pe, *conv_pe, *att_pe, *ffn_pe, moe_gate, moe_up, moe_y, ter_pe)
            run(Pe, pe, lambda: Pe.setup(pe), None, lambda: Pe.ternary(pe))

        @block.scalar
        def _(act):
            begin(act, *mix_act, *route_act, *conv_act, *att_act, *ffn_act, moe_act, ter_act)
            run(Act, act, lambda: Act.setup(act), lambda: Act.split(act), lambda: Act.ternary(act))

        @block.vector
        def _(dve):
            begin(dve, *mix_vec, *route_vec, *conv_vec, *att_vec, *ffn_vec, moe_vec, ter_vec)
            run(Vec, dve, lambda: Vec.setup(dve), None, None)

        @block.gpsimd
        def _(pool):
            begin(pool, *mix_pool, *route_pool, *conv_pool, *att_pool, *ffn_pool, moe_pool, ter_pool)
            run(Pool, pool, nothing, lambda: Pool.split(pool), None)


_INS = ["L0_attn_x", "L0_attn_W_q", "L0_attn_W_k", "L0_attn_W_v", "L0_ffn_Wr1", "L0_ffn_br1", "L0_ffn_ln_scale",
        "L0_ffn_ln_bias", "L0_ffn_Wr2", "L0_ffn_br2", "L0_ffn_W1", "L0_ffn_b1", "L0_ffn_W2", "L0_ffn_b2",
        "L1_attn_conv1_w", "L1_attn_conv1_b", "L1_attn_conv2_w", "L1_attn_conv2_b", "L1_attn_ln0_g", "L1_attn_ln0_b",
        "L1_attn_Wq", "L1_attn_bq", "L1_attn_Wk", "L1_attn_bk", "L1_attn_Wv", "L1_attn_bv", "L1_attn_lnA_g",
        "L1_attn_lnA_b", "L1_attn_W1", "L1_attn_b1", "L1_attn_W2", "L1_attn_b2", "L1_attn_ln2_g", "L1_attn_ln2_b",
        "L1_ffn_w1_w", "L1_ffn_w1_s", "L1_ffn_w2_w", "L1_ffn_w2_s", "L1_ffn_h1_w", "L1_ffn_h1_s", "L1_ffn_h2_w",
        "L1_ffn_h2_s", "L1_ffn_w3_w", "L1_ffn_w3_s"]


def constants():
    f = np.float32
    inv = f(1.0) / f(10000.0) ** (np.arange(0, D, 2, dtype=f) / f(D))
    freqs = np.repeat(np.arange(N, dtype=f)[:, None] * inv[None, :], 2, axis=-1)
    sign = np.where(np.arange(D) % 2 == 0, f(-1), f(1))
    tiles = lambda m: np.ascontiguousarray(m.reshape(N // P, P, D).transpose(1, 0, 2)).astype(f)
    head = np.arange(D) // HD
    e = np.arange(E)
    return {
        "c_ident": np.eye(P, dtype=f),
        "c_mean_of": np.full((P, P), 1.0 / N, f),
        "c_headmask": np.where(head[:, None] == head[None, :], f(1.0 / N), f(0)).astype(f),
        "c_cos": tiles(np.cos(freqs)),
        "c_sin": tiles(np.sin(freqs) * sign),
        "c_earlier": np.broadcast_to((e[None, :] < e[:, None]).astype(f), (P, E, E)).copy(),
    }


def kernel(**inputs):
    import concourse.bacc as _bacc
    from concourse.bass_utils import run_bass_kernel_spmd as _run

    nc = _bacc.Bacc("TRN2", target_bir_lowering=False, num_devices=1)
    arrays, aps = {}, {}
    for name, value in {**{n: inputs[n] for n in _INS}, **constants()}.items():
        v = np.ascontiguousarray(value)
        arrays[f"in_{name}_dram"] = v
        aps[name] = nc.dram_tensor(f"in_{name}_dram", v.shape, mybir.dt.from_np(v.dtype), kind="ExternalInput").ap()
    out = nc.dram_tensor("out_0_dram", (B, N, D), F32, kind="ExternalOutput").ap()
    w_rows = nc.dram_tensor("w_rows", (BLOCKS * E, W), F32, kind="Internal").ap()
    build(nc, aps["L0_attn_x"].rearrange("b n d -> (b n) d"), out.rearrange("b n d -> (b n) d"), w_rows, aps)
    r = _run(nc, [arrays], core_ids=[0])
    return r.results[0]["out_0_dram"]
```
